# Optimizing a Trainium2 kernel written in Bass

```python
import numpy as np
import jax
import jax.numpy as jnp

def _softmax(x, axis=-1):
    return jax.nn.softmax(x, axis=axis)

def _gelu(x):
    return jax.nn.gelu(x, approximate=True)

def _silu(x):
    return jax.nn.silu(x)

def _sigmoid(x):
    return jax.nn.sigmoid(x)

def _layernorm(x, axis=-1, eps=1e-05):
    m = jnp.mean(x, axis=axis, keepdims=True)
    v = jnp.var(x, axis=axis, keepdims=True)
    return (x - m) / jnp.sqrt(v + eps)

def _scatter_add(tgt, idx, src, axis=0):
    return tgt.at[idx].add(src)

def _segment_sum(src, seg, n):
    return jax.ops.segment_sum(src, seg, n)
kernel_name = 'mk_vit_tower_cls_d1_tok_img512_r4_3752cc'

def setup_inputs(seed: int=0):
    np.random.seed(seed)
    _w = jnp.asarray

    def _rec_inputs():
        import jax
        import jax.numpy as jnp
        _rk = jax.random.key(seed)
        x = -0.000190493 + 0.999948 * jax.random.normal(jax.random.fold_in(_rk, 1), (64, 2, 104, 104), jnp.float32)
        cls_tok = 0.02 * jax.random.normal(jax.random.fold_in(_rk, 5), (1, 1, 128), jnp.float32)
        return (x, cls_tok)
    x, cls_tok = _rec_inputs()

    def _L0_tok_setup():
        import jax, jax.numpy as jnp
        import numpy as np
        HP = 4
        PATCH = 8
        EPS = 1e-07

        def _shifts(x):
            h, w = (x.shape[2], x.shape[3])
            pad2 = ((0, 0), (0, 0))
            left_up = jnp.pad(x[:, :, HP:, :w - HP], pad2 + ((0, HP), (HP, 0)))
            right_up = jnp.pad(x[:, :, HP:, HP:], pad2 + ((0, HP), (0, HP)))
            left_down = jnp.pad(x[:, :, :h - HP, :w - HP], pad2 + ((HP, 0), (HP, 0)))
            right_down = jnp.pad(x[:, :, :h - HP, HP:], pad2 + ((HP, 0), (0, HP)))
            return (left_up, right_up, left_down, right_down)
        key = jax.random.key(seed)
        k1, k2, k3, k4 = jax.random.split(key, 4)
        B, C, S = (128, 2, 104)
        embed_dim = 128
        x = jax.random.normal(k1, (B, C, S, S), dtype=jnp.float32)
        gamma = 1.0 + 0.05 * jax.random.normal(k2, (10, S, S), dtype=jnp.float32)
        beta = 0.05 * jax.random.normal(k3, (10, S, S), dtype=jnp.float32)
        W = 0.02 * jax.random.normal(k4, (embed_dim, 10, PATCH, PATCH), dtype=jnp.float32)
        b = jnp.zeros((embed_dim,), dtype=jnp.float32)
        return {'x': x, 'gamma': gamma, 'beta': beta, 'W': W, 'b': b}
    _L0_tok_all = _L0_tok_setup()
    _L0_tok_in = {k: v for k, v in _L0_tok_all.items() if k in ('gamma', 'beta', 'W', 'b')}
    del _L0_tok_all

    def _L0_attn_setup():
        import jax, jax.numpy as jnp
        import numpy as np
        B, T, HID = (4, 512, 128)
        NH = 4
        KD = 64
        VD = 128
        HK = KD // NH
        HV = VD // NH
        GLR = 16
        GATE_NORM = 16.0
        EPS = 1e-05
        key = jax.random.key(seed)
        ks = jax.random.split(key, 9)

        def lin(k, out_dim, in_dim):
            return jax.random.normal(k, (out_dim, in_dim), jnp.float32) / np.float32(np.sqrt(in_dim))
        return {'hidden_states': jax.random.normal(ks[0], (B, T, HID), jnp.float32), 'Wq': lin(ks[1], KD, HID), 'Wk': lin(ks[2], KD, HID), 'Wv': lin(ks[3], VD, HID), 'Wgk1': lin(ks[4], GLR, HID), 'Wgk2': lin(ks[5], KD, GLR), 'bgk2': jax.random.normal(ks[6], (KD,), jnp.float32) * 0.02, 'gnorm_w': jnp.ones((HV,), jnp.float32), 'Wg': lin(ks[7], VD, HID), 'Wo': lin(ks[8], HID, VD)}
    _L0_attn_all = _L0_attn_setup()
    _L0_attn_in = {k: v for k, v in _L0_attn_all.items() if k in ('Wq', 'Wk', 'Wv', 'Wgk1', 'Wgk2', 'bgk2', 'gnorm_w', 'Wg', 'Wo')}
    del _L0_attn_all

    def _L0_ffn_setup():
        import jax, jax.numpy as jnp
        import numpy as np
        K = 2
        EPS = 1e-06

        def _layernorm(x, gamma, beta):
            mu = jnp.mean(x, axis=-1, keepdims=True)
            var = jnp.mean(jnp.square(x - mu), axis=-1, keepdims=True)
            return (x - mu) * jax.lax.rsqrt(var + EPS) * gamma + beta
        key = jax.random.key(seed)
        ks = jax.random.split(key, 5)
        B, S, D, F, E = (8, 512, 128, 512, 8)
        x = jax.random.normal(ks[0], (B, S, D), dtype=jnp.float32)
        router_w = jax.random.normal(ks[1], (D, E), dtype=jnp.float32) * 0.02
        w1 = jax.random.normal(ks[2], (E, D, F), dtype=jnp.float32) * 0.02
        b1 = jnp.zeros((E, F), dtype=jnp.float32)
        w2 = jax.random.normal(ks[3], (E, F, D), dtype=jnp.float32) * 0.02
        b2 = jnp.zeros((E, D), dtype=jnp.float32)
        gamma = jnp.ones((E, D), dtype=jnp.float32)
        beta = jnp.zeros((E, D), dtype=jnp.float32)
        return {'x': x, 'router_w': router_w, 'w1': w1, 'b1': b1, 'w2': w2, 'b2': b2, 'gamma': gamma, 'beta': beta}
    _L0_ffn_all = _L0_ffn_setup()
    _L0_ffn_in = {k: v for k, v in _L0_ffn_all.items() if k in ('router_w', 'w1', 'b1', 'w2', 'b2', 'gamma', 'beta')}
    del _L0_ffn_all
    return {'x': x, 'cls_tok': cls_tok, 'L0_tok_gamma': _L0_tok_in['gamma'], 'L0_tok_beta': _L0_tok_in['beta'], 'L0_tok_W': _L0_tok_in['W'], 'L0_tok_b': _L0_tok_in['b'], 'L0_attn_Wq': _L0_attn_in['Wq'], 'L0_attn_Wk': _L0_attn_in['Wk'], 'L0_attn_Wv': _L0_attn_in['Wv'], 'L0_attn_Wgk1': _L0_attn_in['Wgk1'], 'L0_attn_Wgk2': _L0_attn_in['Wgk2'], 'L0_attn_bgk2': _L0_attn_in['bgk2'], 'L0_attn_gnorm_w': _L0_attn_in['gnorm_w'], 'L0_attn_Wg': _L0_attn_in['Wg'], 'L0_attn_Wo': _L0_attn_in['Wo'], 'L0_ffn_router_w': _L0_ffn_in['router_w'], 'L0_ffn_w1': _L0_ffn_in['w1'], 'L0_ffn_b1': _L0_ffn_in['b1'], 'L0_ffn_w2': _L0_ffn_in['w2'], 'L0_ffn_b2': _L0_ffn_in['b2'], 'L0_ffn_gamma': _L0_ffn_in['gamma'], 'L0_ffn_beta': _L0_ffn_in['beta']}

def reference(x, cls_tok, L0_tok_gamma, L0_tok_beta, L0_tok_W, L0_tok_b, L0_attn_Wq, L0_attn_Wk, L0_attn_Wv, L0_attn_Wgk1, L0_attn_Wgk2, L0_attn_bgk2, L0_attn_gnorm_w, L0_attn_Wg, L0_attn_Wo, L0_ffn_router_w, L0_ffn_w1, L0_ffn_b1, L0_ffn_w2, L0_ffn_b2, L0_ffn_gamma, L0_ffn_beta):
    import jax
    import jax.numpy as jnp

    def _L0_tok_ref(x, gamma, beta, W, b):
        import jax, jax.numpy as jnp
        import numpy as np
        HP = 4
        PATCH = 8
        EPS = 1e-07

        def _shifts(x):
            h, w = (x.shape[2], x.shape[3])
            pad2 = ((0, 0), (0, 0))
            left_up = jnp.pad(x[:, :, HP:, :w - HP], pad2 + ((0, HP), (HP, 0)))
            right_up = jnp.pad(x[:, :, HP:, HP:], pad2 + ((0, HP), (0, HP)))
            left_down = jnp.pad(x[:, :, :h - HP, :w - HP], pad2 + ((HP, 0), (HP, 0)))
            right_down = jnp.pad(x[:, :, :h - HP, HP:], pad2 + ((HP, 0), (0, HP)))
            return (left_up, right_up, left_down, right_down)
        lu, ru, ld, rd = _shifts(x)
        concat = jnp.concatenate((x, lu, ru, ld, rd), axis=1)
        mean = jnp.mean(concat, axis=(1, 2, 3), keepdims=True)
        var = jnp.var(concat, axis=(1, 2, 3), keepdims=True)
        normed = (concat - mean) * jax.lax.rsqrt(var + EPS)
        normed = normed * gamma[None] + beta[None]
        y = jax.lax.conv_general_dilated(normed, W, window_strides=(PATCH, PATCH), padding='VALID', dimension_numbers=('NCHW', 'OIHW', 'NCHW'))
        y = y + b[None, :, None, None]
        B, E = (y.shape[0], y.shape[1])
        y = y.reshape(B, E, -1).transpose(0, 2, 1)
        return y

    def _L0_attn_ref(hidden_states, Wq, Wk, Wv, Wgk1, Wgk2, bgk2, gnorm_w, Wg, Wo):
        import jax, jax.numpy as jnp
        import numpy as np
        B, T, HID = (4, 512, 128)
        NH = 4
        KD = 64
        VD = 128
        HK = KD // NH
        HV = VD // NH
        GLR = 16
        GATE_NORM = 16.0
        EPS = 1e-05
        Bv, Tv, _ = hidden_states.shape
        q = hidden_states @ Wq.T
        k = hidden_states @ Wk.T
        v = hidden_states @ Wv.T
        gk = hidden_states @ Wgk1.T @ Wgk2.T + bgk2
        q = q.reshape(Bv, Tv, NH, HK)
        k = k.reshape(Bv, Tv, NH, HK)
        v = v.reshape(Bv, Tv, NH, HV)
        gk = jax.nn.log_sigmoid(gk.reshape(Bv, Tv, NH, HK)) / GATE_NORM
        scale = np.float32(HK ** (-0.5))

        def step(S, xs):
            q_t, k_t, v_t, g_t = xs
            S = S * jnp.exp(g_t)[..., None] + k_t[..., None] * v_t[..., None, :]
            o_t = jnp.einsum('bhk,bhkv->bhv', q_t * scale, S)
            return (S, o_t)
        to_time_major = lambda x: jnp.swapaxes(x, 0, 1)
        S0 = jnp.zeros((Bv, NH, HK, HV), jnp.float32)
        _, o = jax.lax.scan(step, S0, (to_time_major(q), to_time_major(k), to_time_major(v), to_time_major(gk)))
        o = jnp.swapaxes(o, 0, 1)
        o = o * jax.lax.rsqrt(jnp.mean(o * o, axis=-1, keepdims=True) + EPS)
        o = o * gnorm_w
        o = o.reshape(Bv, Tv, NH * HV)
        g = hidden_states @ Wg.T
        o = o * (g * jax.nn.sigmoid(g))
        return o @ Wo.T

    def _L0_ffn_ref(x, router_w, w1, b1, w2, b2, gamma, beta):
        import jax, jax.numpy as jnp
        import numpy as np
        K = 2
        EPS = 1e-06

        def _layernorm(x, gamma, beta):
            mu = jnp.mean(x, axis=-1, keepdims=True)
            var = jnp.mean(jnp.square(x - mu), axis=-1, keepdims=True)
            return (x - mu) * jax.lax.rsqrt(var + EPS) * gamma + beta
        B, S, D = x.shape
        E = w1.shape[0]
        xf = x.reshape(-1, D)
        logits = xf @ router_w
        gate_vals, idx = jax.lax.top_k(logits, K)
        gates = jax.nn.softmax(gate_vals, axis=-1)
        out = jnp.zeros_like(xf)
        for e in range(E):
            h = jax.nn.relu(xf @ w1[e] + b1[e]) @ w2[e] + b2[e]
            y = _layernorm(xf + h, gamma[e], beta[e])
            w = jnp.sum(jnp.where(idx == e, gates, 0.0), axis=-1)
            out = out + w[:, None] * y
        return out.reshape(B, S, D)
    h = _L0_tok_ref(x, L0_tok_gamma, L0_tok_beta, L0_tok_W, L0_tok_b)
    h = jnp.concatenate([jnp.broadcast_to(cls_tok, (h.shape[0], 1, h.shape[2])), h], axis=1)
    h = h + _L0_attn_ref(_layernorm(h, axis=-1), L0_attn_Wq, L0_attn_Wk, L0_attn_Wv, L0_attn_Wgk1, L0_attn_Wgk2, L0_attn_bgk2, L0_attn_gnorm_w, L0_attn_Wg, L0_attn_Wo)
    h = h + _L0_ffn_ref(_layernorm(h, axis=-1), L0_ffn_router_w, L0_ffn_w1, L0_ffn_b1, L0_ffn_w2, L0_ffn_b2, L0_ffn_gamma, L0_ffn_beta)
    return h

_drawn_inputs = setup_inputs


def setup_inputs(seed=0):
    import zlib

    import numpy as np

    out = dict(_drawn_inputs(seed))
    spreads = {'L0_tok_b': (0.0, 0.1),
     'L0_attn_gnorm_w': (1.0, 0.2),
     'L0_ffn_b1': (0.0, 0.66),
     'L0_ffn_b2': (0.0, 0.1),
     'L0_ffn_gamma': (1.0, 0.2),
     'L0_ffn_beta': (0.0, 0.1)}
    factors = {'L0_attn_bgk2': 5.171}
    for name, (base, spread) in spreads.items():
        noise = np.random.default_rng([zlib.crc32(name.encode()), seed]).standard_normal(out[name].shape)
        drawn = base * np.exp(spread * noise) if base else spread * noise
        out[name] = jnp.asarray(drawn.astype(out[name].dtype))
    for name, factor in factors.items():
        out[name] = (out[name] * factor).astype(out[name].dtype)
    return out
```

```python
from contextlib import ExitStack

import numpy as np

import concourse.bass as bass
from concourse import mybir

DT = mybir.dt
ALU = mybir.AluOpType
ACT = mybir.ActivationFunctionType
AX_X = mybir.AxisListType.X
F32, F16, BF16, I32, U32 = DT.float32, DT.float16, DT.bfloat16, DT.int32, DT.uint32

BATCH, CH, SIDE, PATCH, HALF = 64, 2, 104, 8, 4
GRID = SIDE // PATCH
HGRID = GRID + 1
ROWLEN = PATCH * SIDE
NSHIFT = 5
E_DIM = 128
TOK = GRID * GRID + 1
CHUNK = TOK // 2
NTOK = BATCH * TOK
GROUP = 8
NGROUP = BATCH // GROUP
MROWS, HROWS = GROUP * GRID, GROUP * HGRID
PAIRS = BATCH // 2
PT = 2 * TOK
NH, HK, HV = 4, 16, 32
NEXP, FF = 8, 512
FC = FF // 128
SLOT = 256
REGION = NTOK + SLOT
NTILE = (2 * NTOK + NEXP * (SLOT - 1)) // SLOT
NTILE += NTILE % 2
XW = 130
PAD_ID = 2 * NTOK
W_SCALE = 256.0
N_CONCAT = float(CH * NSHIFT * SIDE * SIDE)
EPS_TOK, EPS_LN, EPS_GN, EPS_FFN = 1e-7, 1e-5, 1e-5, 1e-6


def const_layout():
    cols, at = {}, 0
    for name, n in (
        ("ident", 128), ("stat_all", 2 * HROWS), ("stat_edge", 2 * HROWS), ("causal", CHUNK),
        ("heads", 128), ("meanv", 128), ("before", CHUNK), ("ones", CHUNK), ("reset", PT),
        ("cls_sel", TOK), ("expert", 8), ("region", 8), ("eps", 8), ("tokid", 4), ("slotid", 2),
        ("tiles_k", 43), ("tile_no", NTILE), ("one_row", 128),
    ):
        cols[name] = (at, at + n)
        at += n
    return cols, at


def const_array():
    cols, width = const_layout()
    c = np.zeros((128, width), np.float32)

    def put(name):
        a, b = cols[name]
        return c[:, a:b]

    put("ident")[:] = np.eye(128)
    wt = np.array([1 if m in (0, HGRID - 1) else 2 for m in range(HGRID)] * GROUP, np.float32)
    img_h = np.repeat(np.arange(GROUP), HGRID)
    img_m = np.concatenate([np.repeat(np.arange(GROUP), GRID), np.full(HROWS - MROWS, -1)])
    for k, img in enumerate((img_h, img_m)):
        same = (img_h[:, None] == img[None, :]).astype(np.float32)
        put("stat_all")[:HROWS, k * HROWS:(k + 1) * HROWS] = same * (1 + 2 * wt[:, None])
        put("stat_edge")[:HROWS, k * HROWS:(k + 1) * HROWS] = -same * wt[:, None]
    s = np.arange(CHUNK)
    put("causal")[:CHUNK] = s[:, None] <= s[None, :]
    put("before")[:CHUNK] = s[:, None] < s[None, :]
    put("ones")[:CHUNK] = 1
    h = np.arange(128) // HV
    put("heads")[:] = h[:, None] == h[None, :]
    put("meanv")[:] = (h[:, None] == h[None, :]) / HV
    put("reset")[:] = (np.arange(PT) % CHUNK != 0)[None, :]
    put("cls_sel")[0, 1:] = 1
    put("cls_sel")[1, 0] = 1
    put("expert")[:] = np.arange(8)
    put("region")[:] = np.arange(8) * REGION
    put("eps")[:, 0:5] = [EPS_TOK, EPS_LN, EPS_GN, EPS_FFN, 1.0]
    put("eps")[:, 5] = -1 / 16
    put("eps")[:, 6] = 1 / 16
    put("tokid")[:CHUNK] = 2 * (s[:, None] + CHUNK * np.arange(4)[None, :])
    put("slotid")[:] = np.arange(128)[:, None] + 128 * np.arange(2)[None, :]
    put("tiles_k")[:] = SLOT * np.arange(43)
    put("one_row")[:] = 1
    put("tile_no")[:] = np.arange(NTILE)
    return c


def need(eng, sem, value):
    if not isinstance(value, int) or value > 0:
        eng.wait_ge(sem, value)


ARENA_WORDS = 28900


SPARE = []


def apart(eng):
    eng.sem_inc(SPARE[0], 1)


class Chain:

    def __init__(self, eng, sem):
        self.eng, self.sem, self.base, self.n = eng, sem, 0, 0

    def start(self, base):
        self.base, self.n = base, 0

    def link(self, ins):
        self.n += 1
        ins.then_inc(self.sem, 1)
        self.eng.wait_ge(self.sem, self.base + self.n)

    def step(self, ins):
        self.n += 1
        ins.then_inc(self.sem, 1)

    def settle(self):
        self.eng.wait_ge(self.sem, self.base + self.n)
        apart(self.eng)


MAIN_FILLS = [(0, 4), (4, 7), (7, 10), (10, 13)]
HALF_FILLS = [(0, 4), (4, 8), (8, 11), (11, 14)]
GROUP_DMAS = 2 * GROUP + 2


def build(nc, a, out_rows):
    cols, cwidth = const_layout()
    xs_dram = nc.dram_tensor("x_slots", (NEXP * REGION + SLOT, XW), F32, kind="Internal").ap()
    y_dram = nc.dram_tensor("y_tokens", (2 * NTOK, E_DIM), F32, kind="Internal").ap()

    with ExitStack() as ctx:
        def sb(name, shape, dt=F32):
            return ctx.enter_context(nc.sbuf_tensor(name, shape, dt))

        def sem(name):
            return ctx.enter_context(nc.semaphore(name))

        cst = sb("cst", [128, cwidth])

        def con(name, p=128):
            x, y = cols[name]
            return cst[0:p, x:y]

        ident = con("ident")
        eps = con("eps")
        h = sb("h", [128, PAIRS, 4, E_DIM])
        wt = sb("wt", [128, NSHIFT, E_DIM])
        bt = sb("bt", [CHUNK, 2, E_DIM])
        wproj = sb("wproj", [128, 6, E_DIM])
        nbgk = sb("nbgk", [128, 1])
        gnorm = sb("gnorm", [128, 1])
        rw = sb("rw", [128, NEXP])
        arena = sb("arena", [128, ARENA_WORDS])

        class Arena:
            def __init__(self):
                self.at = 0

            def take(self, *shape, dt=F32):
                n = int(np.prod(shape))
                words = n if dt in (F32, I32, U32) else (n + 1) // 2
                v = arena[:, self.at:self.at + words]
                self.at += words
                assert self.at <= ARENA_WORDS, self.at
                if dt is not F32:
                    v = v.bitcast(dt)
                if len(shape) > 1:
                    names = " ".join(f"d{i}" for i in range(len(shape)))
                    v = v.rearrange(f"p ({names}) -> p {names}", **{f"d{i}": s for i, s in enumerate(shape)})
                return v

        A0 = Arena()
        gx = [A0.take(NSHIFT, GROUP, TOK) for _ in range(2)]
        xm = [A0.take(CH * ROWLEN) for _ in range(2)]
        xh = [A0.take(CH * ROWLEN) for _ in range(2)]
        xmn = A0.take(GRID, CH * PATCH, PATCH)
        xhn = A0.take(HGRID, CH * PATCH, PATCH)
        xe = A0.take(2, CH * PATCH, PATCH)
        sqj = A0.take(CH * ROWLEN, dt=BF16)
        gam_t = A0.take(NSHIFT, GRID, GRID)
        st = sb("st", [128, 24])
        AP_ = Arena()
        wn = AP_.take(NSHIFT, CH * PATCH * PATCH)
        wn2 = AP_.take(6, E_DIM)
        wgk1 = AP_.take(E_DIM)
        wgk2t = AP_.take(E_DIM)
        bc = AP_.take(E_DIM)
        bet_t = AP_.take(NSHIFT, TOK)
        gb = [AP_.take(CH * ROWLEN) for _ in range(2)]
        b1_n = AP_.take(128)
        gbp = [AP_.take(GRID, CH * PATCH, PATCH) for _ in range(2)]
        assert AP_.at <= 13600

        A1 = Arena()
        xn = A1.take(4, E_DIM)
        xn_t = A1.take(PT)
        e_gk, l_gk, cum = A1.take(PT), A1.take(PT), A1.take(PT)
        decay, grow = A1.take(PT), A1.take(PT)
        qd, kd = A1.take(PT), A1.take(PT)
        gate, e_g, l_g = A1.take(PT), A1.take(PT), A1.take(PT)
        val = A1.take(4, E_DIM)
        att = A1.take(NH, 4, CHUNK)
        k_tok = A1.take(2, 128)
        state = A1.take(2, 128)
        o_sq, l_ms, u_exp, fac, o_g, o_f = (A1.take(PT) for _ in range(6))
        bns, mv, rs1, rstd1 = A1.take(4, 6), A1.take(4, 2), A1.take(4), A1.take(4)
        bns2, mv2, rs2, rstd2 = A1.take(4, 6), A1.take(4, 2), A1.take(4), A1.take(4)
        row = A1.take(2, 4, XW)
        xn2_t = A1.take(PT)
        lg, mx = A1.take(4, NEXP), A1.take(4, 8)
        mi = A1.take(4, 8, dt=U32)
        ef, oh, om = A1.take(4, 2), A1.take(4, 2, NEXP), A1.take(4, NEXP)
        rk, base, pos, pp = A1.take(2, 4, NEXP), A1.take(NEXP), A1.take(4, NEXP), A1.take(4, 2, NEXP)
        slot_f, dif, edif, den = A1.take(4, 2), A1.take(4), A1.take(4), A1.take(4)
        slot_i = A1.take(4, 2, dt=I32)
        ids = A1.take(4)
        cnt = A1.take(NEXP)
        cnt_all, pad_f = A1.take(NEXP), A1.take(NEXP)
        pad_i = A1.take(2, NEXP, dt=I32)
        pad_row = A1.take(2, XW)
        more, ntiles, tile_end, skip = A1.take(NEXP, 43), A1.take(NEXP), A1.take(NEXP), A1.take(NEXP)
        assert A1.at <= 11300, A1.at
        A2 = Arena()
        A2.at = 11300
        b2_all, gam_all, bet_all = (A2.take(NEXP, E_DIM) for _ in range(3))
        w1_hi, w1_lo = A2.take(NEXP, FF, dt=F16), A2.take(NEXP, FF, dt=F16)
        w2_sb = A2.take(NEXP, FC, E_DIM)
        w1_raw = A2.take(NEXP, FF)
        at = A2.at
        A3 = Arena()
        A3.at = at - NEXP * FF
        x_sl = [A3.take(2, XW) for _ in range(4)]
        x_hi, x_lo = [A3.take(SLOT, dt=F16) for _ in range(2)], [A3.take(SLOT, dt=F16) for _ in range(2)]
        hid = [A3.take(FC, SLOT)]
        assert A3.at <= at
        A3.at = at
        hid.append(A3.take(FC, SLOT))
        A3.at = 0
        x_b2 = [A3.take(2, E_DIM) for _ in range(2)]
        res, nrm, scl = A3.take(2, E_DIM), A3.take(2, E_DIM), A3.take(2, E_DIM)
        y_sl = [A3.take(2, E_DIM) for _ in range(2)]
        bns3, mv3, ln3, rstd3, rg3 = (A3.take(2, 6), A3.take(2, 2), A3.take(2), A3.take(2), A3.take(2))
        y_id = [A3.take(2, dt=I32) for _ in range(2)]
        y_tok = [A3.take(4, 2, E_DIM) for _ in range(4)]
        assert A3.at <= 11300
        tile_tab = sb("tile_tab", [1, 2, NTILE], I32)
        tab_f = sb("tab_f", [1, 2, NTILE])
        b1_t = sb("b1_t", [128, NEXP * FC])

        ps = [ctx.enter_context(nc.psum_tensor(f"ps{i}", [128, 512], F32)) for i in range(8)]

        names = (
            "c_loaded z_prep w_loaded prep_done xl0 xl1 edge_done dsum_done asum_done stat_ps var_done "
            "h_out "
            "ln1_stats ln1_rstd xn_ready xnt_ps xnt_sb gk_ps qk_ps g_ps v_ps l_ready scan_done e_ready g_copied g_ready "
            "v_ready qk_ready sc_ps att_ready kt_ps kt_ready st_ps state_ready o_ps sq_ready ms_ps lms_ready u_ready "
            "fac_ready o_ready ao_ps h1_ready ln2_stats ln2_rstd xn2_ready xn2t_ps xn2t_sb lg_ps om_ready dif_ready "
            "edif_ready rk_ps slots_ready rows_ready row_copied scattered base_ready aln pln w1_loaded fw_loaded w1_split cnt_ready cnt_ps pad_ready tab_ready pad_gone pad_stored xs0 xs1 xs2 xs3 xt_ps xhi_ready xlo_ready h_ps h_ready w2_ps xb_ready t_ready rstd3_stats rstd3_ready y_ready yg0 yg1 meta_ready yl0 yl1 yl2 yl3 sum_ready pz "
            "rstd0_done nb_done xmn_done xhn_done tr_full tr_free y_full y_free dch ach pch t_prep d_prep xen_done"
        ).split()
        S = {n: sem(n) for n in names}
        x_loaded = [S["xl0"], S["xl1"]]
        SPARE[:] = [sem("passed")]
        block = ctx.enter_context(nc.Block())

        x_sl_loaded = [S[f"xs{n}"] for n in range(4)]
        y_gone = [S["yg0"], S["yg1"]]
        y_loaded = [S[f"yl{n}"] for n in range(4)]
        STEADY = range(4, NTILE - 4)

        def tiles(eng, step):
            for i in range(-1, STEADY.start):
                step(i, i % 4, i // 4)
            with eng.Fori(0, len(STEADY) // 4) as k:
                for j in range(4):
                    i = STEADY.start + j
                    step(4 * k + i, i % 4, k + i // 4)
            for i in range(STEADY.stop, NTILE + 2):
                step(i, i % 4, i // 4)

        def live(i):
            return not isinstance(i, int) or 0 <= i < NTILE

        def expert_sync(sp):
            sp.wait_ge(S["y_free"], 4 * NGROUP)
            sp.dma_start(w1_raw, a["L0_ffn_w1"].rearrange("e d f -> d e f")).then_inc(S["w1_loaded"], 16)
            for e in range(NEXP):
                sp.dma_start(w2_sb[:, e], a["L0_ffn_w2"][e].rearrange("(c f) n -> f c n", c=FC)).then_inc(S["fw_loaded"], 16)
            for dst, name in ((b2_all, "L0_ffn_b2"), (gam_all, "L0_ffn_gamma"), (bet_all, "L0_ffn_beta")):
                src = a[name].rearrange("(o e) n -> o e n", o=1).to_broadcast([128, NEXP, E_DIM])
                sp.dma_start(dst, src).then_inc(S["fw_loaded"], 16)
            sp.wait_ge(S["pad_ready"], 1)
            sp.wait_ge(S["w1_split"], 4)
            sp.dma_start(xs_dram[NEXP * REGION:NEXP * REGION + SLOT, :].rearrange("(s p) w -> p s w", s=2), pad_row)\
              .then_inc(S["pad_stored"], 16)
            sp.wait_ge(S["pad_stored"], 16)
            sp.wait_ge(S["tab_ready"], 1)
            sp.wait_ge(S["w1_split"], 4)
            sp.wait_ge(S["scattered"], 128 * PAIRS)
            sp.wait_ge(S["pad_gone"], 16 * 2 * NEXP)

            def load(i, n):
                need(sp, S["y_ready"], i - 3)
                r = sp.value_load(tile_tab[0:1, 0, bass.ds(i, 1)], min_val=0, max_val=NEXP * REGION)
                sp.dma_start(x_sl[n], xs_dram[bass.ds(r, SLOT), :].rearrange("(s p) w -> p s w", s=2))\
                  .then_inc(x_sl_loaded[n], 16)

            for n in range(4):
                load(n, n)
            with sp.Fori(1, NTILE // 4) as k:
                for n in range(4):
                    load(4 * k + n, n)

            for gone in y_gone:
                sp.wait_ge(gone, 32 * (NTILE // 2))

            def load_y(p, n):
                need(sp, S["sum_ready"], 2 * (p - 3))
                sp.dma_start(y_tok[n][0:CHUNK], y_dram[bass.ds(p * 2 * PT, 2 * PT), :].rearrange(
                    "(c r k) n -> r c k n", c=4, k=2)).then_inc(y_loaded[n], 16)

            for n in range(4):
                load_y(n, n)
            with sp.Fori(1, PAIRS // 4) as k:
                for n in range(4):
                    load_y(4 * k + n, n)

        @block.sync
        def _(sp):
            sp.dma_start(cst[:], a["consts"]).then_inc(S["c_loaded"], 16)
            sp.wait_ge(S["z_prep"], 1)
            n = 0

            def load(dst, src):
                nonlocal n
                n += 1
                sp.dma_start(dst, src).then_inc(S["w_loaded"], 16)

            load(wn[:, :, :], a["L0_tok_W"].rearrange("e (s c) p q -> e s (c p q)", c=CH))
            for k, name in ((0, "L0_tok_gamma"), (1, "L0_tok_beta")):
                for s in range(NSHIFT):
                    load(gb[k][GRID * s:GRID * s + GRID, :].rearrange("i (c r) -> i c r", c=CH),
                         a[name][CH * s:CH * s + CH].rearrange("c (i p) w -> i c (p w)", p=PATCH))
            load(bc[0:1, :], a["L0_tok_b"].rearrange("(o n) -> o n", o=1))
            load(bc[1:2, :], a["cls_tok"][0])
            for hd in range(NH):
                r = slice(HV * hd, HV * hd + HK)
                s = slice(HK * hd, HK * hd + HK)
                load(wn2[r, 0, :], a["L0_attn_Wq"][s, :])
                load(wn2[r, 1, :], a["L0_attn_Wk"][s, :])
                load(wn2[r, 2, 0:16], a["L0_attn_Wgk2"][s, :])
                load(nbgk[r, :], a["L0_attn_bgk2"][s].rearrange("(n o) -> n o", o=1))
                load(gnorm[HV * hd:HV * hd + HV, :], a["L0_attn_gnorm_w"].rearrange("(n o) -> n o", o=1))
            load(wgk1[0:16, :], a["L0_attn_Wgk1"])
            load(wn2[:, 3, :], a["L0_attn_Wg"])
            load(wn2[:, 4, :], a["L0_attn_Wv"])
            load(wn2[:, 5, :], a["L0_attn_Wo"])
            load(rw[:, :], a["L0_ffn_router_w"])
            load(b1_n[0:NEXP * FC, :], a["L0_ffn_b1"].rearrange("e (c f) -> (e c) f", c=FC))
            assert n == N_WLOADS, n

            def load_group(g, par):
                need(sp, S["xmn_done"], g - 1)
                need(sp, S["xhn_done"], g - 1)
                for b in range(GROUP):
                    img = a["x"][bass.ds(g * GROUP + b, 1)]
                    sp.dma_start(
                        xm[par][GRID * b:GRID * b + GRID, :].rearrange("i (c r) -> i c r", c=CH),
                        img.rearrange("o c (i p) w -> (o i) c (p w)", p=PATCH),
                    ).then_inc(x_loaded[par], 16)
                    sp.dma_start(
                        xh[par][HGRID * b + 1:HGRID * b + GRID, :].rearrange("m (c r) -> m c r", c=CH),
                        img[:, :, HALF:SIDE - HALF, :].rearrange("o c (m p) w -> (o m) c (p w)", p=PATCH),
                    ).then_inc(x_loaded[par], 16)
                edge = HALF * SIDE
                imgs = a["x"][bass.ds(g * GROUP, GROUP)]
                for m, r0, at in ((0, 0, edge), (HGRID - 1, SIDE - HALF, 0)):
                    sp.dma_start(
                        xh[par][m:m + (GROUP - 1) * HGRID + 1:HGRID, :].rearrange("b (c r) -> b c r", c=CH)[:, :, at:at + edge],
                        imgs[:, :, r0:r0 + HALF, :].rearrange("b c p w -> b c (p w)"),
                    ).then_inc(x_loaded[par], 16)

            load_group(0, 0)
            load_group(1, 1)
            with sp.Fori(1, NGROUP // 2) as k:
                load_group(2 * k, 0)
                load_group(2 * k + 1, 1)
            expert_sync(sp)

        @block.gpsimd
        def _(pool):
            for t in (wn2, nbgk[:, :], bet_t, xh[0], xh[1]):
                pool.memset(t, 0.0).then_inc(S["pch"], 1)
            pool.wait_ge(S["pch"], 5)
            pool.memset(st[:, :], 0.0).then_inc(S["z_prep"], 1)
            pool.wait_ge(S["prep_done"], 1)
            for t in (gx[0][:, :, :, 0:1], gx[1][:, :, :, 0:1], xe):
                pool.memset(t, 0.0).then_inc(S["pch"], 1)

            sc = S["scattered"]

            def scatter(p):
                pool.wait_ge(S["rows_ready"], p + 1)
                pool.wait_ge(S["row_copied"], p + 1)
                apart(pool)
                for t in range(4):
                    for k in range(2):
                        pool.indirect_dma_start(
                            xs_dram, bass.IndirectOffsetOnAxis(ap=slot_i[0:CHUNK, t, k:k + 1], axis=0),
                            row[0:CHUNK, k, t, :], None).then_inc(sc, 16)

            pool.wait_ge(S["w1_loaded"], 16)
            W = S["w1_split"]
            pool.tensor_scalar(w1_raw, w1_raw, W_SCALE, None, ALU.mult).then_inc(W, 1)
            pool.wait_ge(W, 1)
            pool.tensor_copy(w1_hi, w1_raw).then_inc(W, 1)
            pool.wait_ge(W, 2)
            pool.tensor_tensor(w1_lo, w1_raw, w1_hi, ALU.subtract).then_inc(W, 1)
            pool.wait_ge(W, 3)
            pool.memset(pad_row[:, :, 0:129], 0.0).then_inc(W, 1)
            pool.wait_ge(S["base_ready"], 1)
            pool.memset(pad_row[:, :, 129:130], float(PAD_ID)).then_inc(S["pad_ready"], 1)

            with pool.Fori(0, PAIRS) as p:
                scatter(p)

            pool.wait_ge(S["cnt_ready"], 2)
            pool.wait_ge(W, 4)
            pool.wait_ge(S["pad_ready"], 1)
            for e in range(NEXP):
                for k in range(2):
                    pool.indirect_dma_start(
                        xs_dram, bass.IndirectOffsetOnAxis(ap=pad_i[:, k, e:e + 1], axis=0),
                        pad_row[:, k, :], None).then_inc(S["pad_gone"], 16)

            pool.wait_ge(S["fw_loaded"], 16 * (NEXP + 3))
            pool.wait_ge(S["pad_gone"], 16 * 2 * NEXP)

            def tile_step(i, n, u):
                if live(i):
                    pool.wait_ge(x_sl_loaded[n], 16 * u + 16)
                    need(pool, S["t_ready"], i - 1)
                    apart(pool)
                    e = pool.value_load(tile_tab[0:1, 1, bass.ds(i, 1)], min_val=0, max_val=NEXP - 1)
                    b2 = b2_all[:, bass.ds(e, 1), :].to_broadcast([128, 2, E_DIM])
                    pool.tensor_tensor(x_b2[n % 2], x_sl[n][:, :, 0:E_DIM], b2, ALU.add).then_inc(S["xb_ready"], 1)
                if live(i - 2):
                    pool.wait_ge(S["y_ready"], i - 1)
                    apart(pool)
                    for k in range(2):
                        pool.indirect_dma_start(
                            y_dram, bass.IndirectOffsetOnAxis(ap=y_id[n % 2][:, k:k + 1], axis=0),
                            y_sl[n % 2][:, k, :], None, bounds_check=2 * NTOK - 1, oob_is_err=False,
                        ).then_inc(y_gone[n % 2], 16)

            tiles(pool, tile_step)

        @block.tensor
        def _(pe):
            pe.wait_ge(S["c_loaded"], 16)
            pe.wait_ge(S["w_loaded"], 16 * N_WLOADS)
            T, D = S["t_prep"], S["d_prep"]
            for s in range(NSHIFT):
                ins = pe.transpose(ps[s // 4][:, 128 * (s % 4):128 * (s % 4) + 128], wn[:, s, :], ident)
            ins.then_inc(T, 1)
            for k in range(2):
                pe.wait_ge(D, 2 + k + 1)
                for j in range(GRID):
                    ins = pe.transpose(ps[2 + 2 * k + j // 7][:, 65 * (j % 7):65 * (j % 7) + 65],
                                       gbp[k][0:65, j].rearrange("r a b -> r (a b)"), ident[0:65, 0:65])
                ins.then_inc(T, 1)
            for n, w in enumerate((0, 1, 3, 4)):
                ins = pe.transpose(ps[6][:, 128 * n:128 * n + 128], wn2[:, w, :], ident)
            ins.then_inc(T, 1)
            pe.transpose(ps[7][:, 0:128], wn2[:, 5, :], ident)
            pe.transpose(ps[7][:, 384:384 + NEXP * FC], b1_n[0:NEXP * FC, :], ident[0:NEXP * FC, 0:NEXP * FC])
            pe.transpose(ps[7][0:16, 128:256], wn2[:, 2, 0:16], ident).then_inc(T, 1)
            pe.wait_ge(D, 8)
            pe.matmul(ps[7][:, 256:384], wgk1[0:16, :], wgk2t[0:16, :], start=True, stop=True).then_inc(T, 1)
            pe.wait_ge(D, 9)
            for hf in range(2):
                o = ps[0][0:CHUNK, 128 * hf:128 * hf + 128]
                for s in range(NSHIFT):
                    pe.matmul(o, bet_t[:, s, CHUNK * hf:CHUNK * hf + CHUNK], wt[:, s, :], start=s == 0, stop=False)
                x0, _y = cols["cls_sel"]
                ins = pe.matmul(o, cst[0:2, x0 + CHUNK * hf:x0 + CHUNK * hf + CHUNK], bc[0:2, :], start=False, stop=True)
            ins.then_inc(T, 1)

            fills = [[(xmn[0:MROWS, j], MROWS) for j in range(*f)] for f in MAIN_FILLS]
            fills += [[(xhn[0:HROWS, n], HROWS) for n in range(*f)] for f in HALF_FILLS]

            def transpose_fill(g, par, k):
                if k == 0:
                    pe.wait_ge(S["xmn_done"], g + 1)
                if k == 4:
                    pe.wait_ge(S["xhn_done"], g + 1)
                    pe.wait_ge(S["xen_done"], g + 1)
                need(pe, S["tr_free"], 8 * g + k - 3)
                for n, (src, rows) in enumerate(fills[k]):
                    ins = pe.transpose(ps[k % 4][:, rows * n:rows * n + rows],
                                       src.rearrange("r a b -> r (a b)"), ident[0:rows, 0:rows])
                ins.then_inc(S["tr_full"], 1)

            def y_fill(g, par, k):
                if k == 0:
                    pe.wait_ge(S["tr_free"], 8 * g + 8)
                need(pe, S["y_free"], 4 * g + k - 1)
                for t in range(4):
                    b, hf = 2 * k + t // 2, t % 2
                    for s in range(NSHIFT):
                        ins = pe.matmul(ps[4 + k % 2][0:CHUNK, 128 * t:128 * t + 128],
                                        gx[par][:, s, b, CHUNK * hf:CHUNK * hf + CHUNK], wt[:, s, :],
                                        start=s == 0, stop=s == NSHIFT - 1)
                ins.then_inc(S["y_full"], 1)

            def stats(g):
                pe.wait_ge(S["dsum_done"], g + 1)
                pe.wait_ge(S["asum_done"], g + 1)
                need(pe, S["var_done"], g)
                x0 = cols["stat_all"][0]
                x1 = cols["stat_edge"][0]
                for k in range(2):
                    o = ps[6][0:HROWS, 2 * k:2 * k + 2]
                    pe.matmul(o, cst[0:HROWS, x0 + k * HROWS:x0 + (k + 1) * HROWS], st[0:HROWS, 0:2], start=True, stop=False)
                    ins = pe.matmul(o, cst[0:HROWS, x1 + k * HROWS:x1 + (k + 1) * HROWS], st[0:HROWS, 2:4],
                                    start=False, stop=True)
                ins.then_inc(S["stat_ps"], 1)

            def group(g, par, tr=True, y=True, stat=True):
                for k in range(8):
                    if tr:
                        transpose_fill(g, par, k)
                    if k % 2 and y:
                        y_fill(g - 1, 1 - par, k // 2)
                    if k == 3 and stat:
                        stats(g + 1)

            pe.wait_ge(S["prep_done"], 1)
            stats(0)
            group(0, 0, y=False)
            group(1, 1)
            group(2, 0)
            with pe.Fori(1, NGROUP // 2 - 1) as k:
                group(2 * k + 1, 1)
                group(2 * k + 2, 0)
            group(NGROUP - 1, 1, stat=False)
            group(NGROUP, 0, tr=False, stat=False)

            def chunk(c):
                return slice(CHUNK * c, CHUNK * c + CHUNK)

            def project(p):
                pe.wait_ge(S["xn_ready"], 4 * p + 4)
                need(pe, S["slots_ready"], p - 1)
                for c in range(4):
                    ins = pe.transpose(ps[0][:, chunk(c)], xn[0:CHUNK, c, :], ident[0:CHUNK, 0:CHUNK])
                ins.then_inc(S["xnt_ps"], 1)
                pe.wait_ge(S["xnt_sb"], p + 1)
                need(pe, S["att_ready"], 4 * p)
                pe.matmul(ps[4][:, 0:PT], wproj[:, 2, :], xn_t, start=True, stop=True).then_inc(S["gk_ps"], 1)
                pe.matmul(ps[5][:, 0:PT], wproj[:, 0, :], xn_t, start=True, stop=True)
                pe.matmul(ps[6][:, 0:PT], wproj[:, 1, :], xn_t, start=True, stop=True).then_inc(S["qk_ps"], 1)
                pe.matmul(ps[7][:, 0:PT], wproj[:, 3, :], xn_t, start=True, stop=True).then_inc(S["g_ps"], 1)
                need(pe, S["state_ready"], 2 * p)
                for c in range(4):
                    ins = pe.matmul(ps[1][0:CHUNK, 128 * c:128 * c + 128], xn_t[:, chunk(c)], wproj[:, 4, :],
                                    start=True, stop=True)
                ins.then_inc(S["v_ps"], 1)

            def scores(p):
                pe.wait_ge(S["qk_ready"], 2 * p + 2)
                pe.wait_ge(S["g_copied"], p + 1)
                for hd in range(NH):
                    r = slice(HV * hd, HV * hd + HV)
                    for c in range(4):
                        ins = pe.matmul(ps[4 + hd][0:CHUNK, chunk(c)], kd[r, chunk(c)], qd[r, chunk(c)],
                                        start=True, stop=True, tile_position=(HV * hd, 0))
                    ins.then_inc(S["sc_ps"], 1)

            def keys(p):
                pe.wait_ge(S["v_ready"], p + 1)
                for i in range(2):
                    ins = pe.transpose(ps[1][0:CHUNK, 128 * i:128 * i + 128], kd[:, chunk(2 * i)], ident)
                ins.then_inc(S["kt_ps"], 1)

            def states(p):
                pe.wait_ge(S["kt_ready"], p + 1)
                for i in range(2):
                    ins = pe.matmul(ps[1][:, 256 + 128 * i:384 + 128 * i], k_tok[0:CHUNK, i, :], val[0:CHUNK, 2 * i, :],
                                    start=True, stop=True)
                ins.then_inc(S["st_ps"], 1)

            def outputs(p):
                pe.wait_ge(S["att_ready"], 4 * p + 4)
                need(pe, S["o_ready"], p)
                for c in range(4):
                    if c % 2:
                        pe.wait_ge(S["state_ready"], 2 * p + (c + 1) // 2)
                        pe.matmul(ps[2][:, chunk(c)], state[:, c // 2, :], qd[:, chunk(c)], start=True, stop=True)
                    for hd in range(NH):
                        r = slice(HV * hd, HV * hd + HV)
                        ins = pe.matmul(ps[2][r, chunk(c)], val[0:CHUNK, c, r], att[0:CHUNK, hd, c, :],
                                        start=c % 2 == 0, stop=True, tile_position=(0, HV * hd),
                                        skip_group_check=True)
                ins.then_inc(S["o_ps"], 1)

            def mean_squares(p):
                pe.wait_ge(S["sq_ready"], p + 1)
                need(pe, S["h1_ready"], p)
                pe.matmul(ps[3][:, 0:PT], con("meanv"), o_sq, start=True, stop=True).then_inc(S["ms_ps"], 1)

            def attention_out(p):
                pe.wait_ge(S["o_ready"], p + 1)
                for c in range(4):
                    ins = pe.matmul(ps[3][0:CHUNK, 128 * c:128 * c + 128], o_f[:, chunk(c)], wproj[:, 5, :],
                                    start=True, stop=True)
                ins.then_inc(S["ao_ps"], 1)

            def route_transpose(p):
                pe.wait_ge(S["xn2_ready"], 4 * p + 4)
                for c in range(4):
                    ins = pe.transpose(ps[0][:, chunk(c)], row[0:CHUNK, 0, c, 0:128], ident[0:CHUNK, 0:CHUNK])
                ins.then_inc(S["xn2t_ps"], 1)

            def route_logits(p):
                pe.wait_ge(S["xn2t_sb"], p + 1)
                for c in range(4):
                    ins = pe.matmul(ps[0][0:CHUNK, 352 + 8 * c:360 + 8 * c], xn2_t[:, chunk(c)], rw[:, :],
                                    start=True, stop=True)
                ins.then_inc(S["lg_ps"], 1)

            def ranks(p):
                pe.wait_ge(S["om_ready"], p + 1)
                o2 = om[0:CHUNK].rearrange("p c e -> p (c e)")
                pe.matmul(ps[0][0:CHUNK, 384:416], con("before", CHUNK), o2, start=True, stop=True)
                pe.matmul(ps[0][0:CHUNK, 416:448], con("ones", CHUNK), o2, start=True, stop=True).then_inc(S["rk_ps"], 1)

            def pair(p, route=True, attend=True):
                if attend:
                    project(p)
                if route:
                    if attend:
                        pe.wait_ge(S["xnt_sb"], p + 1)
                    route_transpose(p - 1)
                if attend:
                    scores(p)
                    keys(p)
                if route:
                    route_logits(p - 1)
                if attend:
                    states(p)
                if route:
                    ranks(p - 1)
                if attend:
                    outputs(p)
                    mean_squares(p)
                    attention_out(p)

            pair(0, route=False)
            pair(1)
            with pe.Fori(2, PAIRS) as p:
                pair(p)
            pair(PAIRS, attend=False)

            pe.wait_ge(S["cnt_ready"], 1)
            pe.matmul(ps[0][:, 0:NEXP], con("one_row", 1), cnt[0:1, :], start=True, stop=True).then_inc(S["cnt_ps"], 1)
            pe.wait_ge(S["tab_ready"], 1)
            pe.wait_ge(S["w1_split"], 3)
            pe.wait_ge(S["fw_loaded"], 16 * (NEXP + 3))

            def tile_step(i, n, u):
                m = n % 2
                if live(i):
                    pe.wait_ge(S["xlo_ready"], i + 1)
                    need(pe, S["h_ready"], 4 * (i - 1))
                    apart(pe)
                    e = pe.value_load(tile_tab[0:1, 1, bass.ds(i, 1)], min_val=0, max_val=NEXP - 1)
                    for c in range(FC):
                        o = ps[2 + 2 * m + c // 2][:, SLOT * (c % 2):SLOT * (c % 2) + SLOT]
                        f = slice(128 * c, 128 * c + 128)
                        hi = w1_hi[:, bass.ds(e, 1), f].rearrange("p o f -> p (o f)")
                        lo = w1_lo[:, bass.ds(e, 1), f].rearrange("p o f -> p (o f)")
                        pe.matmul(o, hi, x_hi[m], start=True, stop=False)
                        pe.matmul(o, hi, x_lo[m], start=False, stop=False)
                        pe.matmul(o, lo, x_hi[m], start=False, stop=True).then_inc(S["h_ps"], 1)
                if live(i + 1):
                    n1 = (n + 1) % 4
                    u1 = u + (n == 3)
                    pe.wait_ge(x_sl_loaded[n1], 16 * u1 + 16)
                    need(pe, S["xlo_ready"], i)
                    for k in range(2):
                        ins = pe.transpose(ps[1 - m][:, 128 * k:128 * k + 128], x_sl[n1][:, k, 0:E_DIM], ident)
                    ins.then_inc(S["xt_ps"], 1)
                if live(i - 1):
                    pe.wait_ge(S["h_ready"], 4 * i)
                    need(pe, S["t_ready"], i - 2)
                    apart(pe)
                    e = pe.value_load(tile_tab[0:1, 1, bass.ds(i - 1, 1)], min_val=0, max_val=NEXP - 1)
                    for k in range(2):
                        for c in range(FC):
                            ins = pe.matmul(ps[7 - m][:, 128 * k:128 * k + 128], hid[1 - m][:, c, 128 * k:128 * k + 128],
                                            w2_sb[:, bass.ds(e, 1), c, :].rearrange("p o n -> p (o n)"),
                                            start=c == 0, stop=c == FC - 1)
                    ins.then_inc(S["w2_ps"], 1)

            tiles(pe, tile_step)

        @block.vector
        def _(dve):
            ch = Chain(dve, S["dch"])
            T, D = S["t_prep"], S["d_prep"]
            dve.wait_ge(T, 1)
            dve.tensor_copy(wt[:, 0:4, :], ps[0][:, :].rearrange("p (s n) -> p s n", s=4)).then_inc(D, 1)
            dve.tensor_copy(wt[:, 4, :], ps[1][:, 0:128]).then_inc(D, 1)
            dve.wait_ge(S["w_loaded"], 16 * N_WLOADS)
            for k in range(2):
                dve.tensor_copy(gbp[k][0:65], gb[k][0:65, :].rearrange(
                    "r (cp j q) -> r j cp q", j=GRID, q=PATCH)).then_inc(D, 1)
            dve.wait_ge(T, 3)
            for k in range(2):
                for half, (j0, j1) in enumerate(((0, 7), (7, 13))):
                    src = ps[2 + 2 * k + half][:, 0:65 * (j1 - j0)].rearrange("p (j s i) -> p s i j", s=NSHIFT, i=GRID)
                    for s in range(NSHIFT):
                        dst = (gam_t[:, s] if k == 0 else
                               bet_t[:, s, 1:TOK].rearrange("p (i j) -> p i j", i=GRID))[:, :, j0:j1]
                        ins = dve.tensor_copy(dst, src[:, s])
                        if not (k and half and s == NSHIFT - 1):
                            ins.then_inc(S["dch"], 1)
                            ch.n += 1
            ins.then_inc(D, 1)
            dve.wait_ge(T, 5)
            dve.tensor_copy(b1_t[:, :], ps[7][:, 384:384 + NEXP * FC]).then_inc(S["dch"], 1)
            ch.n += 1
            dve.tensor_scalar(wproj[:, 0, :], ps[6][:, 0:128], HK ** -0.5, None, ALU.mult).then_inc(D, 1)
            dve.tensor_copy(wproj[:, 1, :], ps[6][:, 128:256]).then_inc(D, 1)
            dve.tensor_copy(wgk2t[0:16, :], ps[7][0:16, 128:256]).then_inc(D, 1)
            dve.wait_ge(T, 6)
            dve.tensor_copy(wproj[:, 3:5, :], ps[6][:, 256:512].rearrange("p (a n) -> p a n", a=2)).then_inc(S["dch"], 1)
            dve.tensor_scalar(wproj[:, 5, :], ps[7][:, 0:128], gnorm[:, 0:1], None, ALU.mult).then_inc(S["dch"], 1)
            dve.tensor_scalar(nbgk[:, :], nbgk[:, :], -1.0, None, ALU.mult).then_inc(S["dch"], 1)
            ch.n += 3
            dve.tensor_copy(wproj[:, 2, :], ps[7][:, 256:384]).then_inc(D, 1)
            dve.wait_ge(T, 7)
            ch.link(dve.tensor_copy(bt[:, :, :], ps[0][0:CHUNK, 0:256].rearrange("p (a n) -> p a n", a=2)))
            dve.tensor_copy(st[0:1, 20:21], st[0:1, 21:22]).then_inc(S["prep_done"], 1)
            dve.wait_ge(S["pch"], 8)
            dbase = ch.n

            def stats_sums(g, par, u):
                dve.wait_ge(x_loaded[par], 16 * GROUP_DMAS * (u + 1))
                need(dve, S["xen_done"], g)
                need(dve, S["asum_done"], g)
                need(dve, S["stat_ps"], g)
                x3 = xh[par][0:HROWS, :].rearrange("r (cp w) -> r cp w", w=SIDE)
                ch.link(dve.tensor_copy(xe[0:HROWS, 0, :, HALF:PATCH], x3[:, :, 0:HALF]))
                dve.tensor_copy(xe[0:HROWS, 1, :, 0:HALF], x3[:, :, SIDE - HALF:SIDE]).then_inc(S["edge_done"], 1)
                dve.wait_ge(S["edge_done"], g + 1)
                ch.link(dve.tensor_reduce(st[0:HROWS, 2:3], xe[0:HROWS].rearrange("r a b c -> r (a b c)"), AX_X, ALU.add))
                dve.tensor_reduce(st[0:HROWS, 0:1], xh[par][0:HROWS, :], AX_X, ALU.add).then_inc(S["dsum_done"], 1)

            def stats_small(g):
                dve.wait_ge(S["stat_ps"], g + 1)
                need(dve, S["xhn_done"], g)
                m = st[0:HROWS, 4:8].rearrange("r (k a) -> r k a", k=2)
                ch.link(dve.tensor_scalar(st[0:HROWS, 4:8], ps[6][0:HROWS, 0:4], 1.0 / N_CONCAT, None, ALU.mult))
                ch.link(dve.tensor_tensor(st[0:HROWS, 8:10], m[:, :, 0], m[:, :, 0], ALU.mult))
                dve.tensor_tensor(st[0:HROWS, 10:12], m[:, :, 1], st[0:HROWS, 8:10], ALU.subtract).then_inc(S["var_done"], 1)

            def normalise(g, par):
                m = st[0:HROWS, 4:8].rearrange("r (k a) -> r k a", k=2)
                dve.wait_ge(S["rstd0_done"], g + 1)
                dve.scalar_tensor_tensor(st[0:HROWS, 16:18], m[:, :, 0], -1.0, st[0:HROWS, 14:16],
                                         ALU.mult, ALU.mult).then_inc(S["nb_done"], 1)
                dve.wait_ge(S["nb_done"], g + 1)
                need(dve, S["tr_full"], 8 * g)
                dve.tensor_scalar(xhn[0:HROWS, 0:HGRID:HGRID - 1], xe[0:HROWS], st[0:HROWS, 14:15], st[0:HROWS, 16:17],
                                  ALU.mult, ALU.add).then_inc(S["xen_done"], 1)
                dve.tensor_scalar(xmn[0:MROWS], xm[par][0:MROWS, :].rearrange("r (cp j q) -> r j cp q", j=GRID, q=PATCH), st[0:MROWS, 15:16], st[0:MROWS, 17:18],
                                  ALU.mult, ALU.add).then_inc(S["xmn_done"], 1)

            def scale_fill(g, par, k):
                dve.wait_ge(S["tr_full"], 8 * g + k + 1)
                if k == 0:
                    need(dve, S["y_full"], 4 * g - 4)

                def put(s, j0, j1, src):
                    dst = gx[par][:, s, :, 1:TOK].rearrange("p b (i j) -> p b i j", i=GRID)[:, :, :, j0:j1]
                    gm = gam_t[:, s, :, j0:j1].unsqueeze(1).to_broadcast([128, GROUP, GRID, j1 - j0])
                    return dve.tensor_tensor(dst, src, gm, ALU.mult)

                if k < 4:
                    j0, j1 = MAIN_FILLS[k]
                    v = ps[k][:, 0:MROWS * (j1 - j0)].rearrange("p (j b i) -> p b i j", b=GROUP, i=GRID)
                    put(0, j0, j1, v).then_inc(S["tr_free"], 1)
                    return
                n0, n1 = HALF_FILLS[k - 4]
                v = ps[k - 4][:, 0:HROWS * (n1 - n0)].rearrange("p (j b m) -> p b m j", b=GROUP, m=HGRID)
                for s in range(1, NSHIFT):
                    m0 = 1 if s <= 2 else 0
                    right = (s - 1) % 2
                    j0, j1 = max(n0 - right, 0), min(n1 - right, GRID)
                    ins = put(s, j0, j1, v[:, :, m0:m0 + GRID, j0 + right - n0:j1 + right - n0])
                    ins.then_inc(S["tr_free"] if s == NSHIFT - 1 else S["dch"], 1)
                    ch.n += s < NSHIFT - 1

            def y_out(g, k):
                dve.wait_ge(S["y_full"], 4 * g + k + 1)
                src = ps[4 + k % 2][0:CHUNK, :].rearrange("p (i t n) -> p i t n", i=2, t=2)
                dst = h[0:CHUNK, bass.ds(4 * g + k, 1), :, :].rearrange("p o (i t) n -> p (o i) t n", i=2)
                b4 = bt[:, :, :].unsqueeze(1).to_broadcast([CHUNK, 2, 2, E_DIM])
                dve.tensor_tensor(dst, src, b4, ALU.add).then_inc(S["y_free"], 1)

            def group(g, par, base, u, tr=True, y=True, stat=True):
                ch.start(base)
                for k in range(8):
                    if k == 2 and stat:
                        stats_sums(g + 1, 1 - par, u)
                    if tr:
                        scale_fill(g, par, k)
                    if k % 2 and y:
                        y_out(g - 1, k // 2)
                    if k == 4 and stat:
                        stats_small(g + 1)
                if stat:
                    normalise(g + 1, 1 - par)
                return ch.n

            ch.start(dbase)
            stats_sums(0, 0, 0)
            stats_small(0)
            normalise(0, 0)
            dbase += ch.n
            per = group(0, 0, dbase, 0, y=False)
            dbase += per
            for g in (1, 2):
                assert group(g, g % 2, dbase + (g - 1) * per, g // 2 + g % 2) == per
            with dve.Fori(1, NGROUP // 2 - 1) as k:
                assert group(2 * k + 1, 1, dbase + k * (2 * per), k + 1) == per
                assert group(2 * k + 2, 0, dbase + per + k * (2 * per), k + 1) == per
            dbase += per * (NGROUP - 2)
            dbase += group(NGROUP - 1, 1, dbase, 0, stat=False)
            dbase += group(NGROUP, 0, dbase, 0, tr=False, stat=False)

            R = slice(0, CHUNK)

            def ln_stats(p, b, m, done):
                for c in range(4):
                    ch.step(dve.bn_stats(b[R, c], h[R, bass.ds(p, 1), c, :].rearrange("p o n -> p (o n)")))
                ch.settle()
                for c in range(4):
                    ins = dve.bn_aggr(m[R, c], b[R, c])
                    if c < 3:
                        ch.step(ins)
                ins.then_inc(done, 1)
                dve.wait_ge(done, p + 1)

            def ln_apply(p, dst, m, rstd, done):
                for c in range(4):
                    dve.tensor_scalar(dst(c), h[R, bass.ds(p, 1), c, :].rearrange("p o n -> p (o n)"),
                                      m[R, c, 0:1], rstd[R, c:c + 1], ALU.subtract, ALU.mult).then_inc(done, 1)

            def normalise1(p):
                dve.wait_ge(S["ln1_rstd"], p + 1)
                need(dve, S["xnt_ps"], p)
                ln_apply(p, lambda c: xn[R, c, :], mv, rstd1, S["xn_ready"])

            def scan(p):
                dve.wait_ge(S["l_ready"], p + 1)
                need(dve, S["e_ready"], 2 * p)
                dve.tensor_tensor_scan(cum, con("reset"), l_gk, 0.0, ALU.mult, ALU.add).then_inc(S["scan_done"], 1)

            def decayed(p):
                dve.wait_ge(S["e_ready"], 2 * p + 2)
                dve.wait_ge(S["qk_ps"], p + 1)
                need(dve, S["o_ps"], p)
                dve.tensor_tensor(qd, ps[5][:, 0:PT], decay, ALU.mult).then_inc(S["qk_ready"], 1)
                dve.tensor_tensor(kd, ps[6][:, 0:PT], grow, ALU.mult).then_inc(S["qk_ready"], 1)

            def masked(p):
                for hd in range(NH):
                    dve.wait_ge(S["sc_ps"], 4 * p + hd + 1)
                    src = ps[4 + hd][R, 0:PT].rearrange("p (c t) -> p c t", c=4)
                    mask = con("causal", CHUNK).unsqueeze(1).to_broadcast([CHUNK, 4, CHUNK])
                    dve.tensor_tensor(att[R, hd], src, mask, ALU.mult).then_inc(S["att_ready"], 1)

            def state_out(p):
                dve.wait_ge(S["st_ps"], p + 1)
                for i in range(2):
                    end = CHUNK * (2 * i + 1) - 1
                    dve.scalar_tensor_tensor(state[:, i, :], ps[1][:, 256 + 128 * i:384 + 128 * i],
                                             decay[:, end:end + 1], con("heads"), ALU.mult, ALU.mult)\
                       .then_inc(S["state_ready"], 1)

            def gated(p):
                dve.wait_ge(S["sq_ready"], p + 1)
                dve.wait_ge(S["g_ready"], p + 1)
                need(dve, S["ao_ps"], p)
                ch.link(dve.tensor_tensor(o_g, ps[2][:, 0:PT], gate, ALU.mult))
                dve.wait_ge(S["lms_ready"], p + 1)
                dve.scalar_tensor_tensor(u_exp, l_ms, -0.5, l_g, ALU.mult, ALU.subtract).then_inc(S["u_ready"], 1)
                dve.wait_ge(S["fac_ready"], p + 1)
                dve.tensor_tensor(o_f, o_g, fac, ALU.mult).then_inc(S["o_ready"], 1)

            def residual(p):
                dve.wait_ge(S["ao_ps"], p + 1)
                hp = h[R, bass.ds(p, 1), :, :].rearrange("p o c n -> p (o c n)")
                dve.tensor_tensor(hp, hp, ps[3][R, :], ALU.add).then_inc(S["h1_ready"], 1)
                dve.wait_ge(S["h1_ready"], p + 1)

            def normalise2(p):
                dve.wait_ge(S["ln2_rstd"], p + 1)
                need(dve, S["scattered"], 128 * p)
                ln_apply(p, lambda c: row[R, 0, c, 0:128], mv2, rstd2, S["xn2_ready"])

            def choose(p):
                dve.wait_ge(S["lg_ps"], p + 1)
                ch.link(dve.tensor_copy(lg[R], ps[0][R, 352:384].rearrange("p (c e) -> p c e", c=4)))
                apart(dve)
                for c in range(4):
                    ch.step(dve.max(mx[R, c], lg[R, c]))
                ch.settle()
                for c in range(4):
                    ch.step(dve.max_index(mi[R, c], mx[R, c], lg[R, c]))
                ch.settle()
                dve.tensor_tensor(dif[R, :], mx[R, :, 1], mx[R, :, 0], ALU.subtract).then_inc(S["dif_ready"], 1)
                ch.link(dve.tensor_copy(ef[R], mi[R, :, 0:2]))
                x0, x1 = cols["expert"]
                ex = cst[R, x0:x1].unsqueeze(1).to_broadcast([CHUNK, 8, NEXP])
                ef3 = ef[R].rearrange("p c k -> p (c k)").unsqueeze(2).to_broadcast([CHUNK, 8, NEXP])
                ch.link(dve.tensor_tensor(oh[R].rearrange("p c k e -> p (c k) e"), ex, ef3, ALU.is_equal))
                dve.tensor_tensor(om[R], oh[R, :, 0], oh[R, :, 1], ALU.add).then_inc(S["om_ready"], 1)

            def place(p):
                dve.wait_ge(S["rk_ps"], p + 1)
                ch.link(dve.tensor_copy(rk[R], ps[0][R, 384:448].rearrange("p (a c e) -> p a c e", a=2, c=4)))
                for c in range(4):
                    dve.tensor_tensor(pos[R, c], rk[R, 0, c], base[R, :], ALU.add).then_inc(S["dch"], 1)
                    ch.n += 1
                    ch.link(dve.tensor_tensor(base[R, :], base[R, :], rk[R, 1, c], ALU.add))
                p4 = pos[R].unsqueeze(2).to_broadcast([CHUNK, 4, 2, NEXP])
                ch.link(dve.tensor_tensor(pp[R], oh[R], p4, ALU.mult))
                ch.link(dve.tensor_reduce(slot_f[R], pp[R], AX_X, ALU.add))
                dve.tensor_copy(slot_i[R], slot_f[R]).then_inc(S["slots_ready"], 1)
                dve.wait_ge(S["edif_ready"], p + 1)
                ch.link(dve.tensor_scalar(den[R, :], edif[R, :], 1.0, None, ALU.add))
                ch.link(dve.reciprocal(row[R, 0, :, 128], den[R, :]))
                ch.link(dve.tensor_tensor(row[R, 1, :, 128], row[R, 0, :, 128], edif[R, :], ALU.mult))
                ch.link(dve.tensor_copy(row[R, 0, :, 129], ids[R, :]))
                ch.link(dve.tensor_scalar(row[R, 1, :, 129], ids[R, :], 1.0, None, ALU.add))
                dve.tensor_scalar(ids[R, :], ids[R, :], float(2 * PT), None, ALU.add).then_inc(S["rows_ready"], 1)

            def pair(p, base_, route=True, attend=True, first=False, last=False):
                ch.start(base_)
                if first:
                    ln_stats(p, bns, mv, S["ln1_stats"])
                if attend:
                    normalise1(p)
                if route:
                    ln_stats(p - 1, bns2, mv2, S["ln2_stats"])
                if attend:
                    scan(p)
                if route:
                    normalise2(p - 1)
                if attend:
                    decayed(p)
                    masked(p)
                if route:
                    choose(p - 1)
                if attend:
                    state_out(p)
                if route:
                    place(p - 1)
                if attend:
                    gated(p)
                    residual(p)
                    if not last:
                        ln_stats(p + 1, bns, mv, S["ln1_stats"])
                return ch.n

            ch.start(dbase)
            ch.link(dve.tensor_copy(base[R, :], con("region", CHUNK)))
            dve.tensor_copy(ids[R, :], con("tokid", CHUNK)).then_inc(S["base_ready"], 1)
            dve.wait_ge(S["base_ready"], 1)
            dbase += 1
            dbase += pair(0, dbase, route=False, first=True)
            assert pair(1, dbase) == DVE_PAIR, ch.n
            with dve.Fori(2, PAIRS - 1) as p:
                assert pair(p, dbase + (p - 1) * DVE_PAIR) == DVE_PAIR, ch.n
            dbase += DVE_PAIR * (PAIRS - 2)
            dbase += pair(PAIRS - 1, dbase, last=True)
            dbase += pair(PAIRS, dbase, attend=False)

            ch.start(dbase)
            dve.tensor_tensor(cnt[R, :], base[R, :], con("region", CHUNK), ALU.subtract).then_inc(S["cnt_ready"], 1)
            dve.wait_ge(S["cnt_ps"], 1)
            ch.link(dve.tensor_copy(cnt_all, ps[0][:, 0:NEXP]))
            ch.link(dve.tensor_tensor(pad_f, cnt_all, con("region"), ALU.add))
            sid = con("slotid")
            for k in range(2):
                ins = dve.tensor_scalar(pad_i[:, k, :], pad_f, sid[:, k:k + 1], None, ALU.add)
                if k == 0:
                    ch.link(ins)
            ins.then_inc(S["cnt_ready"], 1)
            c1 = cnt_all[0:1, :].unsqueeze(2).to_broadcast([1, NEXP, 43])
            k1 = con("tiles_k", 1).unsqueeze(1).to_broadcast([1, NEXP, 43])
            ch.link(dve.tensor_tensor(more[0:1], c1, k1, ALU.is_gt))
            ch.link(dve.tensor_reduce(ntiles[0:1, :], more[0:1], AX_X, ALU.add))
            ch.link(dve.tensor_tensor_scan(tile_end[0:1, :], con("one_row", 1)[:, 0:NEXP], ntiles[0:1, :], 0.0, ALU.mult, ALU.add))
            ch.link(dve.tensor_scalar(skip[0:1, :], ntiles[0:1, :], -float(SLOT), float(REGION), ALU.mult, ALU.add))
            ch.link(dve.tensor_scalar(tab_f[:, 0, :], con("tile_no", 1), float(SLOT), None, ALU.mult))
            ch.link(dve.memset(tab_f[:, 1, :], 0.0))
            for e in range(NEXP):
                past = more[0:1].rearrange("p a b -> p (a b)")[:, 0:NTILE]
                ch.link(dve.tensor_scalar(past, con("tile_no", 1), tile_end[0:1, e:e + 1], None, ALU.is_ge))
                ch.link(dve.tensor_tensor(tab_f[:, 1, :], tab_f[:, 1, :], past, ALU.add))
                ch.link(dve.scalar_tensor_tensor(tab_f[:, 0, :], past, skip[0:1, e:e + 1], tab_f[:, 0, :], ALU.mult, ALU.add))
            ch.link(dve.tensor_scalar(tab_f[:, 0, :], tab_f[:, 0, :], float(NEXP * REGION), None, ALU.min))
            ch.link(dve.tensor_scalar(tab_f[:, 1, :], tab_f[:, 1, :], float(NEXP - 1), None, ALU.min))
            dve.tensor_copy(tile_tab[:, :, :], tab_f[:, :, :]).then_inc(S["tab_ready"], 1)
            dbase += ch.n
            dve.wait_ge(S["tab_ready"], 1)
            dve.wait_ge(S["pad_gone"], 16 * 2 * NEXP)
            dve.wait_ge(S["fw_loaded"], 16 * (NEXP + 3))

            def tile_step(i, n, u):
                m = n % 2
                if isinstance(i, int):
                    ch.start(dtile)
                if live(i - 2):
                    g = x_sl[(n + 2) % 4][:, :, E_DIM]
                    dve.wait_ge(S["rstd3_ready"], i - 1)
                    need(dve, y_gone[m], 32 * (2 * u + n // 2 - 1))
                    e = dve.value_load(tile_tab[0:1, 1, bass.ds(i - 2, 1)], min_val=0, max_val=NEXP - 1)
                    ch.link(dve.tensor_tensor(rg3, rstd3, g, ALU.mult))
                    dve.tensor_copy(y_id[m], x_sl[(n + 2) % 4][:, :, E_DIM + 1]).then_inc(S["dch"], 1)
                    ch.n += 1
                    for k in range(2):
                        ins = dve.tensor_scalar(nrm[:, k, :], res[:, k, :], mv3[:, k, 0:1], rg3[:, k:k + 1],
                                                ALU.subtract, ALU.mult)
                        ch.link(ins)
                    gm = gam_all[:, bass.ds(e, 1), :].to_broadcast([128, 2, E_DIM])
                    ch.link(dve.tensor_tensor(scl, nrm, gm, ALU.mult))
                    be = bet_all[:, bass.ds(e, 1), :].rearrange("p o n -> p (o n)")
                    for k in range(2):
                        ins = dve.scalar_tensor_tensor(y_sl[m][:, k, :], be, g[:, k:k + 1], scl[:, k, :], ALU.mult, ALU.add)
                        if k == 0:
                            ch.link(ins)
                    ins.then_inc(S["y_ready"], 1)
                if live(i + 1):
                    dve.wait_ge(S["xhi_ready"], i + 2)
                    need(dve, S["h_ps"], 4 * i)
                    dve.tensor_tensor(x_lo[1 - m], ps[1 - m][:, 0:SLOT], x_hi[1 - m], ALU.subtract).then_inc(S["xlo_ready"], 1)
                if live(i - 1):
                    dve.wait_ge(S["w2_ps"], i)
                    dve.wait_ge(S["xb_ready"], i)
                    need(dve, S["y_ready"], i - 1)
                    ins = dve.tensor_tensor(res, ps[7 - m][:, 0:SLOT].rearrange("p (k n) -> p k n", k=2), x_b2[1 - m], ALU.add)
                    ins.then_inc(S["t_ready"], 1)
                    dve.wait_ge(S["t_ready"], i)
                    for k in range(2):
                        ch.step(dve.bn_stats(bns3[:, k], res[:, k, :]))
                    ch.settle()
                    for k in range(2):
                        ins = dve.bn_aggr(mv3[:, k], bns3[:, k])
                        if k == 0:
                            ch.step(ins)
                    ins.then_inc(S["rstd3_stats"], 1)

            dtile = dbase
            for i in range(-1, STEADY.start):
                tile_step(i, i % 4, i // 4)
                dtile += ch.n
            with dve.Fori(0, len(STEADY) // 4) as k:
                for j in range(4):
                    i = STEADY.start + j
                    ch.start(dtile + (4 * k + j) * DVE_TILE)
                    tile_step(4 * k + i, i % 4, k + i // 4)
                    assert ch.n == DVE_TILE, ch.n
            dtile += DVE_TILE * len(STEADY)
            for i in range(STEADY.stop, NTILE + 2):
                tile_step(i, i % 4, i // 4)
                dtile += ch.n

            def combine(p, n, u):
                dve.wait_ge(y_loaded[n], 16 * u + 16)
                hp = h[R, bass.ds(p, 1), :, :].rearrange("p o c n -> p (o c) n")
                for k in range(2):
                    dve.tensor_tensor(hp, hp, y_tok[n][R, :, k, :], ALU.add).then_inc(S["sum_ready"], 1)
                    dve.wait_ge(S["sum_ready"], 2 * p + k + 1)

            with dve.Fori(0, PAIRS // 4) as k:
                for n in range(4):
                    combine(4 * k + n, n, k)

        @block.scalar
        def _(act):
            act.preload_act_table_set("natural_log_exp_and_others")
            act.wait_ge(S["c_loaded"], 16)
            act.wait_ge(S["z_prep"], 1)
            act.wait_ge(S["prep_done"], 1)

            def stats_squares(g, par, u, base):
                act.wait_ge(x_loaded[par], 16 * GROUP_DMAS * (u + 1))
                need(act, S["stat_ps"], g)
                act.activation(sqj[0:HROWS, :], xh[par][0:HROWS, :], ACT.Square,
                               accum_out=st[0:HROWS, 1:2]).then_inc(S["ach"], 1)
                act.wait_ge(S["ach"], base + 1)
                act.wait_ge(S["edge_done"], g + 1)
                act.activation(sqj[0:HROWS, 0:256], xe[0:HROWS].rearrange("r a b c -> r (a b c)"), ACT.Square,
                               accum_out=st[0:HROWS, 3:4]).then_inc(S["asum_done"], 1)

            def rstd(g, base):
                act.wait_ge(S["var_done"], g + 1)
                act.activation(st[0:HROWS, 12:14], st[0:HROWS, 10:12], ACT.Ln, bias=eps[0:HROWS, 0:1]).then_inc(S["ach"], 1)
                act.wait_ge(S["ach"], base + 2)
                act.activation(st[0:HROWS, 14:16], st[0:HROWS, 12:14], ACT.Exp, scale=-0.5).then_inc(S["rstd0_done"], 1)

            def normalise(g, par):
                act.wait_ge(S["nb_done"], g + 1)
                need(act, S["tr_full"], 8 * g)
                mid = xh[par][0:HROWS, :].rearrange("r (cp w) -> r cp w", w=SIDE)[:, :, HALF:SIDE - HALF]
                act.activation(xhn[0:HROWS, 1:GRID], mid.rearrange("r cp (n q) -> r n cp q", q=PATCH), ACT.Identity, bias=st[0:HROWS, 16:17],
                               scale=st[0:HROWS, 14:15]).then_inc(S["xhn_done"], 1)

            def group(g, par, u):
                stats_squares(g, par, u, 2 * g)
                rstd(g, 2 * g)
                normalise(g, par)

            group(0, 0, 0)
            group(1, 1, 0)
            with act.Fori(1, NGROUP // 2) as k:
                group(2 * k, 0, k)
                group(2 * k + 1, 1, k)

            R = slice(0, CHUNK)
            ach = Chain(act, S["ach"])

            def rstd_of(p, m, tmp, dst, stats, done):
                act.wait_ge(stats, p + 1)
                ach.link(act.activation(tmp[R, :], m[R, :, 1], ACT.Ln, bias=eps[R, 1:2]))
                act.activation(dst[R, :], tmp[R, :], ACT.Exp, scale=-0.5).then_inc(done, 1)

            def projections(p):
                act.wait_ge(S["xnt_ps"], p + 1)
                act.activation(xn_t, ps[0][:, 0:PT], ACT.Copy).then_inc(S["xnt_sb"], 1)
                act.wait_ge(S["gk_ps"], p + 1)
                need(act, S["scan_done"], p)
                ach.link(act.activation(e_gk, ps[4][:, 0:PT], ACT.Exp, bias=nbgk[:, 0:1], scale=-1.0))
                act.activation(l_gk, e_gk, ACT.Ln, bias=eps[:, 4:5]).then_inc(S["l_ready"], 1)
                act.wait_ge(S["g_ps"], p + 1)
                need(act, S["o_ready"], p)
                act.activation(gate, ps[7][:, 0:PT], ACT.Copy).then_inc(S["g_copied"], 1)
                act.wait_ge(S["scan_done"], p + 1)
                need(act, S["state_ready"], 2 * p)
                act.activation(decay, cum, ACT.Exp, scale=eps[:, 5:6]).then_inc(S["e_ready"], 1)
                act.activation(grow, cum, ACT.Exp, scale=eps[:, 6:7]).then_inc(S["e_ready"], 1)
                act.wait_ge(S["g_copied"], p + 1)
                ach.link(act.activation(e_g, gate, ACT.Exp, scale=-1.0))
                act.activation(l_g, e_g, ACT.Ln, bias=eps[:, 4:5]).then_inc(S["g_ready"], 1)

            def values(p):
                act.wait_ge(S["v_ps"], p + 1)
                need(act, S["o_ps"], p)
                act.activation(val[R], ps[1][R, :].rearrange("p (c n) -> p c n", c=4), ACT.Copy).then_inc(S["v_ready"], 1)

            def keys(p):
                act.wait_ge(S["kt_ps"], p + 1)
                act.activation(k_tok[R], ps[1][R, 0:256].rearrange("p (i n) -> p i n", i=2), ACT.Copy)\
                   .then_inc(S["kt_ready"], 1)

            def head_norm(p):
                act.wait_ge(S["o_ps"], p + 1)
                act.activation(o_sq, ps[2][:, 0:PT], ACT.Square).then_inc(S["sq_ready"], 1)
                act.wait_ge(S["ms_ps"], p + 1)
                act.activation(l_ms, ps[3][:, 0:PT], ACT.Ln, bias=eps[:, 2:3]).then_inc(S["lms_ready"], 1)
                act.wait_ge(S["u_ready"], p + 1)
                act.activation(fac, u_exp, ACT.Exp).then_inc(S["fac_ready"], 1)

            def route_copy(p):
                act.wait_ge(S["xn2t_ps"], p + 1)
                act.activation(xn2_t, ps[0][:, 0:PT], ACT.Copy).then_inc(S["xn2t_sb"], 1)

            def row_copy(p):
                act.activation(row[R, 1, :, 0:128], row[R, 0, :, 0:128], ACT.Copy).then_inc(S["row_copied"], 1)

            def gate_exp(p):
                act.wait_ge(S["dif_ready"], p + 1)
                act.activation(edif[R, :], dif[R, :], ACT.Exp).then_inc(S["edif_ready"], 1)

            def pair(p, base_, route=True, attend=True):
                ach.start(base_)
                if attend:
                    rstd_of(p, mv, rs1, rstd1, S["ln1_stats"], S["ln1_rstd"])
                if route:
                    rstd_of(p - 1, mv2, rs2, rstd2, S["ln2_stats"], S["ln2_rstd"])
                if attend:
                    projections(p)
                if route:
                    route_copy(p - 1)
                if attend:
                    values(p)
                if route:
                    row_copy(p - 1)
                if attend:
                    keys(p)
                if route:
                    gate_exp(p - 1)
                if attend:
                    head_norm(p)
                return ach.n

            abase = 2 * NGROUP
            abase += pair(0, abase, route=False)
            assert pair(1, abase) == ACT_PAIR
            with act.Fori(2, PAIRS) as p:
                assert pair(p, abase + (p - 1) * ACT_PAIR) == ACT_PAIR, ach.n
            abase += ACT_PAIR * (PAIRS - 1)
            abase += pair(PAIRS, abase, attend=False)

            act.wait_ge(S["tab_ready"], 1)
            act.wait_ge(S["w1_split"], 4)

            def tile_step(i, n, u):
                m = n % 2
                if isinstance(i, int):
                    ach.start(abase)
                if live(i - 2):
                    act.wait_ge(S["rstd3_stats"], i - 1)
                    need(act, S["y_ready"], i - 2)
                    ach.link(act.activation(ln3, mv3[:, :, 1], ACT.Ln, bias=eps[:, 3:4]))
                    act.activation(rstd3, ln3, ACT.Exp, scale=-0.5).then_inc(S["rstd3_ready"], 1)
                if live(i):
                    e = act.value_load(tile_tab[0:1, 1, bass.ds(i, 1)], min_val=0, max_val=NEXP - 1)
                    need(act, S["w2_ps"], i - 1)
                    for c in range(FC):
                        act.wait_ge(S["h_ps"], 4 * i + c + 2 - c % 2)
                        act.activation(hid[m][:, c, :], ps[2 + 2 * m + c // 2][:, SLOT * (c % 2):SLOT * (c % 2) + SLOT],
                                       ACT.Relu, bias=b1_t[:, bass.ds(e * FC + c, 1)], scale=1.0 / W_SCALE)\
                           .then_inc(S["h_ready"], 1)
                if live(i + 1):
                    act.wait_ge(S["xt_ps"], i + 2)
                    need(act, S["h_ps"], 4 * i)
                    act.activation(x_hi[1 - m], ps[1 - m][:, 0:SLOT], ACT.Copy).then_inc(S["xhi_ready"], 1)

            for i in range(-1, STEADY.start):
                tile_step(i, i % 4, i // 4)
                abase += ach.n
            with act.Fori(0, len(STEADY) // 4) as k:
                for j in range(4):
                    i = STEADY.start + j
                    ach.start(abase + 4 * k + j)
                    tile_step(4 * k + i, i % 4, k + i // 4)
                    assert ach.n == 1
            abase += len(STEADY)
            for i in range(STEADY.stop, NTILE + 2):
                tile_step(i, i % 4, i // 4)
                abase += ach.n

            def store(p):
                act.wait_ge(S["sum_ready"], 2 * p + 2)
                act.dma_start(out_rows[bass.ds(p * PT, PT), :].rearrange("(c r) n -> r c n", c=4),
                              h[R, bass.ds(p, 1), :, :].rearrange("p o c n -> p (o c) n")).then_inc(S["h_out"], 16)

            with act.Fori(0, PAIRS) as p:
                store(p)
            act.wait_ge(S["h_out"], 16 * PAIRS)


DVE_PAIR = 42
DVE_TILE = 9
ACT_PAIR = 4
N_WLOADS = 1 + 10 + 2 + 20 + 6


_INPUTS = [
    "x", "cls_tok", "L0_tok_gamma", "L0_tok_beta", "L0_tok_W", "L0_tok_b", "L0_attn_Wq", "L0_attn_Wk", "L0_attn_Wv",
    "L0_attn_Wgk1", "L0_attn_Wgk2", "L0_attn_bgk2", "L0_attn_gnorm_w", "L0_attn_Wg", "L0_attn_Wo", "L0_ffn_router_w",
    "L0_ffn_w1", "L0_ffn_b1", "L0_ffn_w2", "L0_ffn_b2", "L0_ffn_gamma", "L0_ffn_beta",
]


def kernel(**inputs):
    import concourse.bacc as bacc
    from concourse.bass_utils import run_bass_kernel_spmd

    nc = bacc.Bacc("TRN2", target_bir_lowering=False, num_devices=1)
    arrays, aps = {}, {}
    for name in _INPUTS + ["consts"]:
        arr = const_array() if name == "consts" else np.ascontiguousarray(inputs[name])
        arrays[name + "_in"] = arr
        aps[name] = nc.dram_tensor(name + "_in", arr.shape, DT.from_np(arr.dtype), kind="ExternalInput").ap()
    out = nc.dram_tensor("out", (NTOK, E_DIM), F32, kind="ExternalOutput").ap()
    build(nc, aps, out)
    r = run_bass_kernel_spmd(nc, [arrays], core_ids=[0])
    return r.results[0]["out"].reshape(BATCH, TOK, E_DIM)
```

```python
from contextlib import ExitStack

import numpy as np

import concourse.bass as bass
from concourse import mybir

DT = mybir.dt
ALU = mybir.AluOpType
ACT = mybir.ActivationFunctionType
AX_X = mybir.AxisListType.X
F32, F16, BF16, I32, U32 = DT.float32, DT.float16, DT.bfloat16, DT.int32, DT.uint32

BATCH, CH, SIDE, PATCH, HALF = 64, 2, 104, 8, 4
GRID = SIDE // PATCH
HGRID = GRID + 1
ROWLEN = PATCH * SIDE
NSHIFT = 5
E_DIM = 128
TOK = GRID * GRID + 1
CHUNK = TOK // 2
NTOK = BATCH * TOK
GROUP = 8
NGROUP = BATCH // GROUP
MROWS, HROWS = GROUP * GRID, GROUP * HGRID
PAIRS = BATCH // 2
PT = 2 * TOK
NH, HK, HV = 4, 16, 32
NEXP, FF = 8, 512
FC = FF // 128
XBUF = 6
SLOT = 256
REGION = NTOK + SLOT
NTILE = (2 * NTOK + NEXP * (SLOT - 1)) // SLOT
NTILE += NTILE % 2
XW = 130
PAD_ID = 2 * NTOK
LAST_TILE_LAG = 5
NBLOCK = -(-(NTILE + LAST_TILE_LAG) // XBUF)
W_SCALE = 256.0
N_CONCAT = float(CH * NSHIFT * SIDE * SIDE)
EPS_TOK, EPS_LN, EPS_GN, EPS_FFN = 1e-7, 1e-5, 1e-5, 1e-6


def const_layout():
    cols, at = {}, 0
    for name, n in (
        ("ident", 128), ("stat_all", 2 * HROWS), ("stat_edge", 2 * HROWS), ("causal", CHUNK),
        ("heads", 128), ("meanv", 128), ("before", CHUNK), ("ones", CHUNK), ("reset", PT),
        ("cls_sel", TOK), ("expert", 8), ("region", 8), ("eps", 8), ("tokid", 4), ("slotid", 2),
        ("tiles_k", 43), ("tile_no", XBUF * NBLOCK), ("one_row", 128),
    ):
        cols[name] = (at, at + n)
        at += n
    return cols, at


def const_array():
    cols, width = const_layout()
    c = np.zeros((128, width), np.float32)

    def put(name):
        a, b = cols[name]
        return c[:, a:b]

    put("ident")[:] = np.eye(128)
    wt = np.array([1 if m in (0, HGRID - 1) else 2 for m in range(HGRID)] * GROUP, np.float32)
    img_h = np.repeat(np.arange(GROUP), HGRID)
    img_m = np.concatenate([np.repeat(np.arange(GROUP), GRID), np.full(HROWS - MROWS, -1)])
    for k, img in enumerate((img_h, img_m)):
        same = (img_h[:, None] == img[None, :]).astype(np.float32)
        put("stat_all")[:HROWS, k * HROWS:(k + 1) * HROWS] = same * (1 + 2 * wt[:, None])
        put("stat_edge")[:HROWS, k * HROWS:(k + 1) * HROWS] = -same * wt[:, None]
    s = np.arange(CHUNK)
    put("causal")[:CHUNK] = s[:, None] <= s[None, :]
    put("before")[:CHUNK] = s[:, None] < s[None, :]
    put("ones")[:CHUNK] = 1
    h = np.arange(128) // HV
    put("heads")[:] = h[:, None] == h[None, :]
    put("meanv")[:] = (h[:, None] == h[None, :]) / HV
    put("reset")[:] = (np.arange(PT) % CHUNK != 0)[None, :]
    put("cls_sel")[0, 1:] = 1
    put("cls_sel")[1, 0] = 1
    put("expert")[:] = np.arange(8)
    put("region")[:] = np.arange(8) * REGION
    put("eps")[:, 0:5] = [EPS_TOK, EPS_LN, EPS_GN, EPS_FFN, 1.0]
    put("eps")[:, 5] = -1 / 16
    put("eps")[:, 6] = 1 / 16
    put("tokid")[:CHUNK] = 2 * (s[:, None] + CHUNK * np.arange(4)[None, :])
    put("slotid")[:] = np.arange(128)[:, None] + 128 * np.arange(2)[None, :]
    put("tiles_k")[:] = SLOT * np.arange(43)
    put("one_row")[:] = 1
    put("tile_no")[:] = np.arange(XBUF * NBLOCK)
    return c


def need(eng, sem, value):
    if not isinstance(value, int) or value > 0:
        eng.wait_ge(sem, value)


ARENA_WORDS = 30800
PHASE1_WORDS = 13184


SPARE = []


def apart(eng):
    eng.sem_inc(SPARE[0], 1)


class Chain:

    def __init__(self, eng, sem):
        self.eng, self.sem, self.base, self.n = eng, sem, 0, 0

    def start(self, base):
        self.base, self.n = base, 0

    def link(self, ins):
        self.n += 1
        ins.then_inc(self.sem, 1)
        self.eng.wait_ge(self.sem, self.base + self.n)

    def step(self, ins):
        self.n += 1
        ins.then_inc(self.sem, 1)

    def settle(self):
        self.eng.wait_ge(self.sem, self.base + self.n)
        apart(self.eng)


MAIN_FILLS = [(0, 4), (4, 7), (7, 10), (10, 13)]
HALF_FILLS = [(0, 4), (4, 8), (8, 11), (11, 14)]
GROUP_DMAS = 2 * GROUP + 2


def build(nc, a, out_rows):
    cols, cwidth = const_layout()
    xs_dram = nc.dram_tensor("x_slots", (NEXP * REGION + SLOT, XW), F32, kind="Internal").ap()
    y_dram = nc.dram_tensor("y_tokens", (2 * NTOK, E_DIM), F32, kind="Internal").ap()

    with ExitStack() as ctx:
        def sb(name, shape, dt=F32):
            return ctx.enter_context(nc.sbuf_tensor(name, shape, dt))

        def sem(name):
            return ctx.enter_context(nc.semaphore(name))

        cst = sb("cst", [128, cwidth])

        def con(name, p=128):
            x, y = cols[name]
            return cst[0:p, x:y]

        ident = con("ident")
        eps = con("eps")
        h = sb("h", [128, PAIRS, 4, E_DIM])
        wt = sb("wt", [128, NSHIFT, E_DIM])
        bt = sb("bt", [CHUNK, 2, E_DIM])
        wproj = sb("wproj", [128, 6, E_DIM])
        nbgk = sb("nbgk", [128, 1])
        gnorm = sb("gnorm", [128, 1])
        rw = sb("rw", [128, NEXP])
        arena = sb("arena", [128, ARENA_WORDS])

        class Arena:
            def __init__(self):
                self.at = 0

            def take(self, *shape, dt=F32):
                n = int(np.prod(shape))
                words = n if dt in (F32, I32, U32) else (n + 1) // 2
                v = arena[:, self.at:self.at + words]
                self.at += words
                assert self.at <= ARENA_WORDS, self.at
                if dt is not F32:
                    v = v.bitcast(dt)
                if len(shape) > 1:
                    names = " ".join(f"d{i}" for i in range(len(shape)))
                    v = v.rearrange(f"p ({names}) -> p {names}", **{f"d{i}": s for i, s in enumerate(shape)})
                return v

        A0 = Arena()
        gx = [A0.take(NSHIFT, GROUP, TOK) for _ in range(2)]
        xm = [A0.take(CH * ROWLEN) for _ in range(2)]
        xh = [A0.take(CH * ROWLEN) for _ in range(2)]
        xmn = A0.take(GRID, CH * PATCH, PATCH)
        xhn = A0.take(HGRID, CH * PATCH, PATCH)
        xe = A0.take(2, CH * PATCH, PATCH)
        sqj = A0.take(CH * ROWLEN, dt=BF16)
        gam_t = A0.take(NSHIFT, GRID, GRID)
        st = sb("st", [128, 24])
        AP_ = Arena()
        wn = AP_.take(NSHIFT, CH * PATCH * PATCH)
        wn2 = AP_.take(6, E_DIM)
        wgk1 = AP_.take(E_DIM)
        wgk2t = AP_.take(E_DIM)
        bc = AP_.take(E_DIM)
        bet_t = AP_.take(NSHIFT, TOK)
        gb = [AP_.take(CH * ROWLEN) for _ in range(2)]
        b1_n = AP_.take(128)
        gbp = [AP_.take(GRID, CH * PATCH, PATCH) for _ in range(2)]
        assert AP_.at <= 13600

        A1 = Arena()
        xn = A1.take(4, E_DIM)
        xn_t = A1.take(PT)
        e_gk, l_gk, cum, grow = (A1.take(PT) for _ in range(4))

        def two(*shape, **kw):
            return [A1.take(*shape, **kw) for _ in range(2)]

        decay = two(PT)
        qd, kd = two(PT), two(PT)
        gate, l_g = two(PT), two(PT)
        val = two(4, E_DIM)
        att = A1.take(NH, 4, CHUNK)
        k_tok = A1.take(2, 128)
        state = A1.take(2, 128)
        o_sq, fac, o_f = (A1.take(PT) for _ in range(3))
        bns, mv, rs1, rstd1, nb1 = A1.take(4, 6), A1.take(4, 2), A1.take(4), A1.take(4), A1.take(4)
        bns2, mv2, rs2, rstd2, nb2 = A1.take(4, 6), A1.take(4, 2), A1.take(4), A1.take(4), A1.take(4)
        row = two(2, 4, XW)
        xn2_t = A1.take(PT)
        lg, mx = A1.take(4, NEXP), A1.take(4, 8)
        mi = A1.take(4, 8, dt=U32)
        ef, oh, om = A1.take(4, 2), A1.take(4, 2, NEXP), A1.take(4, NEXP)
        rk, base, pos, pp = A1.take(2, 4, NEXP), A1.take(NEXP), A1.take(4, NEXP), A1.take(4, 2, NEXP)
        slot_f, dif, edif, den = A1.take(4, 2), A1.take(4), A1.take(4), A1.take(4)
        slot_i = two(4, 2, dt=I32)
        ids = A1.take(4)
        cnt = A1.take(NEXP)
        cnt_all, pad_f = A1.take(NEXP), A1.take(NEXP)
        pad_i = A1.take(2, NEXP, dt=I32)
        pad_row = A1.take(2, XW)
        more, ntiles, tile_end, skip = A1.take(NEXP, 43), A1.take(NEXP), A1.take(NEXP), A1.take(NEXP)
        assert A1.at <= PHASE1_WORDS, A1.at
        A2 = Arena()
        A2.at = PHASE1_WORDS
        b2_all, gam_all, bet_all = (A2.take(NEXP, E_DIM) for _ in range(3))
        w1_hi, w1_lo = A2.take(NEXP, FF, dt=F16), A2.take(NEXP, FF, dt=F16)
        w2_sb = A2.take(NEXP, FC, E_DIM)
        w1_raw = A2.take(NEXP, FF)
        at = A2.at
        A3 = Arena()
        A3.at = at - NEXP * FF
        x_sl = [A3.take(2, XW) for _ in range(XBUF)]
        x_hi, x_lo = [A3.take(SLOT, dt=F16) for _ in range(2)], [A3.take(SLOT, dt=F16) for _ in range(2)]
        hid = [A3.take(FC, SLOT)]
        assert A3.at <= at
        A3.at = at
        hid.append(A3.take(FC, SLOT))
        A3.at = 0
        x_b2 = [A3.take(2, E_DIM) for _ in range(2)]
        res = [A3.take(2, E_DIM) for _ in range(2)]
        nrm, scl = A3.take(2, E_DIM), A3.take(2, E_DIM)
        y_sl = [A3.take(2, E_DIM) for _ in range(2)]
        bns3, mv3, ln3, rstd3, rg3 = (A3.take(2, 6), A3.take(2, 2), A3.take(2), A3.take(2), A3.take(2))
        y_id = [A3.take(2, dt=I32) for _ in range(2)]
        y_tok = [A3.take(4, 2, E_DIM) for _ in range(4)]
        assert A3.at <= PHASE1_WORDS
        tile_tab = sb("tile_tab", [1, XBUF * NBLOCK], I32)
        expert_tab = sb("expert_tab", [1, NBLOCK, 2 * XBUF], I32)
        tab_f = sb("tab_f", [1, 2, XBUF * NBLOCK])
        b1_t = sb("b1_t", [128, NEXP * FC])

        ps = [ctx.enter_context(nc.psum_tensor(f"ps{i}", [128, 512], F32)) for i in range(8)]

        names = (
            "c_loaded z_prep w_loaded prep_done xl0 xl1 edge_done dsum_done asum_done stat_ps var_done "
            "h_out "
            "ln1_stats ln1_rstd xn_ready xnt_ps xnt_sb gk_ps q_ps k_ps g_ps v_ps l_ready scan_done e_ready g_copied g_ready "
            "v_ready qk_ready sc_ps att_ready kt_ps kt_ready st_ps state_ready o_ps sq_ready ms_ps lms_ready u_ready "
            "fac_ready o_ready ao_ps h1_ready ln2_stats ln2_rstd xn2_ready xn2t_ps xn2t_sb lg_ps om_ready dif_ready "
            "edif_ready rk_ps slots_ready rank_copied lg_ready row_copied sc0 sc1 base_ready q_copied k_copied og_ready nb1_ready nb2_ready aln pln w1_loaded fw_loaded w1_split cnt_ready cnt_ps pad_ready tab_ready pad_gone pad_stored xs0 xs1 xs2 xs3 xs4 xs5 norm_ready scl_ready gate_ready bns3_ready xt_ps xhi_ready xlo_ready h_ps h_ready w2_ps xb_ready t_ready rstd3_stats rstd3_ready y_ready yg0 yg1 meta_ready yl0 yl1 yl2 yl3 sum_ready pz "
            "rstd0_done nb_done xmn_done xhn_done tr_full tr_free y_full y_free dch ach pch t_prep d_prep xen_done"
        ).split()
        S = {n: sem(n) for n in names}
        x_loaded = [S["xl0"], S["xl1"]]
        SPARE[:] = [sem("passed")]
        block = ctx.enter_context(nc.Block())

        x_sl_loaded = [S[f"xs{n}"] for n in range(XBUF)]
        scattered = [S["sc0"], S["sc1"]]
        y_gone = [S["yg0"], S["yg1"]]
        y_loaded = [S[f"yl{n}"] for n in range(4)]
        STEADY_PAIRS = range(8, PAIRS)
        LAST_LAG = 4

        def pairs(eng, chain, base, steps, step):
            def iteration(p, half, par):
                def at(lag, work, *args):
                    q = p - lag
                    if not isinstance(q, int) or 0 <= q < PAIRS:
                        work(q, (par - lag) % 2, half + (par - lag) // 2, *args)
                step(at)

            for p in range(STEADY_PAIRS.start):
                chain.start(base)
                iteration(p, p // 2, p % 2)
                base += chain.n
            with eng.Fori(STEADY_PAIRS.start // 2, STEADY_PAIRS.stop // 2) as k:
                for par in range(2):
                    chain.start(base + (2 * k + (par - STEADY_PAIRS.start)) * steps)
                    iteration(2 * k + par, k, par)
                    assert chain.n == steps, chain.n
            base += steps * len(STEADY_PAIRS)
            for p in range(STEADY_PAIRS.stop, PAIRS + LAST_LAG):
                chain.start(base)
                iteration(p, p // 2, p % 2)
                base += chain.n
            return base

        STEADY_TILES = range(12, 12 + XBUF * ((NTILE - 12) // XBUF))

        def tiles(eng, chain, base, steps, step):
            experts, loads = [], []

            def iteration(i, u, n):
                if n == 0:
                    regs = [eng.alloc_register(name=f"expert_{len(loads)}_{r}") for r in range(2 * XBUF)]
                    loads.append(regs)
                    experts[:] = [bass.RuntimeValue.of_register_unchecked(r, min_val=0, max_val=NEXP - 1) for r in regs]
                    eng.load(regs, expert_tab[0:1, bass.ds(u, 1), :].rearrange("p o e -> p (o e)"))

                def at(lag, work, *args):
                    q = i - lag
                    if not isinstance(q, int) or 0 <= q < NTILE:
                        work(q, (n - lag) % XBUF, u + (n - lag) // XBUF, experts[XBUF + n - lag], *args)
                step(at)

            for i in range(STEADY_TILES.start):
                chain.start(base)
                iteration(i, i // XBUF, i % XBUF)
                base += chain.n
            u0 = STEADY_TILES.start // XBUF
            with eng.Fori(u0, STEADY_TILES.stop // XBUF) as u:
                for n in range(XBUF):
                    chain.start(base + (XBUF * u + (n - XBUF * u0)) * steps)
                    iteration(XBUF * u + n, u, n)
                    assert chain.n == steps, chain.n
            base += steps * len(STEADY_TILES)
            for i in range(STEADY_TILES.stop, NTILE + LAST_TILE_LAG):
                chain.start(base)
                iteration(i, i // XBUF, i % XBUF)
                base += chain.n
            return base

        def expert_sync(sp):
            sp.wait_ge(S["y_free"], 4 * NGROUP)
            sp.dma_start(w1_raw, a["L0_ffn_w1"].rearrange("e d f -> d e f")).then_inc(S["w1_loaded"], 16)
            for e in range(NEXP):
                sp.dma_start(w2_sb[:, e], a["L0_ffn_w2"][e].rearrange("(c f) n -> f c n", c=FC)).then_inc(S["fw_loaded"], 16)
            for dst, name in ((b2_all, "L0_ffn_b2"), (gam_all, "L0_ffn_gamma"), (bet_all, "L0_ffn_beta")):
                src = a[name].rearrange("(o e) n -> o e n", o=1).to_broadcast([128, NEXP, E_DIM])
                sp.dma_start(dst, src).then_inc(S["fw_loaded"], 16)
            sp.wait_ge(S["pad_ready"], 1)
            sp.wait_ge(S["w1_split"], 4)
            sp.dma_start(xs_dram[NEXP * REGION:NEXP * REGION + SLOT, :].rearrange("(s p) w -> p s w", s=2), pad_row)\
              .then_inc(S["pad_stored"], 16)
            sp.wait_ge(S["pad_stored"], 16)
            sp.wait_ge(S["tab_ready"], 1)
            sp.wait_ge(S["w1_split"], 4)
            for sc in scattered:
                sp.wait_ge(sc, 64 * PAIRS)
            sp.wait_ge(S["pad_gone"], 16 * 2 * NEXP)

            def load(i, n):
                need(sp, S["y_ready"], i - XBUF + 1)
                r = sp.value_load(tile_tab[0:1, bass.ds(i, 1)], min_val=0, max_val=NEXP * REGION)
                sp.dma_start(x_sl[n], xs_dram[bass.ds(r, SLOT), :].rearrange("(s p) w -> p s w", s=2))\
                  .then_inc(x_sl_loaded[n], 16)

            for n in range(XBUF):
                load(n, n)
            with sp.Fori(1, NTILE // XBUF) as u:
                for n in range(XBUF):
                    load(XBUF * u + n, n)
            for i in range(NTILE // XBUF * XBUF, NTILE):
                load(i, i % XBUF)

            for gone in y_gone:
                sp.wait_ge(gone, 32 * (NTILE // 2))

            def load_y(p, n):
                need(sp, S["sum_ready"], 2 * (p - 3))
                sp.dma_start(y_tok[n][0:CHUNK], y_dram[bass.ds(p * 2 * PT, 2 * PT), :].rearrange(
                    "(c r k) n -> r c k n", c=4, k=2)).then_inc(y_loaded[n], 16)

            for n in range(4):
                load_y(n, n)
            with sp.Fori(1, PAIRS // 4) as k:
                for n in range(4):
                    load_y(4 * k + n, n)

        @block.sync
        def _(sp):
            sp.dma_start(cst[:], a["consts"]).then_inc(S["c_loaded"], 16)
            sp.wait_ge(S["z_prep"], 1)
            n = 0

            def load(dst, src):
                nonlocal n
                n += 1
                sp.dma_start(dst, src).then_inc(S["w_loaded"], 16)

            load(wn[:, :, :], a["L0_tok_W"].rearrange("e (s c) p q -> e s (c p q)", c=CH))
            for k, name in ((0, "L0_tok_gamma"), (1, "L0_tok_beta")):
                for s in range(NSHIFT):
                    load(gb[k][GRID * s:GRID * s + GRID, :].rearrange("i (c r) -> i c r", c=CH),
                         a[name][CH * s:CH * s + CH].rearrange("c (i p) w -> i c (p w)", p=PATCH))
            load(bc[0:1, :], a["L0_tok_b"].rearrange("(o n) -> o n", o=1))
            load(bc[1:2, :], a["cls_tok"][0])
            for hd in range(NH):
                r = slice(HV * hd, HV * hd + HK)
                s = slice(HK * hd, HK * hd + HK)
                load(wn2[r, 0, :], a["L0_attn_Wq"][s, :])
                load(wn2[r, 1, :], a["L0_attn_Wk"][s, :])
                load(wn2[r, 2, 0:16], a["L0_attn_Wgk2"][s, :])
                load(nbgk[r, :], a["L0_attn_bgk2"][s].rearrange("(n o) -> n o", o=1))
                load(gnorm[HV * hd:HV * hd + HV, :], a["L0_attn_gnorm_w"].rearrange("(n o) -> n o", o=1))
            load(wgk1[0:16, :], a["L0_attn_Wgk1"])
            load(wn2[:, 3, :], a["L0_attn_Wg"])
            load(wn2[:, 4, :], a["L0_attn_Wv"])
            load(wn2[:, 5, :], a["L0_attn_Wo"])
            load(rw[:, :], a["L0_ffn_router_w"])
            load(b1_n[0:NEXP * FC, :], a["L0_ffn_b1"].rearrange("e (c f) -> (e c) f", c=FC))
            assert n == N_WLOADS, n

            def load_group(g, par):
                need(sp, S["xmn_done"], g - 1)
                need(sp, S["xhn_done"], g - 1)
                for b in range(GROUP):
                    img = a["x"][bass.ds(g * GROUP + b, 1)]
                    sp.dma_start(
                        xm[par][GRID * b:GRID * b + GRID, :].rearrange("i (c r) -> i c r", c=CH),
                        img.rearrange("o c (i p) w -> (o i) c (p w)", p=PATCH),
                    ).then_inc(x_loaded[par], 16)
                    sp.dma_start(
                        xh[par][HGRID * b + 1:HGRID * b + GRID, :].rearrange("m (c r) -> m c r", c=CH),
                        img[:, :, HALF:SIDE - HALF, :].rearrange("o c (m p) w -> (o m) c (p w)", p=PATCH),
                    ).then_inc(x_loaded[par], 16)
                edge = HALF * SIDE
                imgs = a["x"][bass.ds(g * GROUP, GROUP)]
                for m, r0, at in ((0, 0, edge), (HGRID - 1, SIDE - HALF, 0)):
                    sp.dma_start(
                        xh[par][m:m + (GROUP - 1) * HGRID + 1:HGRID, :].rearrange("b (c r) -> b c r", c=CH)[:, :, at:at + edge],
                        imgs[:, :, r0:r0 + HALF, :].rearrange("b c p w -> b c (p w)"),
                    ).then_inc(x_loaded[par], 16)

            load_group(0, 0)
            load_group(1, 1)
            with sp.Fori(1, NGROUP // 2) as k:
                load_group(2 * k, 0)
                load_group(2 * k + 1, 1)
            expert_sync(sp)

        @block.gpsimd
        def _(pool):
            for t in (wn2, nbgk[:, :], bet_t, xh[0], xh[1]):
                pool.memset(t, 0.0).then_inc(S["pch"], 1)
            pool.wait_ge(S["pch"], 5)
            pool.memset(st[:, :], 0.0).then_inc(S["z_prep"], 1)
            pool.wait_ge(S["prep_done"], 1)
            for t in (gx[0][:, :, :, 0:1], gx[1][:, :, :, 0:1], xe):
                pool.memset(t, 0.0).then_inc(S["pch"], 1)

            def scatter(p, par):
                pool.wait_ge(S["slots_ready"], p + 1)
                pool.wait_ge(S["row_copied"], p + 1)
                apart(pool)
                for t in range(4):
                    for k in range(2):
                        pool.indirect_dma_start(
                            xs_dram, bass.IndirectOffsetOnAxis(ap=slot_i[par][0:CHUNK, t, k:k + 1], axis=0),
                            row[par][0:CHUNK, k, t, :], None).then_inc(scattered[par], 16)

            pool.wait_ge(S["w1_loaded"], 16)
            W = S["w1_split"]
            pool.tensor_scalar(w1_raw, w1_raw, W_SCALE, None, ALU.mult).then_inc(W, 1)
            pool.wait_ge(W, 1)
            pool.tensor_copy(w1_hi, w1_raw).then_inc(W, 1)
            pool.wait_ge(W, 2)
            pool.tensor_tensor(w1_lo, w1_raw, w1_hi, ALU.subtract).then_inc(W, 1)
            pool.wait_ge(W, 3)
            pool.memset(pad_row[:, :, 0:129], 0.0).then_inc(W, 1)
            pool.wait_ge(S["base_ready"], 1)
            pool.memset(pad_row[:, :, 129:130], float(PAD_ID)).then_inc(S["pad_ready"], 1)

            with pool.Fori(0, PAIRS // 2) as k:
                scatter(2 * k, 0)
                scatter(2 * k + 1, 1)

            pool.wait_ge(S["cnt_ready"], 2)
            pool.wait_ge(W, 4)
            pool.wait_ge(S["pad_ready"], 1)
            for e in range(NEXP):
                for k in range(2):
                    pool.indirect_dma_start(
                        xs_dram, bass.IndirectOffsetOnAxis(ap=pad_i[:, k, e:e + 1], axis=0),
                        pad_row[:, k, :], None).then_inc(S["pad_gone"], 16)

            pool.wait_ge(S["fw_loaded"], 16 * (NEXP + 3))
            pool.wait_ge(S["pad_gone"], 16 * 2 * NEXP)

            def with_bias(i, n, u, e):
                pool.wait_ge(x_sl_loaded[n], 16 * u + 16)
                need(pool, S["t_ready"], i - 1)
                apart(pool)
                b2 = b2_all[:, bass.ds(e, 1), :].to_broadcast([128, 2, E_DIM])
                pool.tensor_tensor(x_b2[n % 2], x_sl[n][:, :, 0:E_DIM], b2, ALU.add).then_inc(S["xb_ready"], 1)

            def scatter_y(i, n, u, e):
                pool.wait_ge(S["y_ready"], i + 1)
                apart(pool)
                for k in range(2):
                    pool.indirect_dma_start(
                        y_dram, bass.IndirectOffsetOnAxis(ap=y_id[n % 2][:, k:k + 1], axis=0),
                        y_sl[n % 2][:, k, :], None, bounds_check=2 * NTOK - 1, oob_is_err=False,
                    ).then_inc(y_gone[n % 2], 16)

            def tile_iteration(at):
                at(1, with_bias)
                at(5, scatter_y)

            pool.wait_ge(S["tab_ready"], 1)
            tiles(pool, Chain(pool, None), 0, 0, tile_iteration)

        @block.tensor
        def _(pe):
            pe.wait_ge(S["c_loaded"], 16)
            pe.wait_ge(S["w_loaded"], 16 * N_WLOADS)
            T, D = S["t_prep"], S["d_prep"]
            for s in range(NSHIFT):
                ins = pe.transpose(ps[s // 4][:, 128 * (s % 4):128 * (s % 4) + 128], wn[:, s, :], ident)
            ins.then_inc(T, 1)
            for k in range(2):
                pe.wait_ge(D, 2 + k + 1)
                for j in range(GRID):
                    ins = pe.transpose(ps[2 + 2 * k + j // 7][:, 65 * (j % 7):65 * (j % 7) + 65],
                                       gbp[k][0:65, j].rearrange("r a b -> r (a b)"), ident[0:65, 0:65])
                ins.then_inc(T, 1)
            for n, w in enumerate((0, 1, 3, 4)):
                ins = pe.transpose(ps[6][:, 128 * n:128 * n + 128], wn2[:, w, :], ident)
            ins.then_inc(T, 1)
            pe.transpose(ps[7][:, 0:128], wn2[:, 5, :], ident)
            pe.transpose(ps[7][:, 384:384 + NEXP * FC], b1_n[0:NEXP * FC, :], ident[0:NEXP * FC, 0:NEXP * FC])
            pe.transpose(ps[7][0:16, 128:256], wn2[:, 2, 0:16], ident).then_inc(T, 1)
            pe.wait_ge(D, 8)
            pe.matmul(ps[7][:, 256:384], wgk1[0:16, :], wgk2t[0:16, :], start=True, stop=True).then_inc(T, 1)
            pe.wait_ge(D, 9)
            for hf in range(2):
                o = ps[0][0:CHUNK, 128 * hf:128 * hf + 128]
                for s in range(NSHIFT):
                    pe.matmul(o, bet_t[:, s, CHUNK * hf:CHUNK * hf + CHUNK], wt[:, s, :], start=s == 0, stop=False)
                x0, _y = cols["cls_sel"]
                ins = pe.matmul(o, cst[0:2, x0 + CHUNK * hf:x0 + CHUNK * hf + CHUNK], bc[0:2, :], start=False, stop=True)
            ins.then_inc(T, 1)

            fills = [[(xmn[0:MROWS, j], MROWS) for j in range(*f)] for f in MAIN_FILLS]
            fills += [[(xhn[0:HROWS, n], HROWS) for n in range(*f)] for f in HALF_FILLS]

            def transpose_fill(g, par, k):
                if k == 0:
                    pe.wait_ge(S["xmn_done"], g + 1)
                if k == 4:
                    pe.wait_ge(S["xhn_done"], g + 1)
                    pe.wait_ge(S["xen_done"], g + 1)
                need(pe, S["tr_free"], 8 * g + k - 3)
                for n, (src, rows) in enumerate(fills[k]):
                    ins = pe.transpose(ps[k % 4][:, rows * n:rows * n + rows],
                                       src.rearrange("r a b -> r (a b)"), ident[0:rows, 0:rows])
                ins.then_inc(S["tr_full"], 1)

            def y_fill(g, par, k):
                if k == 0:
                    pe.wait_ge(S["tr_free"], 8 * g + 8)
                need(pe, S["y_free"], 4 * g + k - 1)
                for t in range(4):
                    b, hf = 2 * k + t // 2, t % 2
                    for s in range(NSHIFT):
                        ins = pe.matmul(ps[4 + k % 2][0:CHUNK, 128 * t:128 * t + 128],
                                        gx[par][:, s, b, CHUNK * hf:CHUNK * hf + CHUNK], wt[:, s, :],
                                        start=s == 0, stop=s == NSHIFT - 1)
                ins.then_inc(S["y_full"], 1)

            def stats(g):
                pe.wait_ge(S["dsum_done"], g + 1)
                pe.wait_ge(S["asum_done"], g + 1)
                need(pe, S["var_done"], g)
                x0 = cols["stat_all"][0]
                x1 = cols["stat_edge"][0]
                for k in range(2):
                    o = ps[6][0:HROWS, 2 * k:2 * k + 2]
                    pe.matmul(o, cst[0:HROWS, x0 + k * HROWS:x0 + (k + 1) * HROWS], st[0:HROWS, 0:2], start=True, stop=False)
                    ins = pe.matmul(o, cst[0:HROWS, x1 + k * HROWS:x1 + (k + 1) * HROWS], st[0:HROWS, 2:4],
                                    start=False, stop=True)
                ins.then_inc(S["stat_ps"], 1)

            def group(g, par, tr=True, y=True, stat=True):
                for k in range(8):
                    if tr:
                        transpose_fill(g, par, k)
                    if k % 2 and y:
                        y_fill(g - 1, 1 - par, k // 2)
                    if k == 3 and stat:
                        stats(g + 1)

            pe.wait_ge(S["prep_done"], 1)
            stats(0)
            group(0, 0, y=False)
            group(1, 1)
            group(2, 0)
            with pe.Fori(1, NGROUP // 2 - 1) as k:
                group(2 * k + 1, 1)
                group(2 * k + 2, 0)
            group(NGROUP - 1, 1, stat=False)
            group(NGROUP, 0, tr=False, stat=False)

            def chunk(c):
                return slice(CHUNK * c, CHUNK * c + CHUNK)

            def front_transpose(p, par, half):
                pe.wait_ge(S["xn_ready"], 4 * p + 4)
                need(pe, S["g_copied"], p)
                for c in range(4):
                    ins = pe.transpose(ps[0][:, chunk(c)], xn[0:CHUNK, c, :], ident[0:CHUNK, 0:CHUNK])
                ins.then_inc(S["xnt_ps"], 1)

            def project(bank, w, done):
                pe.matmul(ps[bank][:, 0:PT], wproj[:, w, :], xn_t, start=True, stop=True).then_inc(S[done], 1)

            def project_gk(p, par, half):
                pe.wait_ge(S["xnt_sb"], p + 1)
                need(pe, S["v_ready"], p)
                project(1, 2, "gk_ps")

            def project_q(p, par, half):
                project(0, 0, "q_ps")

            def project_k(p, par, half):
                pe.wait_ge(S["l_ready"], p + 1)
                project(1, 1, "k_ps")

            def project_g(p, par, half):
                pe.wait_ge(S["q_copied"], p + 1)
                project(0, 3, "g_ps")

            def values(p, par, half):
                pe.wait_ge(S["k_copied"], p + 1)
                for c in range(4):
                    ins = pe.matmul(ps[1][0:CHUNK, 128 * c:128 * c + 128], xn_t[:, chunk(c)], wproj[:, 4, :],
                                    start=True, stop=True)
                ins.then_inc(S["v_ps"], 1)

            def scores(p, par, half, hd):
                if hd == 0:
                    pe.wait_ge(S["qk_ready"], 2 * p + 2)
                need(pe, S["att_ready"], 4 * p + hd - 1)
                r = slice(HV * hd, HV * hd + HV)
                for c in range(4):
                    ins = pe.matmul(ps[2 + hd % 2][0:CHUNK, chunk(c)], kd[par][r, chunk(c)], qd[par][r, chunk(c)],
                                    start=True, stop=True, tile_position=(HV * hd, 0))
                ins.then_inc(S["sc_ps"], 1)

            def keys(p, par, half):
                pe.wait_ge(S["qk_ready"], 2 * p + 2)
                need(pe, S["state_ready"], 2 * p)
                for i in range(2):
                    ins = pe.transpose(ps[6][0:CHUNK, 128 * i:128 * i + 128], kd[par][:, chunk(2 * i)], ident)
                ins.then_inc(S["kt_ps"], 1)

            def states(p, par, half):
                pe.wait_ge(S["v_ready"], p + 1)
                pe.wait_ge(S["kt_ready"], p + 1)
                for i in range(2):
                    ins = pe.matmul(ps[6][:, 256 + 128 * i:384 + 128 * i], k_tok[0:CHUNK, i, :],
                                    val[par][0:CHUNK, 2 * i, :], start=True, stop=True)
                ins.then_inc(S["st_ps"], 1)

            def outputs(p, par, half):
                pe.wait_ge(S["att_ready"], 4 * p + 4)
                pe.wait_ge(S["state_ready"], 2 * p + 2)
                need(pe, S["og_ready"], p)
                for c in range(4):
                    if c % 2:
                        pe.matmul(ps[4][:, chunk(c)], state[:, c // 2, :], qd[par][:, chunk(c)], start=True, stop=True)
                    for hd in range(NH):
                        r = slice(HV * hd, HV * hd + HV)
                        ins = pe.matmul(ps[4][r, chunk(c)], val[par][0:CHUNK, c, r], att[0:CHUNK, hd, c, :],
                                        start=c % 2 == 0, stop=True, tile_position=(0, HV * hd),
                                        skip_group_check=True)
                ins.then_inc(S["o_ps"], 1)

            def mean_squares(p, par, half):
                pe.wait_ge(S["sq_ready"], p + 1)
                need(pe, S["h1_ready"], p)
                pe.matmul(ps[5][:, 0:PT], con("meanv"), o_sq, start=True, stop=True).then_inc(S["ms_ps"], 1)

            def attention_out(p, par, half):
                pe.wait_ge(S["o_ready"], p + 1)
                for c in range(4):
                    ins = pe.matmul(ps[5][0:CHUNK, 128 * c:128 * c + 128], o_f[:, chunk(c)], wproj[:, 5, :],
                                    start=True, stop=True)
                ins.then_inc(S["ao_ps"], 1)

            def route_transpose(p, par, half):
                pe.wait_ge(S["xn2_ready"], 4 * p + 4)
                need(pe, S["rank_copied"], p)
                for c in range(4):
                    ins = pe.transpose(ps[7][:, chunk(c)], row[par][0:CHUNK, 0, c, 0:128], ident[0:CHUNK, 0:CHUNK])
                ins.then_inc(S["xn2t_ps"], 1)

            def route_logits(p, par, half):
                pe.wait_ge(S["xn2t_sb"], p + 1)
                for c in range(4):
                    ins = pe.matmul(ps[7][0:CHUNK, 352 + 8 * c:360 + 8 * c], xn2_t[:, chunk(c)], rw[:, :],
                                    start=True, stop=True)
                ins.then_inc(S["lg_ps"], 1)

            def ranks(p, par, half):
                pe.wait_ge(S["om_ready"], p + 1)
                o2 = om[0:CHUNK].rearrange("p c e -> p (c e)")
                pe.matmul(ps[7][0:CHUNK, 384:416], con("before", CHUNK), o2, start=True, stop=True)
                pe.matmul(ps[7][0:CHUNK, 416:448], con("ones", CHUNK), o2, start=True, stop=True).then_inc(S["rk_ps"], 1)

            def iteration(at):
                at(4, route_logits)
                at(1, scores, 1)
                at(0, front_transpose)
                at(2, mean_squares)
                at(0, project_gk)
                at(0, project_q)
                at(0, project_k)
                at(0, project_g)
                at(1, scores, 2)
                at(0, values)
                at(1, scores, 3)
                at(4, ranks)
                at(0, keys)
                at(0, scores, 0)
                at(2, attention_out)
                at(0, states)
                at(3, route_transpose)
                at(1, outputs)

            pairs(pe, Chain(pe, None), 0, 0, iteration)

            pe.wait_ge(S["cnt_ready"], 1)
            pe.matmul(ps[0][:, 0:NEXP], con("one_row", 1), cnt[0:1, :], start=True, stop=True).then_inc(S["cnt_ps"], 1)
            pe.wait_ge(S["tab_ready"], 1)
            pe.wait_ge(S["w1_split"], 3)
            pe.wait_ge(S["fw_loaded"], 16 * (NEXP + 3))

            copies = []

            def own(e):
                copies.append(pe.alloc_register(name=f"expert_copy_{len(copies)}"))
                pe.reg_mov(copies[-1], e)
                return bass.RuntimeValue.of_register_unchecked(copies[-1], min_val=0, max_val=NEXP - 1)

            def slots_transpose(i, n, u, e):
                pe.wait_ge(x_sl_loaded[n], 16 * u + 16)
                need(pe, S["xlo_ready"], i - 1)
                for k in range(2):
                    ins = pe.transpose(ps[n % 2][:, 128 * k:128 * k + 128], x_sl[n][:, k, 0:E_DIM], ident)
                ins.then_inc(S["xt_ps"], 1)

            def hidden(i, n, u, e):
                m = n % 2
                e = own(e)
                pe.wait_ge(S["xlo_ready"], i + 1)
                need(pe, S["h_ready"], 4 * (i - 2) + 2)
                for c in range(FC):
                    if c == 2:
                        need(pe, S["h_ready"], 4 * (i - 2) + 4)
                    o = ps[2 + 2 * m + c // 2][:, SLOT * (c % 2):SLOT * (c % 2) + SLOT]
                    f = slice(128 * c, 128 * c + 128)
                    hi = w1_hi[:, bass.ds(e, 1), f].rearrange("p o f -> p (o f)")
                    lo = w1_lo[:, bass.ds(e, 1), f].rearrange("p o f -> p (o f)")
                    pe.matmul(o, hi, x_hi[m], start=True, stop=False)
                    pe.matmul(o, hi, x_lo[m], start=False, stop=False)
                    pe.matmul(o, lo, x_hi[m], start=False, stop=True).then_inc(S["h_ps"], 1)

            def second_layer(i, n, u, e):
                m = n % 2
                e = own(e)
                pe.wait_ge(S["h_ready"], 4 * i + 4)
                need(pe, S["t_ready"], i - 1)
                for k in range(2):
                    for c in range(FC):
                        ins = pe.matmul(ps[6 + m][:, 128 * k:128 * k + 128], hid[m][:, c, 128 * k:128 * k + 128],
                                        w2_sb[:, bass.ds(e, 1), c, :].rearrange("p o n -> p (o n)"),
                                        start=c == 0, stop=c == FC - 1)
                ins.then_inc(S["w2_ps"], 1)

            def tile_iteration(at):
                at(1, hidden)
                at(0, slots_transpose)
                at(2, second_layer)

            tiles(pe, Chain(pe, None), 0, 0, tile_iteration)

        @block.vector
        def _(dve):
            ch = Chain(dve, S["dch"])
            T, D = S["t_prep"], S["d_prep"]
            dve.wait_ge(T, 1)
            dve.tensor_copy(wt[:, 0:4, :], ps[0][:, :].rearrange("p (s n) -> p s n", s=4)).then_inc(D, 1)
            dve.tensor_copy(wt[:, 4, :], ps[1][:, 0:128]).then_inc(D, 1)
            dve.wait_ge(S["w_loaded"], 16 * N_WLOADS)
            for k in range(2):
                dve.tensor_copy(gbp[k][0:65], gb[k][0:65, :].rearrange(
                    "r (cp j q) -> r j cp q", j=GRID, q=PATCH)).then_inc(D, 1)
            dve.wait_ge(T, 3)
            for k in range(2):
                for half, (j0, j1) in enumerate(((0, 7), (7, 13))):
                    src = ps[2 + 2 * k + half][:, 0:65 * (j1 - j0)].rearrange("p (j s i) -> p s i j", s=NSHIFT, i=GRID)
                    for s in range(NSHIFT):
                        dst = (gam_t[:, s] if k == 0 else
                               bet_t[:, s, 1:TOK].rearrange("p (i j) -> p i j", i=GRID))[:, :, j0:j1]
                        ins = dve.tensor_copy(dst, src[:, s])
                        if not (k and half and s == NSHIFT - 1):
                            ins.then_inc(S["dch"], 1)
                            ch.n += 1
            ins.then_inc(D, 1)
            dve.wait_ge(T, 5)
            dve.tensor_copy(b1_t[:, :], ps[7][:, 384:384 + NEXP * FC]).then_inc(S["dch"], 1)
            ch.n += 1
            dve.tensor_scalar(wproj[:, 0, :], ps[6][:, 0:128], HK ** -0.5, None, ALU.mult).then_inc(D, 1)
            dve.tensor_copy(wproj[:, 1, :], ps[6][:, 128:256]).then_inc(D, 1)
            dve.tensor_copy(wgk2t[0:16, :], ps[7][0:16, 128:256]).then_inc(D, 1)
            dve.wait_ge(T, 6)
            dve.tensor_copy(wproj[:, 3:5, :], ps[6][:, 256:512].rearrange("p (a n) -> p a n", a=2)).then_inc(S["dch"], 1)
            dve.tensor_scalar(wproj[:, 5, :], ps[7][:, 0:128], gnorm[:, 0:1], None, ALU.mult).then_inc(S["dch"], 1)
            dve.tensor_scalar(nbgk[:, :], nbgk[:, :], -1.0, None, ALU.mult).then_inc(S["dch"], 1)
            ch.n += 3
            dve.tensor_copy(wproj[:, 2, :], ps[7][:, 256:384]).then_inc(D, 1)
            dve.wait_ge(T, 7)
            ch.link(dve.tensor_copy(bt[:, :, :], ps[0][0:CHUNK, 0:256].rearrange("p (a n) -> p a n", a=2)))
            dve.tensor_copy(st[0:1, 20:21], st[0:1, 21:22]).then_inc(S["prep_done"], 1)
            dve.wait_ge(S["pch"], 8)
            dbase = ch.n

            def stats_sums(g, par, u):
                dve.wait_ge(x_loaded[par], 16 * GROUP_DMAS * (u + 1))
                need(dve, S["xen_done"], g)
                need(dve, S["asum_done"], g)
                need(dve, S["stat_ps"], g)
                x3 = xh[par][0:HROWS, :].rearrange("r (cp w) -> r cp w", w=SIDE)
                ch.link(dve.tensor_copy(xe[0:HROWS, 0, :, HALF:PATCH], x3[:, :, 0:HALF]))
                dve.tensor_copy(xe[0:HROWS, 1, :, 0:HALF], x3[:, :, SIDE - HALF:SIDE]).then_inc(S["edge_done"], 1)
                dve.wait_ge(S["edge_done"], g + 1)
                ch.link(dve.tensor_reduce(st[0:HROWS, 2:3], xe[0:HROWS].rearrange("r a b c -> r (a b c)"), AX_X, ALU.add))
                dve.tensor_reduce(st[0:HROWS, 0:1], xh[par][0:HROWS, :], AX_X, ALU.add).then_inc(S["dsum_done"], 1)

            def stats_small(g):
                dve.wait_ge(S["stat_ps"], g + 1)
                need(dve, S["xhn_done"], g)
                m = st[0:HROWS, 4:8].rearrange("r (k a) -> r k a", k=2)
                ch.link(dve.tensor_scalar(st[0:HROWS, 4:8], ps[6][0:HROWS, 0:4], 1.0 / N_CONCAT, None, ALU.mult))
                ch.link(dve.tensor_tensor(st[0:HROWS, 8:10], m[:, :, 0], m[:, :, 0], ALU.mult))
                dve.tensor_tensor(st[0:HROWS, 10:12], m[:, :, 1], st[0:HROWS, 8:10], ALU.subtract).then_inc(S["var_done"], 1)

            def normalise(g, par):
                m = st[0:HROWS, 4:8].rearrange("r (k a) -> r k a", k=2)
                dve.wait_ge(S["rstd0_done"], g + 1)
                dve.scalar_tensor_tensor(st[0:HROWS, 16:18], m[:, :, 0], -1.0, st[0:HROWS, 14:16],
                                         ALU.mult, ALU.mult).then_inc(S["nb_done"], 1)
                dve.wait_ge(S["nb_done"], g + 1)
                need(dve, S["tr_full"], 8 * g)
                dve.tensor_scalar(xhn[0:HROWS, 0:HGRID:HGRID - 1], xe[0:HROWS], st[0:HROWS, 14:15], st[0:HROWS, 16:17],
                                  ALU.mult, ALU.add).then_inc(S["xen_done"], 1)
                dve.tensor_scalar(xmn[0:MROWS], xm[par][0:MROWS, :].rearrange("r (cp j q) -> r j cp q", j=GRID, q=PATCH), st[0:MROWS, 15:16], st[0:MROWS, 17:18],
                                  ALU.mult, ALU.add).then_inc(S["xmn_done"], 1)

            def scale_fill(g, par, k):
                dve.wait_ge(S["tr_full"], 8 * g + k + 1)
                if k == 0:
                    need(dve, S["y_full"], 4 * g - 4)

                def put(s, j0, j1, src):
                    dst = gx[par][:, s, :, 1:TOK].rearrange("p b (i j) -> p b i j", i=GRID)[:, :, :, j0:j1]
                    gm = gam_t[:, s, :, j0:j1].unsqueeze(1).to_broadcast([128, GROUP, GRID, j1 - j0])
                    return dve.tensor_tensor(dst, src, gm, ALU.mult)

                if k < 4:
                    j0, j1 = MAIN_FILLS[k]
                    v = ps[k][:, 0:MROWS * (j1 - j0)].rearrange("p (j b i) -> p b i j", b=GROUP, i=GRID)
                    put(0, j0, j1, v).then_inc(S["tr_free"], 1)
                    return
                n0, n1 = HALF_FILLS[k - 4]
                v = ps[k - 4][:, 0:HROWS * (n1 - n0)].rearrange("p (j b m) -> p b m j", b=GROUP, m=HGRID)
                for s in range(1, NSHIFT):
                    m0 = 1 if s <= 2 else 0
                    right = (s - 1) % 2
                    j0, j1 = max(n0 - right, 0), min(n1 - right, GRID)
                    ins = put(s, j0, j1, v[:, :, m0:m0 + GRID, j0 + right - n0:j1 + right - n0])
                    ins.then_inc(S["tr_free"] if s == NSHIFT - 1 else S["dch"], 1)
                    ch.n += s < NSHIFT - 1

            def y_out(g, k):
                dve.wait_ge(S["y_full"], 4 * g + k + 1)
                src = ps[4 + k % 2][0:CHUNK, :].rearrange("p (i t n) -> p i t n", i=2, t=2)
                dst = h[0:CHUNK, bass.ds(4 * g + k, 1), :, :].rearrange("p o (i t) n -> p (o i) t n", i=2)
                b4 = bt[:, :, :].unsqueeze(1).to_broadcast([CHUNK, 2, 2, E_DIM])
                dve.tensor_tensor(dst, src, b4, ALU.add).then_inc(S["y_free"], 1)

            def group(g, par, base, u, tr=True, y=True, stat=True):
                ch.start(base)
                for k in range(8):
                    if k == 2 and stat:
                        stats_sums(g + 1, 1 - par, u)
                    if tr:
                        scale_fill(g, par, k)
                    if k % 2 and y:
                        y_out(g - 1, k // 2)
                    if k == 4 and stat:
                        stats_small(g + 1)
                if stat:
                    normalise(g + 1, 1 - par)
                return ch.n

            ch.start(dbase)
            stats_sums(0, 0, 0)
            stats_small(0)
            normalise(0, 0)
            dbase += ch.n
            per = group(0, 0, dbase, 0, y=False)
            dbase += per
            for g in (1, 2):
                assert group(g, g % 2, dbase + (g - 1) * per, g // 2 + g % 2) == per
            with dve.Fori(1, NGROUP // 2 - 1) as k:
                assert group(2 * k + 1, 1, dbase + k * (2 * per), k + 1) == per
                assert group(2 * k + 2, 0, dbase + per + k * (2 * per), k + 1) == per
            dbase += per * (NGROUP - 2)
            dbase += group(NGROUP - 1, 1, dbase, 0, stat=False)
            dbase += group(NGROUP, 0, dbase, 0, tr=False, stat=False)

            R = slice(0, CHUNK)

            def ln_stats(p, b, m, done):
                for c in range(4):
                    ch.step(dve.bn_stats(b[R, c], h[R, bass.ds(p, 1), c, :].rearrange("p o n -> p (o n)")))
                ch.settle()
                for c in range(4):
                    ins = dve.bn_aggr(m[R, c], b[R, c])
                    if c < 3:
                        ch.step(ins)
                ins.then_inc(S[done], 1)

            def shift(p, m, rstd, nb, ready, done):
                dve.wait_ge(S[ready], p + 1)
                dve.scalar_tensor_tensor(nb[R, :], m[R, :, 0], -1.0, rstd[R, :], ALU.mult, ALU.mult).then_inc(S[done], 1)

            def ln1_stats(p, par, half):
                ln_stats(p, bns, mv, "ln1_stats")

            def ln1_shift(p, par, half):
                shift(p, mv, rstd1, nb1, "ln1_rstd", "nb1_ready")

            def ln2_stats(p, par, half):
                dve.wait_ge(S["h1_ready"], p + 1)
                apart(dve)
                ln_stats(p, bns2, mv2, "ln2_stats")

            def ln2_shift(p, par, half):
                shift(p, mv2, rstd2, nb2, "ln2_rstd", "nb2_ready")

            def scan(p, par, half):
                dve.wait_ge(S["l_ready"], p + 1)
                need(dve, S["e_ready"], 2 * p)
                dve.tensor_tensor_scan(cum, con("reset"), l_gk, 0.0, ALU.mult, ALU.add).then_inc(S["scan_done"], 1)

            def decayed(p, par, half):
                dve.wait_ge(S["e_ready"], 2 * p + 2)
                dve.wait_ge(S["k_copied"], p + 1)
                dve.tensor_tensor(qd[par], qd[par], decay[par], ALU.mult).then_inc(S["qk_ready"], 1)
                dve.tensor_tensor(kd[par], kd[par], grow, ALU.mult).then_inc(S["qk_ready"], 1)

            def masked(p, par, half, hd):
                if hd == 0:
                    need(dve, S["o_ps"], p)
                dve.wait_ge(S["sc_ps"], 4 * p + hd + 1)
                src = ps[2 + hd % 2][R, 0:PT].rearrange("p (c t) -> p c t", c=4)
                mask = con("causal", CHUNK).unsqueeze(1).to_broadcast([CHUNK, 4, CHUNK])
                dve.tensor_tensor(att[R, hd], src, mask, ALU.mult).then_inc(S["att_ready"], 1)

            def state_out(p, par, half):
                dve.wait_ge(S["st_ps"], p + 1)
                need(dve, S["o_ps"], p)
                for i in range(2):
                    end = CHUNK * (2 * i + 1) - 1
                    dve.scalar_tensor_tensor(state[:, i, :], ps[6][:, 256 + 128 * i:384 + 128 * i],
                                             decay[par][:, end:end + 1], con("heads"), ALU.mult, ALU.mult)\
                       .then_inc(S["state_ready"], 1)

            def gated(p, par, half):
                dve.wait_ge(S["sq_ready"], p + 1)
                need(dve, S["ao_ps"], p)
                dve.tensor_tensor(o_f, ps[4][:, 0:PT], gate[par], ALU.mult).then_inc(S["og_ready"], 1)

            def log_factor(p, par, half):
                dve.wait_ge(S["lms_ready"], p + 1)
                dve.wait_ge(S["g_ready"], p + 1)
                dve.scalar_tensor_tensor(fac, fac, -0.5, l_g[par], ALU.mult, ALU.subtract).then_inc(S["u_ready"], 1)

            def factored(p, par, half):
                dve.wait_ge(S["fac_ready"], p + 1)
                dve.wait_ge(S["og_ready"], p + 1)
                dve.tensor_tensor(o_f, o_f, fac, ALU.mult).then_inc(S["o_ready"], 1)

            def residual(p, par, half):
                dve.wait_ge(S["ao_ps"], p + 1)
                hp = h[R, bass.ds(p, 1), :, :].rearrange("p o c n -> p (o c n)")
                dve.tensor_tensor(hp, hp, ps[5][R, :], ALU.add).then_inc(S["h1_ready"], 1)

            def logits_out(p, par, half):
                dve.wait_ge(S["lg_ps"], p + 1)
                dve.tensor_copy(lg[R], ps[7][R, 352:384].rearrange("p (c e) -> p c e", c=4)).then_inc(S["lg_ready"], 1)

            def choose(p, par, half):
                dve.wait_ge(S["lg_ready"], p + 1)
                apart(dve)
                for c in range(4):
                    ch.step(dve.max(mx[R, c], lg[R, c]))
                ch.settle()
                for c in range(4):
                    ch.step(dve.max_index(mi[R, c], mx[R, c], lg[R, c]))
                dve.tensor_tensor(dif[R, :], mx[R, :, 1], mx[R, :, 0], ALU.subtract).then_inc(S["dif_ready"], 1)
                ch.settle()
                ch.link(dve.tensor_copy(ef[R], mi[R, :, 0:2]))
                x0, x1 = cols["expert"]
                ex = cst[R, x0:x1].unsqueeze(1).to_broadcast([CHUNK, 8, NEXP])
                ef3 = ef[R].rearrange("p c k -> p (c k)").unsqueeze(2).to_broadcast([CHUNK, 8, NEXP])
                ch.link(dve.tensor_tensor(oh[R].rearrange("p c k e -> p (c k) e"), ex, ef3, ALU.is_equal))
                dve.tensor_tensor(om[R], oh[R, :, 0], oh[R, :, 1], ALU.add).then_inc(S["om_ready"], 1)

            def place(p, par, half):
                rw0, rw1 = row[par][R, 0], row[par][R, 1]
                dve.wait_ge(S["rk_ps"], p + 1)
                dve.tensor_copy(rk[R], ps[7][R, 384:448].rearrange("p (a c e) -> p a c e", a=2, c=4))\
                   .then_inc(S["rank_copied"], 1)
                dve.wait_ge(S["edif_ready"], p + 1)
                need(dve, scattered[par], 128 * half)
                ch.step(dve.tensor_scalar(den[R, :], edif[R, :], 1.0, None, ALU.add))
                ch.link(dve.tensor_copy(rw0[:, :, 129], ids[R, :]))
                dve.wait_ge(S["rank_copied"], p + 1)
                for c in range(4):
                    ch.step(dve.tensor_tensor(pos[R, c], rk[R, 0, c], base[R, :], ALU.add))
                    if c == 0:
                        ch.link(dve.reciprocal(rw0[:, :, 128], den[R, :]))
                        ch.step(dve.tensor_tensor(base[R, :], base[R, :], rk[R, 1, c], ALU.add))
                        ch.link(dve.tensor_scalar(rw1[:, :, 129], ids[R, :], 1.0, None, ALU.add))
                    elif c == 1:
                        ch.step(dve.tensor_tensor(base[R, :], base[R, :], rk[R, 1, c], ALU.add))
                        ch.link(dve.tensor_tensor(rw1[:, :, 128], rw0[:, :, 128], edif[R, :], ALU.mult))
                    elif c == 2:
                        ch.step(dve.tensor_tensor(base[R, :], base[R, :], rk[R, 1, c], ALU.add))
                        ch.link(dve.tensor_scalar(ids[R, :], ids[R, :], float(2 * PT), None, ALU.add))
                    else:
                        ch.link(dve.tensor_tensor(base[R, :], base[R, :], rk[R, 1, c], ALU.add))
                p4 = pos[R].unsqueeze(2).to_broadcast([CHUNK, 4, 2, NEXP])
                ch.link(dve.tensor_tensor(pp[R], oh[R], p4, ALU.mult))
                ch.link(dve.tensor_reduce(slot_f[R], pp[R], AX_X, ALU.add))
                dve.tensor_copy(slot_i[par][R], slot_f[R]).then_inc(S["slots_ready"], 1)

            def iteration(at):
                at(0, ln1_stats)
                at(3, residual)
                at(0, ln1_shift)
                at(3, ln2_stats)
                at(1, masked, 0)
                at(4, logits_out)
                at(2, gated)
                at(3, ln2_shift)
                at(1, masked, 1)
                at(1, state_out)
                at(2, log_factor)
                at(0, scan)
                at(4, choose)
                at(0, decayed)
                at(1, masked, 2)
                at(1, masked, 3)
                at(2, factored)
                at(4, place)

            ch.start(dbase)
            ch.link(dve.tensor_copy(base[R, :], con("region", CHUNK)))
            dve.tensor_copy(ids[R, :], con("tokid", CHUNK)).then_inc(S["base_ready"], 1)
            dve.wait_ge(S["base_ready"], 1)
            dbase = pairs(dve, ch, dbase + 1, DVE_PAIR, iteration)

            ch.start(dbase)
            dve.tensor_tensor(cnt[R, :], base[R, :], con("region", CHUNK), ALU.subtract).then_inc(S["cnt_ready"], 1)
            dve.wait_ge(S["cnt_ps"], 1)
            ch.link(dve.tensor_copy(cnt_all, ps[0][:, 0:NEXP]))
            ch.link(dve.tensor_tensor(pad_f, cnt_all, con("region"), ALU.add))
            sid = con("slotid")
            for k in range(2):
                ins = dve.tensor_scalar(pad_i[:, k, :], pad_f, sid[:, k:k + 1], None, ALU.add)
                if k == 0:
                    ch.link(ins)
            ins.then_inc(S["cnt_ready"], 1)
            c1 = cnt_all[0:1, :].unsqueeze(2).to_broadcast([1, NEXP, 43])
            k1 = con("tiles_k", 1).unsqueeze(1).to_broadcast([1, NEXP, 43])
            ch.link(dve.tensor_tensor(more[0:1], c1, k1, ALU.is_gt))
            ch.link(dve.tensor_reduce(ntiles[0:1, :], more[0:1], AX_X, ALU.add))
            ch.link(dve.tensor_tensor_scan(tile_end[0:1, :], con("one_row", 1)[:, 0:NEXP], ntiles[0:1, :], 0.0, ALU.mult, ALU.add))
            ch.link(dve.tensor_scalar(skip[0:1, :], ntiles[0:1, :], -float(SLOT), float(REGION), ALU.mult, ALU.add))
            ch.link(dve.tensor_scalar(tab_f[:, 0, :], con("tile_no", 1), float(SLOT), None, ALU.mult))
            ch.link(dve.memset(tab_f[:, 1, :], 0.0))
            for e in range(NEXP):
                past = more[0:1].rearrange("p a b -> p (a b)")[:, 0:XBUF * NBLOCK]
                ch.link(dve.tensor_scalar(past, con("tile_no", 1), tile_end[0:1, e:e + 1], None, ALU.is_ge))
                ch.link(dve.tensor_tensor(tab_f[:, 1, :], tab_f[:, 1, :], past, ALU.add))
                ch.link(dve.scalar_tensor_tensor(tab_f[:, 0, :], past, skip[0:1, e:e + 1], tab_f[:, 0, :], ALU.mult, ALU.add))
            ch.link(dve.tensor_scalar(tab_f[:, 0, :], tab_f[:, 0, :], float(NEXP * REGION), None, ALU.min))
            ch.link(dve.tensor_scalar(tab_f[:, 1, :], tab_f[:, 1, :], float(NEXP - 1), None, ALU.min))
            ch.link(dve.tensor_copy(tile_tab[:, :], tab_f[:, 0, :]))
            ch.link(dve.memset(expert_tab[:, :, :], 0))
            by_block = tab_f[:, 1, :].rearrange("p (u n) -> p u n", n=XBUF)
            ch.link(dve.tensor_copy(expert_tab[:, :, XBUF:2 * XBUF], by_block))
            dve.tensor_copy(expert_tab[:, 1:NBLOCK, 0:XBUF], by_block[:, 0:NBLOCK - 1, :]).then_inc(S["tab_ready"], 1)
            dbase += ch.n
            dve.wait_ge(S["tab_ready"], 1)
            dve.wait_ge(S["pad_gone"], 16 * 2 * NEXP)
            dve.wait_ge(S["fw_loaded"], 16 * (NEXP + 3))

            def lower_half(i, n, u, e):
                m = n % 2
                dve.wait_ge(S["xhi_ready"], i + 1)
                need(dve, S["h_ps"], 4 * (i - 1))
                dve.tensor_tensor(x_lo[m], ps[m][:, 0:SLOT], x_hi[m], ALU.subtract).then_inc(S["xlo_ready"], 1)

            def sums(i, n, u, e):
                m = n % 2
                dve.wait_ge(S["w2_ps"], i + 1)
                dve.wait_ge(S["xb_ready"], i + 1)
                need(dve, S["norm_ready"], i - 1)
                dve.tensor_tensor(res[m], ps[6 + m][:, 0:SLOT].rearrange("p (k n) -> p k n", k=2), x_b2[m],
                                  ALU.add).then_inc(S["t_ready"], 1)

            def tile_stats(i, n, u, e):
                dve.wait_ge(S["t_ready"], i + 1)
                need(dve, S["rstd3_stats"], i)
                ch.step(dve.bn_stats(bns3[:, 0], res[n % 2][:, 0, :]))
                dve.bn_stats(bns3[:, 1], res[n % 2][:, 1, :]).then_inc(S["bns3_ready"], 1)

            def tile_moments(i, n, u, e):
                dve.wait_ge(S["bns3_ready"], i + 1)
                need(dve, S["norm_ready"], i)
                apart(dve)
                ch.step(dve.bn_aggr(mv3[:, 0], bns3[:, 0]))
                dve.bn_aggr(mv3[:, 1], bns3[:, 1]).then_inc(S["rstd3_stats"], 1)

            def gated_rstd(i, n, u, e):
                dve.wait_ge(S["rstd3_ready"], i + 1)
                dve.tensor_tensor(rg3, rstd3, x_sl[n][:, :, E_DIM], ALU.mult).then_inc(S["gate_ready"], 1)

            def tile_norm(i, n, u, e):
                dve.wait_ge(S["gate_ready"], i + 1)
                need(dve, S["scl_ready"], i)
                for k in range(2):
                    ins = dve.tensor_scalar(nrm[:, k, :], res[n % 2][:, k, :], mv3[:, k, 0:1], rg3[:, k:k + 1],
                                            ALU.subtract, ALU.mult)
                    if k == 0:
                        ch.step(ins)
                ins.then_inc(S["norm_ready"], 1)

            def scaled(i, n, u, e):
                dve.wait_ge(S["norm_ready"], i + 1)
                need(dve, S["y_ready"], i)
                gm = gam_all[:, bass.ds(e, 1), :].to_broadcast([128, 2, E_DIM])
                dve.tensor_tensor(scl, nrm, gm, ALU.mult).then_inc(S["scl_ready"], 1)

            def shifted(i, n, u, e):
                g = x_sl[n][:, :, E_DIM]
                dve.wait_ge(S["scl_ready"], i + 1)
                need(dve, y_gone[n % 2], 32 * (XBUF // 2 * u + n // 2))
                ch.step(dve.tensor_copy(y_id[n % 2], x_sl[n][:, :, E_DIM + 1]))
                be = bet_all[:, bass.ds(e, 1), :].rearrange("p o n -> p (o n)")
                for k in range(2):
                    ins = dve.scalar_tensor_tensor(y_sl[n % 2][:, k, :], be, g[:, k:k + 1], scl[:, k, :],
                                                   ALU.mult, ALU.add)
                    if k == 0:
                        ch.step(ins)
                ins.then_inc(S["y_ready"], 1)

            def tile_iteration(at):
                at(1, lower_half)
                at(5, scaled)
                at(4, tile_moments)
                at(5, shifted)
                at(3, sums)
                at(4, gated_rstd)
                at(4, tile_norm)
                at(3, tile_stats)

            dbase = tiles(dve, ch, dbase, DVE_TILE, tile_iteration)

            def combine(p, n, u):
                dve.wait_ge(y_loaded[n], 16 * u + 16)
                hp = h[R, bass.ds(p, 1), :, :].rearrange("p o c n -> p (o c) n")
                for k in range(2):
                    dve.tensor_tensor(hp, hp, y_tok[n][R, :, k, :], ALU.add).then_inc(S["sum_ready"], 1)
                    dve.wait_ge(S["sum_ready"], 2 * p + k + 1)

            with dve.Fori(0, PAIRS // 4) as k:
                for n in range(4):
                    combine(4 * k + n, n, k)

        @block.scalar
        def _(act):
            act.preload_act_table_set("natural_log_exp_and_others")
            act.wait_ge(S["c_loaded"], 16)
            act.wait_ge(S["z_prep"], 1)
            act.wait_ge(S["prep_done"], 1)

            def stats_squares(g, par, u, base):
                act.wait_ge(x_loaded[par], 16 * GROUP_DMAS * (u + 1))
                need(act, S["stat_ps"], g)
                act.activation(sqj[0:HROWS, :], xh[par][0:HROWS, :], ACT.Square,
                               accum_out=st[0:HROWS, 1:2]).then_inc(S["ach"], 1)
                act.wait_ge(S["ach"], base + 1)
                act.wait_ge(S["edge_done"], g + 1)
                act.activation(sqj[0:HROWS, 0:256], xe[0:HROWS].rearrange("r a b c -> r (a b c)"), ACT.Square,
                               accum_out=st[0:HROWS, 3:4]).then_inc(S["asum_done"], 1)

            def rstd(g, base):
                act.wait_ge(S["var_done"], g + 1)
                act.activation(st[0:HROWS, 12:14], st[0:HROWS, 10:12], ACT.Ln, bias=eps[0:HROWS, 0:1]).then_inc(S["ach"], 1)
                act.wait_ge(S["ach"], base + 2)
                act.activation(st[0:HROWS, 14:16], st[0:HROWS, 12:14], ACT.Exp, scale=-0.5).then_inc(S["rstd0_done"], 1)

            def normalise(g, par):
                act.wait_ge(S["nb_done"], g + 1)
                need(act, S["tr_full"], 8 * g)
                mid = xh[par][0:HROWS, :].rearrange("r (cp w) -> r cp w", w=SIDE)[:, :, HALF:SIDE - HALF]
                act.activation(xhn[0:HROWS, 1:GRID], mid.rearrange("r cp (n q) -> r n cp q", q=PATCH), ACT.Identity, bias=st[0:HROWS, 16:17],
                               scale=st[0:HROWS, 14:15]).then_inc(S["xhn_done"], 1)

            def group(g, par, u):
                stats_squares(g, par, u, 2 * g)
                rstd(g, 2 * g)
                normalise(g, par)

            group(0, 0, 0)
            group(1, 1, 0)
            with act.Fori(1, NGROUP // 2) as k:
                group(2 * k, 0, k)
                group(2 * k + 1, 1, k)

            R = slice(0, CHUNK)
            ach = Chain(act, S["ach"])

            def rstd_of(p, m, tmp, dst, stats, done):
                act.wait_ge(S[stats], p + 1)
                ach.link(act.activation(tmp[R, :], m[R, :, 1], ACT.Ln, bias=eps[R, 1:2]))
                act.activation(dst[R, :], tmp[R, :], ACT.Exp, scale=-0.5).then_inc(S[done], 1)

            def normalised(p, dst, rstd, nb, ready, done):
                act.wait_ge(S[ready], p + 1)
                for c in range(4):
                    act.activation(dst(c), h[R, bass.ds(p, 1), c, :].rearrange("p o n -> p (o n)"), ACT.Identity,
                                   bias=nb[R, c:c + 1], scale=rstd[R, c:c + 1]).then_inc(S[done], 1)

            def copied(ready, value, dst, src, done):
                act.wait_ge(S[ready], value)
                act.activation(dst, src, ACT.Copy).then_inc(S[done], 1)

            def ln1_rstd(p, par, half):
                rstd_of(p, mv, rs1, rstd1, "ln1_stats", "ln1_rstd")

            def ln1(p, par, half):
                need(act, S["xnt_ps"], p)
                normalised(p, lambda c: xn[R, c, :], rstd1, nb1, "nb1_ready", "xn_ready")

            def ln2_rstd(p, par, half):
                rstd_of(p, mv2, rs2, rstd2, "ln2_stats", "ln2_rstd")

            def ln2(p, par, half):
                need(act, scattered[par], 128 * half)
                normalised(p, lambda c: row[par][R, 0, c, 0:128], rstd2, nb2, "nb2_ready", "xn2_ready")

            def second_rows(p, par, half):
                act.wait_ge(S["xn2_ready"], 4 * p + 4)
                act.activation(row[par][R, 1, :, 0:128], row[par][R, 0, :, 0:128], ACT.Copy).then_inc(S["row_copied"], 1)

            def xnt_out(p, par, half):
                need(act, S["v_ps"], p)
                copied("xnt_ps", p + 1, xn_t, ps[0][:, 0:PT], "xnt_sb")

            def xn2t_out(p, par, half):
                need(act, S["lg_ps"], p)
                copied("xn2t_ps", p + 1, xn2_t, ps[7][:, 0:PT], "xn2t_sb")

            def log_decay(p, par, half):
                act.wait_ge(S["gk_ps"], p + 1)
                need(act, S["scan_done"], p)
                ach.link(act.activation(e_gk, ps[1][:, 0:PT], ACT.Exp, bias=nbgk[:, 0:1], scale=-1.0))
                act.activation(l_gk, e_gk, ACT.Ln, bias=eps[:, 4:5]).then_inc(S["l_ready"], 1)

            def q_out(p, par, half):
                need(act, S["o_ps"], p - 1)
                copied("q_ps", p + 1, qd[par], ps[0][:, 0:PT], "q_copied")

            def k_out(p, par, half):
                copied("k_ps", p + 1, kd[par], ps[1][:, 0:PT], "k_copied")

            def decays(p, par, half):
                act.wait_ge(S["scan_done"], p + 1)
                need(act, S["qk_ready"], 2 * p)
                need(act, S["state_ready"], 2 * (p - 1))
                act.activation(decay[par], cum, ACT.Exp, scale=eps[:, 5:6]).then_inc(S["e_ready"], 1)
                act.activation(grow, cum, ACT.Exp, scale=eps[:, 6:7]).then_inc(S["e_ready"], 1)

            def gate_out(p, par, half):
                need(act, S["og_ready"], p - 1)
                copied("g_ps", p + 1, gate[par], ps[0][:, 0:PT], "g_copied")

            def log_gate(p, par, half):
                act.wait_ge(S["g_copied"], p + 1)
                need(act, S["u_ready"], p - 1)
                ach.link(act.activation(e_gk, gate[par], ACT.Exp, scale=-1.0))
                act.activation(l_g[par], e_gk, ACT.Ln, bias=eps[:, 4:5]).then_inc(S["g_ready"], 1)

            def values_out(p, par, half):
                copied("v_ps", p + 1, val[par][R], ps[1][R, :].rearrange("p (c n) -> p c n", c=4), "v_ready")

            def keys_out(p, par, half):
                need(act, S["st_ps"], p)
                copied("kt_ps", p + 1, k_tok[R], ps[6][R, 0:256].rearrange("p (i n) -> p i n", i=2), "kt_ready")

            def squares(p, par, half):
                act.wait_ge(S["o_ps"], p + 1)
                need(act, S["ms_ps"], p)
                act.activation(o_sq, ps[4][:, 0:PT], ACT.Square).then_inc(S["sq_ready"], 1)

            def log_mean_squares(p, par, half):
                act.wait_ge(S["ms_ps"], p + 1)
                need(act, S["o_ready"], p)
                act.activation(fac, ps[5][:, 0:PT], ACT.Ln, bias=eps[:, 2:3]).then_inc(S["lms_ready"], 1)

            def factors(p, par, half):
                act.wait_ge(S["u_ready"], p + 1)
                act.activation(fac, fac, ACT.Exp).then_inc(S["fac_ready"], 1)

            def gate_ratio(p, par, half):
                act.wait_ge(S["dif_ready"], p + 1)
                act.activation(edif[R, :], dif[R, :], ACT.Exp).then_inc(S["edif_ready"], 1)

            def iteration(at):
                at(0, ln1_rstd)
                at(0, ln1)
                at(2, squares)
                at(3, ln2_rstd)
                at(0, xnt_out)
                at(2, log_mean_squares)
                at(0, log_decay)
                at(0, q_out)
                at(2, factors)
                at(0, decays)
                at(0, k_out)
                at(0, gate_out)
                at(4, gate_ratio)
                at(0, values_out)
                at(0, log_gate)
                at(0, keys_out)
                at(3, ln2)
                at(3, second_rows)
                at(3, xn2t_out)

            abase = pairs(act, ach, 2 * NGROUP, ACT_PAIR, iteration)

            act.wait_ge(S["tab_ready"], 1)
            act.wait_ge(S["w1_split"], 4)

            def upper_half(i, n, u, e):
                m = n % 2
                act.wait_ge(S["xt_ps"], i + 1)
                need(act, S["h_ps"], 4 * (i - 1))
                act.activation(x_hi[m], ps[m][:, 0:SLOT], ACT.Copy).then_inc(S["xhi_ready"], 1)

            def relu(i, n, u, e, chunks):
                m = n % 2
                if 0 in chunks:
                    need(act, S["w2_ps"], i - 1)
                for c in chunks:
                    act.wait_ge(S["h_ps"], 4 * i + c + 2 - c % 2)
                    act.activation(hid[m][:, c, :], ps[2 + 2 * m + c // 2][:, SLOT * (c % 2):SLOT * (c % 2) + SLOT],
                                   ACT.Relu, bias=b1_t[:, bass.ds(e * FC + c, 1)], scale=1.0 / W_SCALE)\
                       .then_inc(S["h_ready"], 1)

            def tile_rstd(i, n, u, e):
                act.wait_ge(S["rstd3_stats"], i + 1)
                need(act, S["gate_ready"], i)
                ach.link(act.activation(ln3, mv3[:, :, 1], ACT.Ln, bias=eps[:, 3:4]))
                act.activation(rstd3, ln3, ACT.Exp, scale=-0.5).then_inc(S["rstd3_ready"], 1)

            def tile_iteration(at):
                at(2, relu, (3,))
                at(4, tile_rstd)
                at(1, relu, (0, 1))
                at(0, upper_half)
                at(1, relu, (2,))

            abase = tiles(act, ach, abase, 1, tile_iteration)

            def store(p):
                act.wait_ge(S["sum_ready"], 2 * p + 2)
                act.dma_start(out_rows[bass.ds(p * PT, PT), :].rearrange("(c r) n -> r c n", c=4),
                              h[R, bass.ds(p, 1), :, :].rearrange("p o c n -> p (o c) n")).then_inc(S["h_out"], 16)

            with act.Fori(0, PAIRS) as p:
                store(p)
            act.wait_ge(S["h_out"], 16 * PAIRS)


DVE_PAIR = 40
DVE_TILE = 5
ACT_PAIR = 4
N_WLOADS = 1 + 10 + 2 + 20 + 6


_INPUTS = [
    "x", "cls_tok", "L0_tok_gamma", "L0_tok_beta", "L0_tok_W", "L0_tok_b", "L0_attn_Wq", "L0_attn_Wk", "L0_attn_Wv",
    "L0_attn_Wgk1", "L0_attn_Wgk2", "L0_attn_bgk2", "L0_attn_gnorm_w", "L0_attn_Wg", "L0_attn_Wo", "L0_ffn_router_w",
    "L0_ffn_w1", "L0_ffn_b1", "L0_ffn_w2", "L0_ffn_b2", "L0_ffn_gamma", "L0_ffn_beta",
]


def kernel(**inputs):
    import concourse.bacc as bacc
    from concourse.bass_utils import run_bass_kernel_spmd

    nc = bacc.Bacc("TRN2", target_bir_lowering=False, num_devices=1)
    arrays, aps = {}, {}
    for name in _INPUTS + ["consts"]:
        arr = const_array() if name == "consts" else np.ascontiguousarray(inputs[name])
        arrays[name + "_in"] = arr
        aps[name] = nc.dram_tensor(name + "_in", arr.shape, DT.from_np(arr.dtype), kind="ExternalInput").ap()
    out = nc.dram_tensor("out", (NTOK, E_DIM), F32, kind="ExternalOutput").ap()
    build(nc, aps, out)
    r = run_bass_kernel_spmd(nc, [arrays], core_ids=[0])
    return r.results[0]["out"].reshape(BATCH, TOK, E_DIM)
```

```python
from contextlib import ExitStack

import numpy as np

import concourse.bass as bass
from concourse import mybir

DT = mybir.dt
ALU = mybir.AluOpType
ACT = mybir.ActivationFunctionType
AX_X = mybir.AxisListType.X
F32, F16, BF16, I32, U32 = DT.float32, DT.float16, DT.bfloat16, DT.int32, DT.uint32

BATCH, CH, SIDE, PATCH, HALF = 64, 2, 104, 8, 4
GRID = SIDE // PATCH
HGRID = GRID + 1
ROWLEN = PATCH * SIDE
NSHIFT = 5
E_DIM = 128
TOK = GRID * GRID + 1
CHUNK = TOK // 2
NTOK = BATCH * TOK
GROUP = 8
NGROUP = BATCH // GROUP
MROWS, HROWS = GROUP * GRID, GROUP * HGRID
GTOK = GROUP * TOK
GTILES = -(-GTOK // 128)
GREST = GTOK - 128 * (GTILES - 1)
PAIRS = BATCH // 2
PT = 2 * TOK
NH, HK, HV = 4, 16, 32
NEXP, FF = 8, 512
FC = FF // 128
YBUF = 8
XBUF = 6
SLOT = 256
REGION = NTOK + SLOT
NTILE = (2 * NTOK + NEXP * (SLOT - 1)) // SLOT
NTILE += NTILE % 2
XW = 130
PAD_ID = 2 * NTOK
LAST_TILE_LAG = 5
NBLOCK = -(-(NTILE + LAST_TILE_LAG) // XBUF)
W_SCALE = 256.0
N_CONCAT = float(CH * NSHIFT * SIDE * SIDE)
EPS_TOK, EPS_LN, EPS_GN, EPS_FFN = 1e-7, 1e-5, 1e-5, 1e-6


def const_layout():
    cols, at = {}, 0
    for name, n in (
        ("ident", 128), ("stat_all", 2 * HROWS), ("stat_edge", 2 * HROWS), ("causal", CHUNK),
        ("heads", 128), ("meanv", 128), ("before", CHUNK), ("ones", CHUNK), ("reset", PT),
        ("cls_sel", TOK), ("expert", 8), ("region", 8), ("eps", 8), ("tokid", 4), ("slotid", 2),
        ("tiles_k", 43), ("one_row", 128),
    ):
        cols[name] = (at, at + n)
        at += n
    return cols, at


def const_array():
    cols, width = const_layout()
    c = np.zeros((128, width), np.float32)

    def put(name):
        a, b = cols[name]
        return c[:, a:b]

    put("ident")[:] = np.eye(128)
    wt = np.array([1 if m in (0, HGRID - 1) else 2 for m in range(HGRID)] * GROUP, np.float32)
    img_h = np.repeat(np.arange(GROUP), HGRID)
    img_m = np.concatenate([np.repeat(np.arange(GROUP), GRID), np.full(HROWS - MROWS, -1)])
    for k, img in enumerate((img_h, img_m)):
        same = (img_h[:, None] == img[None, :]).astype(np.float32)
        put("stat_all")[:HROWS, k * HROWS:(k + 1) * HROWS] = same * (1 + 2 * wt[:, None])
        put("stat_edge")[:HROWS, k * HROWS:(k + 1) * HROWS] = -same * wt[:, None]
    s = np.arange(CHUNK)
    put("causal")[:CHUNK] = s[:, None] <= s[None, :]
    put("before")[:CHUNK] = s[:, None] < s[None, :]
    put("ones")[:CHUNK] = 1
    h = np.arange(128) // HV
    put("heads")[:] = h[:, None] == h[None, :]
    put("meanv")[:] = (h[:, None] == h[None, :]) / HV
    put("reset")[:] = (np.arange(PT) % CHUNK != 0)[None, :]
    put("cls_sel")[0, 1:] = 1
    put("cls_sel")[1, 0] = 1
    put("expert")[:] = np.arange(8)
    put("region")[:] = np.arange(8) * REGION
    put("eps")[:, 0:5] = [EPS_TOK, EPS_LN, EPS_GN, EPS_FFN, 1.0]
    put("eps")[:, 5] = -1 / 16
    put("eps")[:, 6] = 1 / 16
    put("tokid")[:CHUNK] = 2 * (s[:, None] + CHUNK * np.arange(4)[None, :])
    put("slotid")[:] = np.arange(128)[:, None] + 128 * np.arange(2)[None, :]
    put("tiles_k")[:] = SLOT * np.arange(43)
    put("one_row")[:] = 1
    return c


def need(eng, sem, value):
    if not isinstance(value, int) or value > 0:
        eng.wait_ge(sem, value)


ARENA_WORDS = 30800
PHASE1_WORDS = 13184


SPARE = []


def apart(eng):
    eng.sem_inc(SPARE[0], 1)


class Chain:

    def __init__(self, eng, sem):
        self.eng, self.sem, self.base, self.n = eng, sem, 0, 0

    def start(self, base):
        self.base, self.n = base, 0

    def link(self, ins):
        self.n += 1
        ins.then_inc(self.sem, 1)
        self.eng.wait_ge(self.sem, self.base + self.n)

    def step(self, ins):
        self.n += 1
        ins.then_inc(self.sem, 1)

    def settle(self):
        self.eng.wait_ge(self.sem, self.base + self.n)
        apart(self.eng)


MAIN_FILLS = [(0, 4), (4, 7), (7, 10), (10, 13)]
HALF_FILLS = [(0, 4), (4, 8), (8, 11), (11, 14)]
TOKEN_FILLS = [(j, min(j + 4, GTILES)) for j in range(0, GTILES, 4)]
NFILL = len(TOKEN_FILLS)
GROUP_DMAS = 2 * GROUP + 2


def build(nc, a, out_rows):
    cols, cwidth = const_layout()
    xs_dram = nc.dram_tensor("x_slots", (NEXP * REGION + SLOT, XW), F32, kind="Internal").ap()
    tok_dram = nc.dram_tensor("tokens", (NTOK, E_DIM), F32, kind="Internal").ap()
    y_dram = nc.dram_tensor("y_tokens", (2 * NTOK, E_DIM), F32, kind="Internal").ap()

    with ExitStack() as ctx:
        def sb(name, shape, dt=F32):
            return ctx.enter_context(nc.sbuf_tensor(name, shape, dt))

        def sem(name):
            return ctx.enter_context(nc.semaphore(name))

        cst = sb("cst", [128, cwidth])

        def con(name, p=128):
            x, y = cols[name]
            return cst[0:p, x:y]

        ident = con("ident")
        eps = con("eps")
        h = sb("h", [128, PAIRS, 4, E_DIM])
        wt = sb("wt", [128, NSHIFT, E_DIM])
        bt = sb("bt", [CHUNK, 2, E_DIM])
        wproj = sb("wproj", [128, 6, E_DIM])
        nbgk = sb("nbgk", [128, 1])
        gnorm = sb("gnorm", [128, 1])
        rw = sb("rw", [128, NEXP])
        arena = sb("arena", [128, ARENA_WORDS])

        class Arena:
            def __init__(self):
                self.at = 0

            def take(self, *shape, dt=F32):
                n = int(np.prod(shape))
                words = n if dt in (F32, I32, U32) else (n + 1) // 2
                v = arena[:, self.at:self.at + words]
                self.at += words
                assert self.at <= ARENA_WORDS, self.at
                if dt is not F32:
                    v = v.bitcast(dt)
                if len(shape) > 1:
                    names = " ".join(f"d{i}" for i in range(len(shape)))
                    v = v.rearrange(f"p ({names}) -> p {names}", **{f"d{i}": s for i, s in enumerate(shape)})
                return v

        A0 = Arena()
        gx = [A0.take(NSHIFT, GROUP, TOK) for _ in range(2)]
        xm = [A0.take(CH * ROWLEN) for _ in range(2)]
        xh = [A0.take(CH * ROWLEN) for _ in range(2)]
        xmn = A0.take(GRID, CH * PATCH, PATCH)
        xhn = A0.take(HGRID, CH * PATCH, PATCH)
        xe = A0.take(2, CH * PATCH, PATCH)
        sqj = A0.take(CH * ROWLEN, dt=BF16)
        gam_t = A0.take(NSHIFT, GRID, GRID)
        staged = [A0.take(GTILES, E_DIM) for _ in range(2)]
        st = sb("st", [128, 24])
        AP_ = Arena()
        wn = AP_.take(NSHIFT, CH * PATCH * PATCH)
        wn2 = AP_.take(6, E_DIM)
        wgk1 = AP_.take(E_DIM)
        wgk2t = AP_.take(E_DIM)
        bc = AP_.take(E_DIM)
        bet_t = AP_.take(NSHIFT, TOK)
        gb = [AP_.take(CH * ROWLEN) for _ in range(2)]
        b1_n = AP_.take(128)
        gbp = [AP_.take(GRID, CH * PATCH, PATCH) for _ in range(2)]
        assert AP_.at <= 13600

        A1 = Arena()
        xn = A1.take(4, E_DIM)
        xn_t = A1.take(PT)
        e_gk, l_gk, cum, grow = (A1.take(PT) for _ in range(4))

        def two(*shape, **kw):
            return [A1.take(*shape, **kw) for _ in range(2)]

        decay = two(PT)
        qd, kd = two(PT), two(PT)
        gate, l_g = two(PT), two(PT)
        val = two(4, E_DIM)
        att = A1.take(NH, 4, CHUNK)
        k_tok = A1.take(2, 128)
        state = A1.take(2, 128)
        o_sq, fac, o_f = (A1.take(PT) for _ in range(3))
        bns, mv, rs1, rstd1, nb1 = A1.take(4, 6), A1.take(4, 2), A1.take(4), A1.take(4), A1.take(4)
        bns2, mv2, rs2, rstd2, nb2 = A1.take(4, 6), A1.take(4, 2), A1.take(4), A1.take(4), A1.take(4)
        row = two(2, 4, XW)
        xn2_t = A1.take(PT)
        lg, mx = A1.take(4, NEXP), A1.take(4, 8)
        mi = A1.take(4, 8, dt=U32)
        ef, oh = A1.take(4, 2), A1.take(4, 2, NEXP)
        om = A1.take(5, NEXP)
        base, pos, pp = A1.take(NEXP), A1.take(4, NEXP), A1.take(4, 2, NEXP)
        slot_f, dif, edif, den = A1.take(4, 2), A1.take(4), A1.take(4), A1.take(4)
        slot_i = two(4, 2, dt=I32)
        ids = A1.take(4)
        cnt = A1.take(NEXP)
        cnt_all, pad_f = A1.take(NEXP), A1.take(NEXP)
        pad_i = A1.take(NEXP, dt=I32)
        pad_row = A1.take(2, XW)
        more, ntiles, tile_end, skip = A1.take(NEXP, 43), A1.take(NEXP), A1.take(NEXP), A1.take(NEXP)
        past, skipped, tab_f = A1.take(NEXP), A1.take(NEXP), A1.take(2)
        assert A1.at <= PHASE1_WORDS, A1.at
        A2 = Arena()
        A2.at = PHASE1_WORDS
        b2_all, gam_all, bet_all = (A2.take(NEXP, E_DIM) for _ in range(3))
        w1_hi, w1_lo = A2.take(NEXP, FF, dt=F16), A2.take(NEXP, FF, dt=F16)
        w2_sb = A2.take(NEXP, FC, E_DIM)
        w1_raw = A2.take(NEXP, FF)
        at = A2.at
        A3 = Arena()
        A3.at = at - NEXP * FF
        x_sl = [A3.take(2, XW) for _ in range(XBUF)]
        x_hi, x_lo = [A3.take(SLOT, dt=F16) for _ in range(2)], [A3.take(SLOT, dt=F16) for _ in range(2)]
        hid = [A3.take(FC, SLOT)]
        assert A3.at <= at
        A3.at = at
        hid.append(A3.take(FC, SLOT))
        A3.at = 0
        x_b2 = [A3.take(2, E_DIM) for _ in range(2)]
        res = [A3.take(2, E_DIM) for _ in range(2)]
        nrm, scl = A3.take(2, E_DIM), A3.take(2, E_DIM)
        y_sl = [A3.take(2, E_DIM) for _ in range(2)]
        bns3, mv3, ln3, rstd3, rg3 = (A3.take(2, 6), A3.take(2, 2), A3.take(2), A3.take(2), A3.take(2))
        y_id = [A3.take(2, dt=I32) for _ in range(2)]
        y_tok = [A3.take(4, 2, E_DIM) for _ in range(YBUF)]
        assert A3.at <= PHASE1_WORDS
        tile_tab = sb("tile_tab", [1, XBUF * NBLOCK], I32)
        expert_tab = sb("expert_tab", [1, NBLOCK, 2 * XBUF], I32)
        b1_t = sb("b1_t", [128, NEXP * FC])

        ps = [ctx.enter_context(nc.psum_tensor(f"ps{i}", [128, 512], F32)) for i in range(8)]

        names = (
            "c_loaded z_prep w_loaded small_loaded prep_done xl0 xl1 edge_done dsum_done asum_done "
            "stat_ps var_done h_out ln1_stats ln1_rstd xn_ready xnt_ps xnt_sb gk_ps q_ps k_ps g_ps v_ps "
            "l_ready scan_done e_ready g_copied g_ready v_ready qk_ready sc_ps att_ready kt_ps kt_ready "
            "st_ps state_ready o_ps sq_ready ms_ps lms_ready u_ready fac_ready o_ready ao_ps h1_ready "
            "ln2_stats ln2_rstd xn2_ready xn2t_ps xn2t_sb lg_ps om_ready dif_ready edif_ready rk_ps "
            "slots_ready rank_used lg_ready max_ready best_ready pos_ready gate_done row_copied sc0 sc1 "
            "base_ready q_copied k_copied og_ready nb1_ready nb2_ready staged_part w1_loaded fw_loaded w1_split "
            "cnt_ready cnt_ps tab_f_ready tab_ps pad_first pad_ready tab_ready pad_gone pad_stored xs0 "
            "xs1 xs2 xs3 xs4 xs5 norm_ready scl_ready gate_ready bns3_ready xt_ps xhi_ready xlo_ready "
            "h_ps h_ready w2_ps xb_ready t_ready rstd3_stats rstd3_ready y_ready yg0 yg1 yl0 yl1 yl2 yl3 "
            "yl4 yl5 yl6 yl7 sum_ready rstd0_done nb_done xmn_done xhn_done tr_full tr_free y_full "
            "y_staged yst0 yst1 hl0 hl1 h_added dch ach pch t_prep d_prep xen_done "
        ).split()
        S = {n: sem(n) for n in names}
        x_loaded = [S["xl0"], S["xl1"]]
        SPARE[:] = [sem("passed")]
        block = ctx.enter_context(nc.Block())

        x_sl_loaded = [S[f"xs{n}"] for n in range(XBUF)]
        scattered = [S["sc0"], S["sc1"]]
        y_gone = [S["yg0"], S["yg1"]]
        staged_stored = [S["yst0"], S["yst1"]]
        h_loaded = [S["hl0"], S["hl1"]]
        TOKEN_BANKS = (4, 5, 7)
        y_loaded = [S[f"yl{n}"] for n in range(YBUF)]
        STEADY_PAIRS = range(8, PAIRS)
        LAST_LAG = 5

        def pairs(eng, chain, base, steps, step, aside=None):
            def iteration(p, half, par):
                def at(lag, work, *args):
                    q = p - lag
                    if not isinstance(q, int) or 0 <= q < PAIRS:
                        work(q, (par - lag) % 2, half + (par - lag) // 2, *args)
                step(at)

            for p in range(STEADY_PAIRS.start):
                chain.start(base)
                iteration(p, p // 2, p % 2)
                base += chain.n
                if p == 3 and aside:
                    aside()
            with eng.Fori(STEADY_PAIRS.start // 2, STEADY_PAIRS.stop // 2) as k:
                for par in range(2):
                    chain.start(base + (2 * k + (par - STEADY_PAIRS.start)) * steps)
                    iteration(2 * k + par, k, par)
                    assert chain.n == steps, chain.n
            base += steps * len(STEADY_PAIRS)
            for p in range(STEADY_PAIRS.stop, PAIRS + LAST_LAG):
                chain.start(base)
                iteration(p, p // 2, p % 2)
                base += chain.n
            return base

        STEADY_TILES = range(12, 12 + XBUF * ((NTILE - 12) // XBUF))

        def tiles(eng, chain, base, steps, step):
            experts, loads = [], []

            def iteration(i, u, n):
                if n == 0:
                    regs = [eng.alloc_register(name=f"expert_{len(loads)}_{r}") for r in range(2 * XBUF)]
                    loads.append(regs)
                    experts[:] = [bass.RuntimeValue.of_register_unchecked(r, min_val=0, max_val=NEXP - 1) for r in regs]
                    eng.load(regs, expert_tab[0:1, bass.ds(u, 1), :].rearrange("p o e -> p (o e)"))

                def at(lag, work, *args):
                    q = i - lag
                    if not isinstance(q, int) or 0 <= q < NTILE:
                        work(q, (n - lag) % XBUF, u + (n - lag) // XBUF, experts[XBUF + n - lag], *args)
                step(at)

            for i in range(STEADY_TILES.start):
                chain.start(base)
                iteration(i, i // XBUF, i % XBUF)
                base += chain.n
            u0 = STEADY_TILES.start // XBUF
            with eng.Fori(u0, STEADY_TILES.stop // XBUF) as u:
                for n in range(XBUF):
                    chain.start(base + (XBUF * u + (n - XBUF * u0)) * steps)
                    iteration(XBUF * u + n, u, n)
                    assert chain.n == steps, chain.n
            base += steps * len(STEADY_TILES)
            for i in range(STEADY_TILES.stop, NTILE + LAST_TILE_LAG):
                chain.start(base)
                iteration(i, i // XBUF, i % XBUF)
                base += chain.n
            return base

        def expert_sync(sp):
            sp.wait_ge(S["y_full"], NFILL * NGROUP)
            sp.wait_ge(S["y_staged"], NFILL * NGROUP)
            for st_sem in staged_stored:
                sp.wait_ge(st_sem, 32 * (NGROUP // 2))
            sp.dma_start(w1_raw, a["L0_ffn_w1"].rearrange("e d f -> d e f")).then_inc(S["w1_loaded"], 16)
            for e in range(NEXP):
                sp.dma_start(w2_sb[:, e], a["L0_ffn_w2"][e].rearrange("(c f) n -> f c n", c=FC)).then_inc(S["fw_loaded"], 16)
            for dst, name in ((b2_all, "L0_ffn_b2"), (gam_all, "L0_ffn_gamma"), (bet_all, "L0_ffn_beta")):
                src = a[name].rearrange("(o e) n -> o e n", o=1).to_broadcast([128, NEXP, E_DIM])
                sp.dma_start(dst, src).then_inc(S["fw_loaded"], 16)
            sp.wait_ge(S["pad_ready"], 1)
            sp.wait_ge(S["w1_split"], 4)
            sp.dma_start(xs_dram[NEXP * REGION:NEXP * REGION + SLOT, :].rearrange("(s p) w -> p s w", s=2), pad_row)\
              .then_inc(S["pad_stored"], 16)
            sp.wait_ge(S["pad_stored"], 16)
            sp.wait_ge(S["pad_first"], 1)
            regs = [sp.alloc_register(name=f"pad_first_{e}") for e in range(NEXP)]
            sp.load(regs, pad_i[0:1, :])
            for r in regs:
                first = bass.RuntimeValue.of_register_unchecked(r, min_val=0, max_val=NEXP * REGION - SLOT)
                sp.dma_start(xs_dram[bass.ds(first, SLOT), :].rearrange("(s p) w -> p s w", s=2), pad_row)\
                  .then_inc(S["pad_gone"], 16)
            sp.wait_ge(S["tab_ready"], 1)
            sp.wait_ge(S["w1_split"], 4)
            for sc in scattered:
                sp.wait_ge(sc, 64 * PAIRS)
            sp.wait_ge(S["pad_gone"], 16 * NEXP)

            def load(i, n):
                need(sp, S["y_ready"], i - XBUF + 1)
                r = sp.value_load(tile_tab[0:1, bass.ds(i, 1)], min_val=0, max_val=NEXP * REGION)
                sp.dma_start(x_sl[n], xs_dram[bass.ds(r, SLOT), :].rearrange("(s p) w -> p s w", s=2))\
                  .then_inc(x_sl_loaded[n], 16)

            for n in range(XBUF):
                load(n, n)
            with sp.Fori(1, NTILE // XBUF) as u:
                for n in range(XBUF):
                    load(XBUF * u + n, n)
            for i in range(NTILE // XBUF * XBUF, NTILE):
                load(i, i % XBUF)

            for gone in y_gone:
                sp.wait_ge(gone, 32 * (NTILE // 2))

            def load_y(p, n):
                need(sp, S["sum_ready"], 2 * (p - YBUF + 1))
                sp.dma_start(y_tok[n][0:CHUNK], y_dram[bass.ds(p * 2 * PT, 2 * PT), :].rearrange(
                    "(c r k) n -> r c k n", c=4, k=2)).then_inc(y_loaded[n], 16)

            for n in range(YBUF):
                load_y(n, n)
            with sp.Fori(1, PAIRS // YBUF) as k:
                for n in range(YBUF):
                    load_y(YBUF * k + n, n)

        @block.sync
        def _(sp):
            sp.dma_start(cst[:], a["consts"]).then_inc(S["c_loaded"], 16)
            sp.wait_ge(S["z_prep"], 1)
            n = 0

            def load(dst, src):
                nonlocal n
                n += 1
                sp.dma_start(dst, src).then_inc(S["w_loaded"], 16)

            load(wn[:, :, :], a["L0_tok_W"].rearrange("e (s c) p q -> e s (c p q)", c=CH))
            for k, name in ((0, "L0_tok_gamma"), (1, "L0_tok_beta")):
                for s in range(NSHIFT):
                    load(gb[k][GRID * s:GRID * s + GRID, :].rearrange("i (c r) -> i c r", c=CH),
                         a[name][CH * s:CH * s + CH].rearrange("c (i p) w -> i c (p w)", p=PATCH))
            load(bc[0:1, :], a["L0_tok_b"].rearrange("(o n) -> o n", o=1))
            load(bc[1:2, :], a["cls_tok"][0])
            for hd in range(NH):
                r = slice(HV * hd, HV * hd + HK)
                s = slice(HK * hd, HK * hd + HK)
                load(wn2[r, 0, :], a["L0_attn_Wq"][s, :])
                load(wn2[r, 1, :], a["L0_attn_Wk"][s, :])
            load(wgk1[0:16, :], a["L0_attn_Wgk1"])
            load(wn2[:, 3, :], a["L0_attn_Wg"])
            load(wn2[:, 4, :], a["L0_attn_Wv"])
            load(wn2[:, 5, :], a["L0_attn_Wo"])
            load(rw[:, :], a["L0_ffn_router_w"])
            load(b1_n[0:NEXP * FC, :], a["L0_ffn_b1"].rearrange("e (c f) -> (e c) f", c=FC))
            assert n == N_WLOADS, n

            def load_group(g, par):
                need(sp, S["xmn_done"], g - 1)
                need(sp, S["xhn_done"], g - 1)
                for b in range(GROUP):
                    img = a["x"][bass.ds(g * GROUP + b, 1)]
                    sp.dma_start(
                        xm[par][GRID * b:GRID * b + GRID, :].rearrange("i (c r) -> i c r", c=CH),
                        img.rearrange("o c (i p) w -> (o i) c (p w)", p=PATCH),
                    ).then_inc(x_loaded[par], 16)
                    sp.dma_start(
                        xh[par][HGRID * b + 1:HGRID * b + GRID, :].rearrange("m (c r) -> m c r", c=CH),
                        img[:, :, HALF:SIDE - HALF, :].rearrange("o c (m p) w -> (o m) c (p w)", p=PATCH),
                    ).then_inc(x_loaded[par], 16)
                edge = HALF * SIDE
                imgs = a["x"][bass.ds(g * GROUP, GROUP)]
                for m, r0, at in ((0, 0, edge), (HGRID - 1, SIDE - HALF, 0)):
                    sp.dma_start(
                        xh[par][m:m + (GROUP - 1) * HGRID + 1:HGRID, :].rearrange("b (c r) -> b c r", c=CH)[:, :, at:at + edge],
                        imgs[:, :, r0:r0 + HALF, :].rearrange("b c p w -> b c (p w)"),
                    ).then_inc(x_loaded[par], 16)

            load_group(0, 0)
            load_group(1, 1)
            with sp.Fori(1, NGROUP // 2) as k:
                load_group(2 * k, 0)
                load_group(2 * k + 1, 1)
            expert_sync(sp)

        @block.gpsimd
        def _(pool):
            for t in (wn2, nbgk[:, :], bet_t, xh[0], xh[1]):
                pool.memset(t, 0.0).then_inc(S["pch"], 1)
            pool.wait_ge(S["pch"], 5)
            pool.memset(st[:, :], 0.0).then_inc(S["z_prep"], 1)
            for hd in range(NH):
                r = slice(HV * hd, HV * hd + HK)
                s = slice(HK * hd, HK * hd + HK)
                for dst, src in (
                    (wn2[r, 2, 0:16], a["L0_attn_Wgk2"][s, :]),
                    (nbgk[r, :], a["L0_attn_bgk2"][s].rearrange("(n o) -> n o", o=1)),
                    (gnorm[HV * hd:HV * hd + HV, :], a["L0_attn_gnorm_w"].rearrange("(n o) -> n o", o=1)),
                ):
                    pool.dma_start(dst, src).then_inc(S["small_loaded"], 16)
            pool.wait_ge(S["prep_done"], 1)
            for t in (gx[0][:, :, :, 0:1], gx[1][:, :, :, 0:1], xe):
                pool.memset(t, 0.0).then_inc(S["pch"], 1)

            def scatter(p, par):
                pool.wait_ge(S["slots_ready"], p + 1)
                pool.wait_ge(S["row_copied"], p + 1)
                apart(pool)
                for t in range(4):
                    for k in range(2):
                        pool.indirect_dma_start(
                            xs_dram, bass.IndirectOffsetOnAxis(ap=slot_i[par][0:CHUNK, t, k:k + 1], axis=0),
                            row[par][0:CHUNK, k, t, :], None).then_inc(scattered[par], 16)

            def restage(g, par, u):
                pool.wait_ge(S["y_staged"], NFILL * (g + 1))
                apart(pool)
                full = 128 * (GTILES - 1)
                pool.dma_start(tok_dram[bass.ds(g * GTOK, full), :].rearrange("(j p) n -> p j n", p=128),
                               staged[par][:, 0:GTILES - 1, :]).then_inc(staged_stored[par], 16)
                pool.dma_start(tok_dram[bass.ds(g * GTOK + full, GREST), :], staged[par][0:GREST, GTILES - 1, :])\
                    .then_inc(staged_stored[par], 16)
                pool.wait_ge(staged_stored[par], 32 * (u + 1))
                apart(pool)
                hp = h[0:CHUNK, bass.ds(GROUP // 2 * g, GROUP // 2), :, :].rearrange("p o c n -> p (o c) n")
                pool.dma_start(hp, tok_dram[bass.ds(g * GTOK, GTOK), :].rearrange("(c r) n -> r c n", r=CHUNK))\
                    .then_inc(h_loaded[par], 16)

            with pool.Fori(0, NGROUP // 2) as k:
                restage(2 * k, 0, k)
                restage(2 * k + 1, 1, k)

            pool.wait_ge(S["w1_loaded"], 16)
            W = S["w1_split"]
            pool.tensor_scalar(w1_raw, w1_raw, W_SCALE, None, ALU.mult).then_inc(W, 1)
            pool.wait_ge(W, 1)
            pool.tensor_copy(w1_hi, w1_raw).then_inc(W, 1)
            pool.wait_ge(W, 2)
            pool.tensor_tensor(w1_lo, w1_raw, w1_hi, ALU.subtract).then_inc(W, 1)
            pool.wait_ge(W, 3)
            pool.memset(pad_row[:, :, 0:129], 0.0).then_inc(W, 1)
            pool.wait_ge(S["base_ready"], 1)
            pool.memset(pad_row[:, :, 129:130], float(PAD_ID)).then_inc(S["pad_ready"], 1)

            with pool.Fori(0, PAIRS // 2) as k:
                scatter(2 * k, 0)
                scatter(2 * k + 1, 1)

            pool.wait_ge(S["fw_loaded"], 16 * (NEXP + 3))
            pool.wait_ge(S["pad_gone"], 16 * NEXP)

            def with_bias(i, n, u, e):
                pool.wait_ge(x_sl_loaded[n], 16 * u + 16)
                need(pool, S["t_ready"], i - 1)
                apart(pool)
                b2 = b2_all[:, bass.ds(e, 1), :].to_broadcast([128, 2, E_DIM])
                pool.tensor_tensor(x_b2[n % 2], x_sl[n][:, :, 0:E_DIM], b2, ALU.add).then_inc(S["xb_ready"], 1)

            def scatter_y(i, n, u, e):
                pool.wait_ge(S["y_ready"], i + 1)
                apart(pool)
                for k in range(2):
                    pool.indirect_dma_start(
                        y_dram, bass.IndirectOffsetOnAxis(ap=y_id[n % 2][:, k:k + 1], axis=0),
                        y_sl[n % 2][:, k, :], None, bounds_check=2 * NTOK - 1, oob_is_err=False,
                    ).then_inc(y_gone[n % 2], 16)

            def tile_iteration(at):
                at(1, with_bias)
                at(5, scatter_y)

            pool.wait_ge(S["tab_ready"], 1)
            tiles(pool, Chain(pool, None), 0, 0, tile_iteration)

        @block.tensor
        def _(pe):
            pe.wait_ge(S["c_loaded"], 16)
            pe.wait_ge(S["w_loaded"], 16 * N_WLOADS)
            pe.wait_ge(S["small_loaded"], 16 * N_SMALL)
            T, D = S["t_prep"], S["d_prep"]
            for s in range(NSHIFT):
                ins = pe.transpose(ps[s // 4][:, 128 * (s % 4):128 * (s % 4) + 128], wn[:, s, :], ident)
            ins.then_inc(T, 1)
            for k in range(2):
                pe.wait_ge(D, 2 + k + 1)
                for j in range(GRID):
                    ins = pe.transpose(ps[2 + 2 * k + j // 7][:, 65 * (j % 7):65 * (j % 7) + 65],
                                       gbp[k][0:65, j].rearrange("r a b -> r (a b)"), ident[0:65, 0:65])
                ins.then_inc(T, 1)
            for n, w in enumerate((0, 1, 3, 4)):
                ins = pe.transpose(ps[6][:, 128 * n:128 * n + 128], wn2[:, w, :], ident)
            ins.then_inc(T, 1)
            pe.transpose(ps[7][:, 0:128], wn2[:, 5, :], ident)
            pe.transpose(ps[7][:, 384:384 + NEXP * FC], b1_n[0:NEXP * FC, :], ident[0:NEXP * FC, 0:NEXP * FC])
            pe.transpose(ps[7][0:16, 128:256], wn2[:, 2, 0:16], ident).then_inc(T, 1)
            pe.wait_ge(D, 8)
            pe.matmul(ps[7][:, 256:384], wgk1[0:16, :], wgk2t[0:16, :], start=True, stop=True).then_inc(T, 1)
            pe.wait_ge(D, 9)
            for hf in range(2):
                o = ps[0][0:CHUNK, 128 * hf:128 * hf + 128]
                for s in range(NSHIFT):
                    pe.matmul(o, bet_t[:, s, CHUNK * hf:CHUNK * hf + CHUNK], wt[:, s, :], start=s == 0, stop=False)
                x0, _y = cols["cls_sel"]
                ins = pe.matmul(o, cst[0:2, x0 + CHUNK * hf:x0 + CHUNK * hf + CHUNK], bc[0:2, :], start=False, stop=True)
            ins.then_inc(T, 1)

            fills = [[(xmn[0:MROWS, j], MROWS) for j in range(*f)] for f in MAIN_FILLS]
            fills += [[(xhn[0:HROWS, n], HROWS) for n in range(*f)] for f in HALF_FILLS]

            def transpose_fill(g, par, k):
                if k == 0:
                    pe.wait_ge(S["xmn_done"], g + 1)
                if k == 4:
                    pe.wait_ge(S["xhn_done"], g + 1)
                    pe.wait_ge(S["xen_done"], g + 1)
                need(pe, S["tr_free"], 8 * g + k - 3)
                for n, (src, rows) in enumerate(fills[k]):
                    ins = pe.transpose(ps[k % 4][:, rows * n:rows * n + rows],
                                       src.rearrange("r a b -> r (a b)"), ident[0:rows, 0:rows])
                ins.then_inc(S["tr_full"], 1)

            def y_fill(g, par, k):
                f = k // 2
                if k == 0:
                    pe.wait_ge(S["tr_free"], 8 * g + 8)
                if k % 2 == 0:
                    need(pe, S["y_staged"], NFILL * (g - 1) + f + 1)
                j0, j1 = TOKEN_FILLS[f]
                for j in range(2 * k, min(2 * k + 2, GTILES)):
                    rows = 128 if j < GTILES - 1 else GREST
                    for s in range(NSHIFT):
                        tokens = gx[par][:, s].rearrange("p b t -> p (b t)")[:, 128 * j:128 * j + rows]
                        ins = pe.matmul(ps[TOKEN_BANKS[f]][0:rows, 128 * (j - j0):128 * (j - j0) + 128],
                                        tokens, wt[:, s, :], start=s == 0, stop=s == NSHIFT - 1)
                if k % 2:
                    ins.then_inc(S["y_full"], 1)

            def stats(g):
                pe.wait_ge(S["dsum_done"], g + 1)
                pe.wait_ge(S["asum_done"], g + 1)
                need(pe, S["var_done"], g)
                x0 = cols["stat_all"][0]
                x1 = cols["stat_edge"][0]
                for k in range(2):
                    o = ps[6][0:HROWS, 2 * k:2 * k + 2]
                    pe.matmul(o, cst[0:HROWS, x0 + k * HROWS:x0 + (k + 1) * HROWS], st[0:HROWS, 0:2], start=True, stop=False)
                    ins = pe.matmul(o, cst[0:HROWS, x1 + k * HROWS:x1 + (k + 1) * HROWS], st[0:HROWS, 2:4],
                                    start=False, stop=True)
                ins.then_inc(S["stat_ps"], 1)

            def group(g, par, tr=True, y=True, stat=True):
                for k in range(8):
                    if tr:
                        transpose_fill(g, par, k)
                    if k == 5 and stat:
                        stats(g + 1)
                    if 1 <= k <= 2 * NFILL and y:
                        y_fill(g - 1, 1 - par, k - 1)

            pe.wait_ge(S["prep_done"], 1)
            stats(0)
            group(0, 0, y=False)
            group(1, 1)
            group(2, 0)
            with pe.Fori(1, NGROUP // 2 - 1) as k:
                group(2 * k + 1, 1)
                group(2 * k + 2, 0)
            group(NGROUP - 1, 1, stat=False)
            group(NGROUP, 0, tr=False, stat=False)

            def chunk(c):
                return slice(CHUNK * c, CHUNK * c + CHUNK)

            def front_transpose(p, par, half):
                pe.wait_ge(S["xn_ready"], 4 * p + 4)
                need(pe, S["g_copied"], p)
                for c in range(4):
                    ins = pe.transpose(ps[0][:, chunk(c)], xn[0:CHUNK, c, :], ident[0:CHUNK, 0:CHUNK])
                ins.then_inc(S["xnt_ps"], 1)

            def project(bank, w, done):
                pe.matmul(ps[bank][:, 0:PT], wproj[:, w, :], xn_t, start=True, stop=True).then_inc(S[done], 1)

            def project_gk(p, par, half):
                pe.wait_ge(S["xnt_sb"], p + 1)
                need(pe, S["v_ready"], p)
                project(1, 2, "gk_ps")

            def project_q(p, par, half):
                pe.wait_ge(S["xnt_sb"], p + 1)
                project(0, 0, "q_ps")

            def project_k(p, par, half):
                pe.wait_ge(S["l_ready"], p + 1)
                project(1, 1, "k_ps")

            def project_g(p, par, half):
                pe.wait_ge(S["q_copied"], p + 1)
                project(0, 3, "g_ps")

            def values(p, par, half):
                pe.wait_ge(S["k_copied"], p + 1)
                for c in range(4):
                    ins = pe.matmul(ps[1][0:CHUNK, 128 * c:128 * c + 128], xn_t[:, chunk(c)], wproj[:, 4, :],
                                    start=True, stop=True)
                ins.then_inc(S["v_ps"], 1)

            def scores(p, par, half, hd):
                if hd == 0:
                    pe.wait_ge(S["qk_ready"], 2 * p + 2)
                need(pe, S["att_ready"], 4 * p + hd - 1)
                r = slice(HV * hd, HV * hd + HV)
                for c in range(4):
                    ins = pe.matmul(ps[2 + hd % 2][0:CHUNK, chunk(c)], kd[par][r, chunk(c)], qd[par][r, chunk(c)],
                                    start=True, stop=True, tile_position=(HV * hd, 0))
                ins.then_inc(S["sc_ps"], 1)

            def keys(p, par, half):
                pe.wait_ge(S["qk_ready"], 2 * p + 2)
                need(pe, S["state_ready"], 2 * p)
                for i in range(2):
                    ins = pe.transpose(ps[6][0:CHUNK, 128 * i:128 * i + 128], kd[par][:, chunk(2 * i)], ident)
                ins.then_inc(S["kt_ps"], 1)

            def states(p, par, half):
                pe.wait_ge(S["v_ready"], p + 1)
                pe.wait_ge(S["kt_ready"], p + 1)
                for i in range(2):
                    ins = pe.matmul(ps[6][:, 256 + 128 * i:384 + 128 * i], k_tok[0:CHUNK, i, :],
                                    val[par][0:CHUNK, 2 * i, :], start=True, stop=True)
                ins.then_inc(S["st_ps"], 1)

            def outputs(p, par, half):
                pe.wait_ge(S["att_ready"], 4 * p + 4)
                pe.wait_ge(S["state_ready"], 2 * p + 2)
                need(pe, S["og_ready"], p)
                for c in range(4):
                    if c % 2:
                        pe.matmul(ps[4][:, chunk(c)], state[:, c // 2, :], qd[par][:, chunk(c)], start=True, stop=True)
                    for hd in range(NH):
                        r = slice(HV * hd, HV * hd + HV)
                        ins = pe.matmul(ps[4][r, chunk(c)], val[par][0:CHUNK, c, r], att[0:CHUNK, hd, c, :],
                                        start=c % 2 == 0, stop=True, tile_position=(0, HV * hd),
                                        skip_group_check=True)
                ins.then_inc(S["o_ps"], 1)

            def mean_squares(p, par, half):
                pe.wait_ge(S["sq_ready"], p + 1)
                need(pe, S["h1_ready"], p)
                pe.matmul(ps[5][:, 0:PT], con("meanv"), o_sq, start=True, stop=True).then_inc(S["ms_ps"], 1)

            def attention_out(p, par, half):
                pe.wait_ge(S["o_ready"], p + 1)
                for c in range(4):
                    ins = pe.matmul(ps[5][0:CHUNK, 128 * c:128 * c + 128], o_f[:, chunk(c)], wproj[:, 5, :],
                                    start=True, stop=True)
                ins.then_inc(S["ao_ps"], 1)

            def route_transpose(p, par, half):
                pe.wait_ge(S["xn2_ready"], 4 * p + 4)
                need(pe, S["rank_used"], p)
                for c in range(4):
                    ins = pe.transpose(ps[7][:, chunk(c)], row[par][0:CHUNK, 0, c, 0:128], ident[0:CHUNK, 0:CHUNK])
                ins.then_inc(S["xn2t_ps"], 1)

            def route_logits(p, par, half):
                pe.wait_ge(S["xn2t_sb"], p + 1)
                for c in range(4):
                    ins = pe.matmul(ps[7][0:CHUNK, 352 + 8 * c:360 + 8 * c], xn2_t[:, chunk(c)], rw[:, :],
                                    start=True, stop=True)
                ins.then_inc(S["lg_ps"], 1)

            def ranks(p, par, half):
                pe.wait_ge(S["om_ready"], p + 1)
                zeros = om[0:CHUNK, 4:5, :].to_broadcast([CHUNK, 5, NEXP])
                pe.matmul(ps[7][0:CHUNK, 384:424], con("ones", CHUNK), zeros, start=True, stop=False)
                for c in range(4):
                    later = om[0:CHUNK, c:c + 1, :].to_broadcast([CHUNK, 4 - c, NEXP])
                    pe.matmul(ps[7][0:CHUNK, 392 + 8 * c:424], con("ones", CHUNK), later, start=False, stop=False,
                              skip_group_check=True)
                ins = pe.matmul(ps[7][0:CHUNK, 384:424], con("before", CHUNK), om[0:CHUNK].rearrange("p c e -> p (c e)"),
                                start=False, stop=True)
                ins.then_inc(S["rk_ps"], 1)

            def iteration(at):
                at(1, scores, 1)
                at(4, route_logits)
                at(0, front_transpose)
                at(2, mean_squares)
                at(0, project_gk)
                at(0, project_q)
                at(0, project_k)
                at(0, project_g)
                at(1, scores, 2)
                at(1, scores, 3)
                at(4, ranks)
                at(0, values)
                at(0, keys)
                at(0, scores, 0)
                at(2, attention_out)
                at(0, states)
                at(3, route_transpose)
                at(1, outputs)

            pairs(pe, Chain(pe, None), 0, 0, iteration)

            pe.wait_ge(S["cnt_ready"], 1)
            pe.matmul(ps[0][:, 0:NEXP], con("one_row", 1), cnt[0:1, :], start=True, stop=True).then_inc(S["cnt_ps"], 1)
            pe.wait_ge(S["tab_f_ready"], 1)
            pe.transpose(ps[1][0:1, 0:128], tab_f[:, 0:1], ident)
            pe.transpose(ps[1][0:1, 128:256], tab_f[:, 1:2], ident).then_inc(S["tab_ps"], 1)
            pe.wait_ge(S["tab_ready"], 1)
            pe.wait_ge(S["w1_split"], 3)
            pe.wait_ge(S["fw_loaded"], 16 * (NEXP + 3))

            copies = []

            def own(e):
                copies.append(pe.alloc_register(name=f"expert_copy_{len(copies)}"))
                pe.reg_mov(copies[-1], e)
                return bass.RuntimeValue.of_register_unchecked(copies[-1], min_val=0, max_val=NEXP - 1)

            def slots_transpose(i, n, u, e):
                pe.wait_ge(x_sl_loaded[n], 16 * u + 16)
                need(pe, S["xlo_ready"], i - 1)
                for k in range(2):
                    ins = pe.transpose(ps[n % 2][:, 128 * k:128 * k + 128], x_sl[n][:, k, 0:E_DIM], ident)
                ins.then_inc(S["xt_ps"], 1)

            def hidden(i, n, u, e):
                m = n % 2
                e = own(e)
                pe.wait_ge(S["xlo_ready"], i + 1)
                need(pe, S["h_ready"], 4 * (i - 2) + 2)
                for c in range(FC):
                    if c == 2:
                        need(pe, S["h_ready"], 4 * (i - 2) + 4)
                    o = ps[2 + 2 * m + c // 2][:, SLOT * (c % 2):SLOT * (c % 2) + SLOT]
                    f = slice(128 * c, 128 * c + 128)
                    hi = w1_hi[:, bass.ds(e, 1), f].rearrange("p o f -> p (o f)")
                    lo = w1_lo[:, bass.ds(e, 1), f].rearrange("p o f -> p (o f)")
                    pe.matmul(o, hi, x_hi[m], start=True, stop=False)
                    pe.matmul(o, hi, x_lo[m], start=False, stop=False)
                    pe.matmul(o, lo, x_hi[m], start=False, stop=True).then_inc(S["h_ps"], 1)

            def second_layer(i, n, u, e):
                m = n % 2
                e = own(e)
                pe.wait_ge(S["h_ready"], 4 * i + 4)
                need(pe, S["t_ready"], i - 1)
                for k in range(2):
                    for c in range(FC):
                        ins = pe.matmul(ps[6 + m][:, 128 * k:128 * k + 128], hid[m][:, c, 128 * k:128 * k + 128],
                                        w2_sb[:, bass.ds(e, 1), c, :].rearrange("p o n -> p (o n)"),
                                        start=c == 0, stop=c == FC - 1)
                ins.then_inc(S["w2_ps"], 1)

            def tile_iteration(at):
                at(1, hidden)
                at(0, slots_transpose)
                at(2, second_layer)

            tiles(pe, Chain(pe, None), 0, 0, tile_iteration)

        @block.vector
        def _(dve):
            ch = Chain(dve, S["dch"])
            T, D = S["t_prep"], S["d_prep"]
            dve.wait_ge(T, 1)
            dve.tensor_copy(wt[:, 0:4, :], ps[0][:, :].rearrange("p (s n) -> p s n", s=4)).then_inc(D, 1)
            dve.tensor_copy(wt[:, 4, :], ps[1][:, 0:128]).then_inc(D, 1)
            dve.wait_ge(S["w_loaded"], 16 * N_WLOADS)
            dve.wait_ge(S["small_loaded"], 16 * N_SMALL)
            for k in range(2):
                dve.tensor_copy(gbp[k][0:65], gb[k][0:65, :].rearrange(
                    "r (cp j q) -> r j cp q", j=GRID, q=PATCH)).then_inc(D, 1)
            dve.wait_ge(T, 3)
            for k in range(2):
                for half, (j0, j1) in enumerate(((0, 7), (7, 13))):
                    src = ps[2 + 2 * k + half][:, 0:65 * (j1 - j0)].rearrange("p (j s i) -> p s i j", s=NSHIFT, i=GRID)
                    for s in range(NSHIFT):
                        dst = (gam_t[:, s] if k == 0 else
                               bet_t[:, s, 1:TOK].rearrange("p (i j) -> p i j", i=GRID))[:, :, j0:j1]
                        ins = dve.tensor_copy(dst, src[:, s])
                        if not (k and half and s == NSHIFT - 1):
                            ins.then_inc(S["dch"], 1)
                            ch.n += 1
            ins.then_inc(D, 1)
            dve.wait_ge(T, 5)
            dve.tensor_copy(b1_t[:, :], ps[7][:, 384:384 + NEXP * FC]).then_inc(S["dch"], 1)
            ch.n += 1
            dve.tensor_scalar(wproj[:, 0, :], ps[6][:, 0:128], HK ** -0.5, None, ALU.mult).then_inc(D, 1)
            dve.tensor_copy(wproj[:, 1, :], ps[6][:, 128:256]).then_inc(D, 1)
            dve.tensor_copy(wgk2t[0:16, :], ps[7][0:16, 128:256]).then_inc(D, 1)
            dve.wait_ge(T, 6)
            dve.tensor_copy(wproj[:, 3:5, :], ps[6][:, 256:512].rearrange("p (a n) -> p a n", a=2)).then_inc(S["dch"], 1)
            dve.tensor_scalar(wproj[:, 5, :], ps[7][:, 0:128], gnorm[:, 0:1], None, ALU.mult).then_inc(S["dch"], 1)
            dve.tensor_scalar(nbgk[:, :], nbgk[:, :], -1.0, None, ALU.mult).then_inc(S["dch"], 1)
            ch.n += 3
            dve.tensor_copy(wproj[:, 2, :], ps[7][:, 256:384]).then_inc(D, 1)
            dve.wait_ge(T, 7)
            ch.link(dve.tensor_copy(bt[:, :, :], ps[0][0:CHUNK, 0:256].rearrange("p (a n) -> p a n", a=2)))
            dve.tensor_copy(st[0:1, 20:21], st[0:1, 21:22]).then_inc(S["prep_done"], 1)
            dve.wait_ge(S["pch"], 8)
            dbase = ch.n

            def stats_sums(g, par, u):
                dve.wait_ge(x_loaded[par], 16 * GROUP_DMAS * (u + 1))
                need(dve, S["xen_done"], g)
                need(dve, S["asum_done"], g)
                need(dve, S["stat_ps"], g)
                x3 = xh[par][0:HROWS, :].rearrange("r (cp w) -> r cp w", w=SIDE)
                ch.link(dve.tensor_copy(xe[0:HROWS, 0, :, HALF:PATCH], x3[:, :, 0:HALF]))
                dve.tensor_copy(xe[0:HROWS, 1, :, 0:HALF], x3[:, :, SIDE - HALF:SIDE]).then_inc(S["edge_done"], 1)
                dve.wait_ge(S["edge_done"], g + 1)
                ch.link(dve.tensor_reduce(st[0:HROWS, 2:3], xe[0:HROWS].rearrange("r a b c -> r (a b c)"), AX_X, ALU.add))
                dve.tensor_reduce(st[0:HROWS, 0:1], xh[par][0:HROWS, :], AX_X, ALU.add).then_inc(S["dsum_done"], 1)

            def stats_small(g):
                dve.wait_ge(S["stat_ps"], g + 1)
                need(dve, S["xhn_done"], g)
                m = st[0:HROWS, 4:8].rearrange("r (k a) -> r k a", k=2)
                ch.link(dve.tensor_scalar(st[0:HROWS, 4:8], ps[6][0:HROWS, 0:4], 1.0 / N_CONCAT, None, ALU.mult))
                ch.link(dve.tensor_tensor(st[0:HROWS, 8:10], m[:, :, 0], m[:, :, 0], ALU.mult))
                dve.tensor_tensor(st[0:HROWS, 10:12], m[:, :, 1], st[0:HROWS, 8:10], ALU.subtract).then_inc(S["var_done"], 1)

            def normalise(g, par):
                m = st[0:HROWS, 4:8].rearrange("r (k a) -> r k a", k=2)
                dve.wait_ge(S["rstd0_done"], g + 1)
                dve.scalar_tensor_tensor(st[0:HROWS, 16:18], m[:, :, 0], -1.0, st[0:HROWS, 14:16],
                                         ALU.mult, ALU.mult).then_inc(S["nb_done"], 1)
                dve.wait_ge(S["nb_done"], g + 1)
                need(dve, S["tr_full"], 8 * g - 4)
                dve.tensor_scalar(xmn[0:MROWS], xm[par][0:MROWS, :].rearrange("r (cp j q) -> r j cp q", j=GRID, q=PATCH), st[0:MROWS, 15:16], st[0:MROWS, 17:18],
                                  ALU.mult, ALU.add).then_inc(S["xmn_done"], 1)

            def normalise_edges(g):
                need(dve, S["tr_full"], 8 * g)
                dve.tensor_scalar(xhn[0:HROWS, 0:HGRID:HGRID - 1], xe[0:HROWS], st[0:HROWS, 14:15], st[0:HROWS, 16:17],
                                  ALU.mult, ALU.add).then_inc(S["xen_done"], 1)

            def scale_fill(g, par, k):
                dve.wait_ge(S["tr_full"], 8 * g + k + 1)
                if k == 0:
                    need(dve, S["y_full"], NFILL * (g - 1))

                def put(s, j0, j1, src):
                    dst = gx[par][:, s, :, 1:TOK].rearrange("p b (i j) -> p b i j", i=GRID)[:, :, :, j0:j1]
                    gm = gam_t[:, s, :, j0:j1].unsqueeze(1).to_broadcast([128, GROUP, GRID, j1 - j0])
                    return dve.tensor_tensor(dst, src, gm, ALU.mult)

                if k < 4:
                    j0, j1 = MAIN_FILLS[k]
                    v = ps[k][:, 0:MROWS * (j1 - j0)].rearrange("p (j b i) -> p b i j", b=GROUP, i=GRID)
                    put(0, j0, j1, v).then_inc(S["tr_free"], 1)
                    return
                n0, n1 = HALF_FILLS[k - 4]
                v = ps[k - 4][:, 0:HROWS * (n1 - n0)].rearrange("p (j b m) -> p b m j", b=GROUP, m=HGRID)
                for s in range(1, NSHIFT):
                    m0 = 1 if s <= 2 else 0
                    right = (s - 1) % 2
                    j0, j1 = max(n0 - right, 0), min(n1 - right, GRID)
                    ins = put(s, j0, j1, v[:, :, m0:m0 + GRID, j0 + right - n0:j1 + right - n0])
                    ins.then_inc(S["tr_free"] if s == NSHIFT - 1 else S["dch"], 1)
                    ch.n += s < NSHIFT - 1

            def shift_tokens(g, par, u, k):
                dve.wait_ge(h_loaded[par], 16 * (u + 1))
                hp = h[0:CHUNK, bass.ds(GROUP // 2 * g + k, 1), :, :].rearrange("p o (i t) n -> p (o i) t n", i=2)
                b4 = bt[:, :, :].unsqueeze(1).to_broadcast([CHUNK, 2, 2, E_DIM])
                dve.tensor_tensor(hp, hp, b4, ALU.add).then_inc(S["h_added"], 1)

            def group(g, par, base, u, tr=True, shift=True, stat=True):
                ch.start(base)
                for k in range(8):
                    if k == 2 and stat:
                        stats_sums(g + 1, 1 - par, u)
                    if tr:
                        scale_fill(g, par, k)
                    if k % 2 and shift:
                        shift_tokens(g - 2, par, u - par - 1, k // 2)
                    if k == 5 and stat:
                        stats_small(g + 1)
                    if k == 6 and stat:
                        normalise(g + 1, 1 - par)
                if stat:
                    normalise_edges(g + 1)
                return ch.n

            ch.start(dbase)
            stats_sums(0, 0, 0)
            stats_small(0)
            normalise(0, 0)
            normalise_edges(0)
            dbase += ch.n
            per = group(0, 0, dbase, 0, shift=False)
            dbase += per
            for g in (1, 2):
                assert group(g, g % 2, dbase + (g - 1) * per, g // 2 + g % 2, shift=g > 1) == per
            with dve.Fori(1, NGROUP // 2 - 1) as k:
                assert group(2 * k + 1, 1, dbase + k * (2 * per), k + 1) == per
                assert group(2 * k + 2, 0, dbase + per + k * (2 * per), k + 1) == per
            dbase += per * (NGROUP - 2)
            dbase += group(NGROUP - 1, 1, dbase, NGROUP // 2, stat=False)
            dbase += group(NGROUP, 0, dbase, NGROUP // 2, tr=False, stat=False)

            R = slice(0, CHUNK)

            def ln_stats(p, b, m, done):
                for c in range(4):
                    ch.step(dve.bn_stats(b[R, c], h[R, bass.ds(p, 1), c, :].rearrange("p o n -> p (o n)")))
                ch.settle()
                for c in range(4):
                    ins = dve.bn_aggr(m[R, c], b[R, c])
                    if c < 3:
                        ch.step(ins)
                ins.then_inc(S[done], 1)

            def shift(p, m, rstd, nb, ready, done):
                dve.wait_ge(S[ready], p + 1)
                dve.scalar_tensor_tensor(nb[R, :], m[R, :, 0], -1.0, rstd[R, :], ALU.mult, ALU.mult).then_inc(S[done], 1)

            def ln1_stats(p, par, half):
                ln_stats(p, bns, mv, "ln1_stats")

            def ln1_shift(p, par, half):
                shift(p, mv, rstd1, nb1, "ln1_rstd", "nb1_ready")

            def ln2_stats(p, par, half):
                dve.wait_ge(S["h1_ready"], p + 1)
                apart(dve)
                ln_stats(p, bns2, mv2, "ln2_stats")

            def ln2_shift(p, par, half):
                shift(p, mv2, rstd2, nb2, "ln2_rstd", "nb2_ready")

            def scan(p, par, half):
                dve.wait_ge(S["l_ready"], p + 1)
                need(dve, S["e_ready"], 2 * p)
                dve.tensor_tensor_scan(cum, con("reset"), l_gk, 0.0, ALU.mult, ALU.add).then_inc(S["scan_done"], 1)

            def decayed(p, par, half):
                dve.wait_ge(S["e_ready"], 2 * p + 2)
                dve.wait_ge(S["k_copied"], p + 1)
                dve.tensor_tensor(qd[par], qd[par], decay[par], ALU.mult).then_inc(S["qk_ready"], 1)
                dve.tensor_tensor(kd[par], kd[par], grow, ALU.mult).then_inc(S["qk_ready"], 1)

            def masked(p, par, half, hd):
                if hd == 0:
                    need(dve, S["o_ps"], p)
                dve.wait_ge(S["sc_ps"], 4 * p + hd + 1)
                src = ps[2 + hd % 2][R, 0:PT].rearrange("p (c t) -> p c t", c=4)
                mask = con("causal", CHUNK).unsqueeze(1).to_broadcast([CHUNK, 4, CHUNK])
                dve.tensor_tensor(att[R, hd], src, mask, ALU.mult).then_inc(S["att_ready"], 1)

            def state_out(p, par, half):
                dve.wait_ge(S["st_ps"], p + 1)
                need(dve, S["o_ps"], p)
                for i in range(2):
                    end = CHUNK * (2 * i + 1) - 1
                    dve.scalar_tensor_tensor(state[:, i, :], ps[6][:, 256 + 128 * i:384 + 128 * i],
                                             decay[par][:, end:end + 1], con("heads"), ALU.mult, ALU.mult)\
                       .then_inc(S["state_ready"], 1)

            def gated(p, par, half):
                dve.wait_ge(S["sq_ready"], p + 1)
                need(dve, S["ao_ps"], p)
                dve.tensor_tensor(o_f, ps[4][:, 0:PT], gate[par], ALU.mult).then_inc(S["og_ready"], 1)

            def log_factor(p, par, half):
                dve.wait_ge(S["lms_ready"], p + 1)
                dve.wait_ge(S["g_ready"], p + 1)
                dve.scalar_tensor_tensor(fac, fac, -0.5, l_g[par], ALU.mult, ALU.subtract).then_inc(S["u_ready"], 1)

            def factored(p, par, half):
                dve.wait_ge(S["fac_ready"], p + 1)
                dve.wait_ge(S["og_ready"], p + 1)
                dve.tensor_tensor(o_f, o_f, fac, ALU.mult).then_inc(S["o_ready"], 1)

            def residual(p, par, half):
                dve.wait_ge(S["ao_ps"], p + 1)
                hp = h[R, bass.ds(p, 1), :, :].rearrange("p o c n -> p (o c n)")
                dve.tensor_tensor(hp, hp, ps[5][R, :], ALU.add).then_inc(S["h1_ready"], 1)

            def logits_out(p, par, half):
                dve.wait_ge(S["lg_ps"], p + 1)
                dve.tensor_copy(lg[R], ps[7][R, 352:384].rearrange("p (c e) -> p c e", c=4)).then_inc(S["lg_ready"], 1)

            def best_logits(p, par, half):
                dve.wait_ge(S["lg_ready"], p + 1)
                apart(dve)
                for c in range(4):
                    ins = dve.max(mx[R, c], lg[R, c])
                    if c < 3:
                        ch.step(ins)
                ins.then_inc(S["max_ready"], 1)

            def best_experts(p, par, half):
                dve.wait_ge(S["max_ready"], p + 1)
                apart(dve)
                ch.step(dve.max_index(mi[R, 0], mx[R, 0], lg[R, 0]))
                dve.tensor_tensor(dif[R, :], mx[R, :, 1], mx[R, :, 0], ALU.subtract).then_inc(S["dif_ready"], 1)
                for c in range(1, 4):
                    ins = dve.max_index(mi[R, c], mx[R, c], lg[R, c])
                    if c < 3:
                        ch.step(ins)
                ins.then_inc(S["best_ready"], 1)

            def one_hot(p, par, half):
                dve.wait_ge(S["best_ready"], p + 1)
                ch.link(dve.tensor_copy(ef[R], mi[R, :, 0:2]))
                x0, x1 = cols["expert"]
                ex = cst[R, x0:x1].unsqueeze(1).to_broadcast([CHUNK, 8, NEXP])
                ef3 = ef[R].rearrange("p c k -> p (c k)").unsqueeze(2).to_broadcast([CHUNK, 8, NEXP])
                ch.link(dve.tensor_tensor(oh[R].rearrange("p c k e -> p (c k) e"), ex, ef3, ALU.is_equal))
                dve.tensor_tensor(om[R, 0:4], oh[R, :, 0], oh[R, :, 1], ALU.add).then_inc(S["om_ready"], 1)

            def positions(p, par, half):
                dve.wait_ge(S["rk_ps"], p + 1)
                dve.wait_ge(S["edif_ready"], p + 1)
                need(dve, scattered[par], 128 * half)
                b4 = base[R, :].unsqueeze(1).to_broadcast([CHUNK, 4, NEXP])
                rk = ps[7][R, 384:416].rearrange("p (c e) -> p c e", c=4)
                ch.step(dve.tensor_tensor(pos[R], rk, b4, ALU.add))
                ch.step(dve.tensor_scalar(den[R, :], edif[R, :], 1.0, None, ALU.add))
                dve.tensor_copy(row[par][R, 0, :, 129], ids[R, :]).then_inc(S["pos_ready"], 1)

            def gates(p, par, half):
                dve.wait_ge(S["pos_ready"], p + 1)
                p4 = pos[R].unsqueeze(2).to_broadcast([CHUNK, 4, 2, NEXP])
                ch.step(dve.tensor_tensor(pp[R], oh[R], p4, ALU.mult))
                dve.tensor_tensor(base[R, :], base[R, :], ps[7][R, 416:424], ALU.add).then_inc(S["rank_used"], 1)
                ch.step(dve.reciprocal(row[par][R, 0, :, 128], den[R, :]))
                dve.tensor_scalar(row[par][R, 1, :, 129], ids[R, :], 1.0, None, ALU.add).then_inc(S["gate_done"], 1)

            def place(p, par, half):
                dve.wait_ge(S["gate_done"], p + 1)
                ch.step(dve.tensor_reduce(slot_f[R], pp[R], AX_X, ALU.add))
                ch.step(dve.tensor_tensor(row[par][R, 1, :, 128], row[par][R, 0, :, 128], edif[R, :], ALU.mult))
                ch.link(dve.tensor_scalar(ids[R, :], ids[R, :], float(2 * PT), None, ALU.add))
                dve.tensor_copy(slot_i[par][R], slot_f[R]).then_inc(S["slots_ready"], 1)

            def iteration(at):
                at(0, ln1_stats)
                at(5, place)
                at(3, residual)
                at(0, ln1_shift)
                at(3, ln2_stats)
                at(2, gated)
                at(1, masked, 0)
                at(4, logits_out)
                at(3, ln2_shift)
                at(1, masked, 1)
                at(1, state_out)
                at(2, log_factor)
                at(0, scan)
                at(4, best_logits)
                at(4, best_experts)
                at(4, one_hot)
                at(2, factored)
                at(0, decayed)
                at(1, masked, 2)
                at(1, masked, 3)
                at(4, positions)
                at(4, gates)

            ch.start(dbase)
            dve.wait_ge(S["y_full"], NFILL * NGROUP)
            ch.link(dve.tensor_copy(base[R, :], con("region", CHUNK)))
            ch.link(dve.memset(om[R, 4:5], 0.0))
            dve.tensor_copy(ids[R, :], con("tokid", CHUNK)).then_inc(S["base_ready"], 1)
            dve.wait_ge(S["base_ready"], 1)
            
            def last_tokens():
                for k in range(GROUP // 2):
                    shift_tokens(NGROUP - 1, 1, NGROUP // 2 - 1, k)

            dbase = pairs(dve, ch, dbase + ch.n, DVE_PAIR, iteration, last_tokens)

            ch.start(dbase)
            dve.tensor_tensor(cnt[R, :], base[R, :], con("region", CHUNK), ALU.subtract).then_inc(S["cnt_ready"], 1)
            dve.wait_ge(S["cnt_ps"], 1)
            ch.link(dve.tensor_copy(cnt_all, ps[0][:, 0:NEXP]))
            ch.link(dve.tensor_tensor(pad_f[0:1, :], cnt_all[0:1, :], con("region", 1), ALU.add))
            dve.tensor_copy(pad_i[0:1, :], pad_f[0:1, :]).then_inc(S["pad_first"], 1)
            c1 = cnt_all[:, :].unsqueeze(2).to_broadcast([128, NEXP, 43])
            k1 = con("tiles_k").unsqueeze(1).to_broadcast([128, NEXP, 43])
            ch.link(dve.tensor_tensor(more, c1, k1, ALU.is_gt))
            ch.link(dve.tensor_reduce(ntiles[:, :], more, AX_X, ALU.add))
            ch.link(dve.tensor_tensor_scan(tile_end[:, :], con("one_row")[:, 0:NEXP], ntiles[:, :], 0.0, ALU.mult, ALU.add))
            ch.link(dve.tensor_scalar(skip[:, :], ntiles[:, :], -float(SLOT), float(REGION), ALU.mult, ALU.add))
            tile_no = con("slotid")[:, 0:1]
            ch.link(dve.tensor_scalar(past, tile_end[:, :], tile_no, None, ALU.is_le))
            ch.link(dve.tensor_tensor(skipped, past, skip[:, :], ALU.mult))
            ch.link(dve.tensor_reduce(tab_f[:, 0:1], past, AX_X, ALU.add))
            ch.link(dve.tensor_reduce(tab_f[:, 1:2], skipped, AX_X, ALU.add))
            ch.link(dve.scalar_tensor_tensor(tab_f[:, 1:2], tile_no, float(SLOT), tab_f[:, 1:2], ALU.mult, ALU.add))
            ch.link(dve.tensor_scalar(tab_f[:, 1:2], tab_f[:, 1:2], float(NEXP * REGION), None, ALU.min))
            dve.tensor_scalar(tab_f[:, 0:1], tab_f[:, 0:1], float(NEXP - 1), None, ALU.min).then_inc(S["tab_f_ready"], 1)
            ch.link(dve.memset(expert_tab[:, :, :], 0))
            dve.wait_ge(S["tab_ps"], 1)
            by_block = ps[1][0:1, 0:XBUF * NBLOCK].rearrange("p (u n) -> p u n", n=XBUF)
            ch.link(dve.tensor_copy(expert_tab[:, :, XBUF:2 * XBUF], by_block))
            ch.link(dve.tensor_copy(expert_tab[:, 1:NBLOCK, 0:XBUF], by_block[:, 0:NBLOCK - 1, :]))
            dve.tensor_copy(tile_tab[:, :], ps[1][0:1, 128:128 + XBUF * NBLOCK]).then_inc(S["tab_ready"], 1)
            dbase += ch.n
            dve.wait_ge(S["tab_ready"], 1)
            dve.wait_ge(S["pad_gone"], 16 * NEXP)
            dve.wait_ge(S["fw_loaded"], 16 * (NEXP + 3))

            def lower_half(i, n, u, e):
                m = n % 2
                dve.wait_ge(S["xhi_ready"], i + 1)
                need(dve, S["h_ps"], 4 * (i - 1))
                dve.tensor_tensor(x_lo[m], ps[m][:, 0:SLOT], x_hi[m], ALU.subtract).then_inc(S["xlo_ready"], 1)

            def sums(i, n, u, e):
                m = n % 2
                dve.wait_ge(S["w2_ps"], i + 1)
                dve.wait_ge(S["xb_ready"], i + 1)
                need(dve, S["norm_ready"], i - 1)
                dve.tensor_tensor(res[m], ps[6 + m][:, 0:SLOT].rearrange("p (k n) -> p k n", k=2), x_b2[m],
                                  ALU.add).then_inc(S["t_ready"], 1)

            def tile_stats(i, n, u, e):
                dve.wait_ge(S["t_ready"], i + 1)
                need(dve, S["rstd3_stats"], i)
                ch.step(dve.bn_stats(bns3[:, 0], res[n % 2][:, 0, :]))
                dve.bn_stats(bns3[:, 1], res[n % 2][:, 1, :]).then_inc(S["bns3_ready"], 1)

            def tile_moments(i, n, u, e):
                dve.wait_ge(S["bns3_ready"], i + 1)
                need(dve, S["norm_ready"], i)
                apart(dve)
                ch.step(dve.bn_aggr(mv3[:, 0], bns3[:, 0]))
                dve.bn_aggr(mv3[:, 1], bns3[:, 1]).then_inc(S["rstd3_stats"], 1)

            def gated_rstd(i, n, u, e):
                dve.wait_ge(S["rstd3_ready"], i + 1)
                dve.tensor_tensor(rg3, rstd3, x_sl[n][:, :, E_DIM], ALU.mult).then_inc(S["gate_ready"], 1)

            def tile_norm(i, n, u, e):
                dve.wait_ge(S["gate_ready"], i + 1)
                need(dve, S["scl_ready"], i)
                for k in range(2):
                    ins = dve.tensor_scalar(nrm[:, k, :], res[n % 2][:, k, :], mv3[:, k, 0:1], rg3[:, k:k + 1],
                                            ALU.subtract, ALU.mult)
                    if k == 0:
                        ch.step(ins)
                ins.then_inc(S["norm_ready"], 1)

            def scaled(i, n, u, e):
                dve.wait_ge(S["norm_ready"], i + 1)
                need(dve, S["y_ready"], i)
                gm = gam_all[:, bass.ds(e, 1), :].to_broadcast([128, 2, E_DIM])
                dve.tensor_tensor(scl, nrm, gm, ALU.mult).then_inc(S["scl_ready"], 1)

            def shifted(i, n, u, e):
                g = x_sl[n][:, :, E_DIM]
                dve.wait_ge(S["scl_ready"], i + 1)
                need(dve, y_gone[n % 2], 32 * (XBUF // 2 * u + n // 2))
                ch.step(dve.tensor_copy(y_id[n % 2], x_sl[n][:, :, E_DIM + 1]))
                be = bet_all[:, bass.ds(e, 1), :].rearrange("p o n -> p (o n)")
                for k in range(2):
                    ins = dve.scalar_tensor_tensor(y_sl[n % 2][:, k, :], be, g[:, k:k + 1], scl[:, k, :],
                                                   ALU.mult, ALU.add)
                    if k == 0:
                        ch.step(ins)
                ins.then_inc(S["y_ready"], 1)

            def tile_iteration(at):
                at(1, lower_half)
                at(5, scaled)
                at(4, tile_moments)
                at(5, shifted)
                at(3, sums)
                at(4, gated_rstd)
                at(4, tile_norm)
                at(3, tile_stats)

            dbase = tiles(dve, ch, dbase, DVE_TILE, tile_iteration)

            def combine(p, n, u):
                dve.wait_ge(y_loaded[n], 16 * u + 16)
                hp = h[R, bass.ds(p, 1), :, :].rearrange("p o c n -> p (o c) n")
                for k in range(2):
                    dve.tensor_tensor(hp, hp, y_tok[n][R, :, k, :], ALU.add).then_inc(S["sum_ready"], 1)
                    dve.wait_ge(S["sum_ready"], 2 * p + k + 1)

            with dve.Fori(0, PAIRS // YBUF) as k:
                for n in range(YBUF):
                    combine(YBUF * k + n, n, k)

        @block.scalar
        def _(act):
            act.preload_act_table_set("natural_log_exp_and_others")
            act.wait_ge(S["c_loaded"], 16)
            act.wait_ge(S["z_prep"], 1)
            act.wait_ge(S["prep_done"], 1)

            def stats_squares(g, par, u, base):
                act.wait_ge(x_loaded[par], 16 * GROUP_DMAS * (u + 1))
                need(act, S["stat_ps"], g)
                act.activation(sqj[0:HROWS, :], xh[par][0:HROWS, :], ACT.Square,
                               accum_out=st[0:HROWS, 1:2]).then_inc(S["ach"], 1)
                act.wait_ge(S["ach"], base + 1)
                act.wait_ge(S["edge_done"], g + 1)
                act.activation(sqj[0:HROWS, 0:256], xe[0:HROWS].rearrange("r a b c -> r (a b c)"), ACT.Square,
                               accum_out=st[0:HROWS, 3:4]).then_inc(S["asum_done"], 1)

            def rstd(g, base):
                act.wait_ge(S["var_done"], g + 1)
                act.activation(st[0:HROWS, 12:14], st[0:HROWS, 10:12], ACT.Ln, bias=eps[0:HROWS, 0:1]).then_inc(S["ach"], 1)
                act.wait_ge(S["ach"], base + 2)
                act.activation(st[0:HROWS, 14:16], st[0:HROWS, 12:14], ACT.Exp, scale=-0.5).then_inc(S["rstd0_done"], 1)

            def normalise(g, par):
                act.wait_ge(S["nb_done"], g + 1)
                need(act, S["tr_full"], 8 * g)
                mid = xh[par][0:HROWS, :].rearrange("r (cp w) -> r cp w", w=SIDE)[:, :, HALF:SIDE - HALF]
                act.activation(xhn[0:HROWS, 1:GRID], mid.rearrange("r cp (n q) -> r n cp q", q=PATCH), ACT.Identity, bias=st[0:HROWS, 16:17],
                               scale=st[0:HROWS, 14:15]).then_inc(S["xhn_done"], 1)

            def stage(g, par, u, f):
                act.wait_ge(S["y_full"], NFILL * g + f + 1)
                if f == 0:
                    need(act, staged_stored[par], 32 * u)
                j0, j1 = TOKEN_FILLS[f]
                src = ps[TOKEN_BANKS[f]][:, 0:128 * (j1 - j0)].rearrange("p (j n) -> p j n", n=E_DIM)
                whole = min(j1, GTILES - 1)
                ins = act.activation(staged[par][:, j0:whole, :], src[:, 0:whole - j0, :], ACT.Copy)
                if j1 == GTILES:
                    ins.then_inc(S["staged_part"], 1)
                    ins = act.activation(staged[par][0:GREST, whole, :], src[0:GREST, whole - j0, :], ACT.Copy)
                ins.then_inc(S["y_staged"], 1)

            def group(g, par, u, stat=True, out=True):
                nu = u + par
                if stat:
                    stats_squares(g + 1, 1 - par, nu, 2 * (g + 1))
                for f in range(NFILL):
                    if f == 2 and stat:
                        rstd(g + 1, 2 * (g + 1))
                    if out:
                        stage(g - 1, 1 - par, nu - 1, f)
                if stat:
                    normalise(g + 1, 1 - par)

            group(-1, 1, -1, out=False)
            group(0, 0, 0, out=False)
            group(1, 1, 0)
            group(2, 0, 1)
            with act.Fori(1, NGROUP // 2 - 1) as k:
                group(2 * k + 1, 1, k)
                group(2 * k + 2, 0, k + 1)
            group(NGROUP - 1, 1, NGROUP // 2 - 1, stat=False)
            group(NGROUP, 0, NGROUP // 2, stat=False)

            R = slice(0, CHUNK)
            ach = Chain(act, S["ach"])

            def rstd_of(p, m, tmp, dst, stats, done):
                act.wait_ge(S[stats], p + 1)
                ach.link(act.activation(tmp[R, :], m[R, :, 1], ACT.Ln, bias=eps[R, 1:2]))
                act.activation(dst[R, :], tmp[R, :], ACT.Exp, scale=-0.5).then_inc(S[done], 1)

            def normalised(p, dst, rstd, nb, ready, done):
                act.wait_ge(S[ready], p + 1)
                for c in range(4):
                    act.activation(dst(c), h[R, bass.ds(p, 1), c, :].rearrange("p o n -> p (o n)"), ACT.Identity,
                                   bias=nb[R, c:c + 1], scale=rstd[R, c:c + 1]).then_inc(S[done], 1)

            def copied(ready, value, dst, src, done):
                act.wait_ge(S[ready], value)
                act.activation(dst, src, ACT.Copy).then_inc(S[done], 1)

            def ln1_rstd(p, par, half):
                rstd_of(p, mv, rs1, rstd1, "ln1_stats", "ln1_rstd")

            def ln1(p, par, half):
                need(act, S["xnt_ps"], p)
                normalised(p, lambda c: xn[R, c, :], rstd1, nb1, "nb1_ready", "xn_ready")

            def ln2_rstd(p, par, half):
                rstd_of(p, mv2, rs2, rstd2, "ln2_stats", "ln2_rstd")

            def ln2(p, par, half):
                need(act, scattered[par], 128 * half)
                normalised(p, lambda c: row[par][R, 0, c, 0:128], rstd2, nb2, "nb2_ready", "xn2_ready")

            def second_rows(p, par, half):
                act.wait_ge(S["xn2_ready"], 4 * p + 4)
                act.activation(row[par][R, 1, :, 0:128], row[par][R, 0, :, 0:128], ACT.Copy).then_inc(S["row_copied"], 1)

            def xnt_out(p, par, half):
                need(act, S["v_ps"], p)
                copied("xnt_ps", p + 1, xn_t, ps[0][:, 0:PT], "xnt_sb")

            def xn2t_out(p, par, half):
                need(act, S["lg_ps"], p)
                copied("xn2t_ps", p + 1, xn2_t, ps[7][:, 0:PT], "xn2t_sb")

            def log_decay(p, par, half):
                act.wait_ge(S["gk_ps"], p + 1)
                need(act, S["scan_done"], p)
                ach.link(act.activation(e_gk, ps[1][:, 0:PT], ACT.Exp, bias=nbgk[:, 0:1], scale=-1.0))
                act.activation(l_gk, e_gk, ACT.Ln, bias=eps[:, 4:5]).then_inc(S["l_ready"], 1)

            def q_out(p, par, half):
                need(act, S["o_ps"], p - 1)
                copied("q_ps", p + 1, qd[par], ps[0][:, 0:PT], "q_copied")

            def k_out(p, par, half):
                copied("k_ps", p + 1, kd[par], ps[1][:, 0:PT], "k_copied")

            def decays(p, par, half):
                act.wait_ge(S["scan_done"], p + 1)
                need(act, S["qk_ready"], 2 * p)
                need(act, S["state_ready"], 2 * (p - 1))
                act.activation(decay[par], cum, ACT.Exp, scale=eps[:, 5:6]).then_inc(S["e_ready"], 1)
                act.activation(grow, cum, ACT.Exp, scale=eps[:, 6:7]).then_inc(S["e_ready"], 1)

            def gate_out(p, par, half):
                need(act, S["og_ready"], p - 1)
                copied("g_ps", p + 1, gate[par], ps[0][:, 0:PT], "g_copied")

            def log_gate(p, par, half):
                act.wait_ge(S["g_copied"], p + 1)
                need(act, S["u_ready"], p - 1)
                ach.link(act.activation(e_gk, gate[par], ACT.Exp, scale=-1.0))
                act.activation(l_g[par], e_gk, ACT.Ln, bias=eps[:, 4:5]).then_inc(S["g_ready"], 1)

            def values_out(p, par, half):
                copied("v_ps", p + 1, val[par][R], ps[1][R, :].rearrange("p (c n) -> p c n", c=4), "v_ready")

            def keys_out(p, par, half):
                need(act, S["st_ps"], p)
                copied("kt_ps", p + 1, k_tok[R], ps[6][R, 0:256].rearrange("p (i n) -> p i n", i=2), "kt_ready")

            def squares(p, par, half):
                act.wait_ge(S["o_ps"], p + 1)
                need(act, S["ms_ps"], p)
                act.activation(o_sq, ps[4][:, 0:PT], ACT.Square).then_inc(S["sq_ready"], 1)

            def log_mean_squares(p, par, half):
                act.wait_ge(S["ms_ps"], p + 1)
                need(act, S["o_ready"], p)
                act.activation(fac, ps[5][:, 0:PT], ACT.Ln, bias=eps[:, 2:3]).then_inc(S["lms_ready"], 1)

            def factors(p, par, half):
                act.wait_ge(S["u_ready"], p + 1)
                act.activation(fac, fac, ACT.Exp).then_inc(S["fac_ready"], 1)

            def gate_ratio(p, par, half):
                act.wait_ge(S["dif_ready"], p + 1)
                act.activation(edif[R, :], dif[R, :], ACT.Exp).then_inc(S["edif_ready"], 1)

            def iteration(at):
                at(4, second_rows)
                at(0, ln1_rstd)
                at(4, xn2t_out)
                at(0, ln1)
                at(2, squares)
                at(0, xnt_out)
                at(3, ln2_rstd)
                at(2, log_mean_squares)
                at(0, log_decay)
                at(0, q_out)
                at(2, factors)
                at(0, decays)
                at(0, k_out)
                at(0, gate_out)
                at(4, gate_ratio)
                at(0, log_gate)
                at(3, ln2)
                at(0, values_out)
                at(0, keys_out)

            abase = pairs(act, ach, 2 * NGROUP, ACT_PAIR, iteration)

            act.wait_ge(S["tab_ready"], 1)
            act.wait_ge(S["w1_split"], 4)

            def upper_half(i, n, u, e):
                m = n % 2
                act.wait_ge(S["xt_ps"], i + 1)
                need(act, S["h_ps"], 4 * (i - 1))
                act.activation(x_hi[m], ps[m][:, 0:SLOT], ACT.Copy).then_inc(S["xhi_ready"], 1)

            def relu(i, n, u, e, chunks):
                m = n % 2
                if 0 in chunks:
                    need(act, S["w2_ps"], i - 1)
                for c in chunks:
                    act.wait_ge(S["h_ps"], 4 * i + c + 2 - c % 2)
                    act.activation(hid[m][:, c, :], ps[2 + 2 * m + c // 2][:, SLOT * (c % 2):SLOT * (c % 2) + SLOT],
                                   ACT.Relu, bias=b1_t[:, bass.ds(e * FC + c, 1)], scale=1.0 / W_SCALE)\
                       .then_inc(S["h_ready"], 1)

            def tile_rstd(i, n, u, e):
                act.wait_ge(S["rstd3_stats"], i + 1)
                need(act, S["gate_ready"], i)
                ach.link(act.activation(ln3, mv3[:, :, 1], ACT.Ln, bias=eps[:, 3:4]))
                act.activation(rstd3, ln3, ACT.Exp, scale=-0.5).then_inc(S["rstd3_ready"], 1)

            def tile_iteration(at):
                at(2, relu, (3,))
                at(4, tile_rstd)
                at(1, relu, (0, 1))
                at(0, upper_half)
                at(1, relu, (2,))

            abase = tiles(act, ach, abase, 1, tile_iteration)

            def store(p):
                act.wait_ge(S["sum_ready"], 2 * p + 2)
                act.dma_start(out_rows[bass.ds(p * PT, PT), :].rearrange("(c r) n -> r c n", c=4),
                              h[R, bass.ds(p, 1), :, :].rearrange("p o c n -> p (o c) n")).then_inc(S["h_out"], 16)

            with act.Fori(0, PAIRS) as p:
                store(p)
            act.wait_ge(S["h_out"], 16 * PAIRS)


DVE_PAIR = 29
DVE_TILE = 5
ACT_PAIR = 4
N_WLOADS = 1 + 10 + 2 + 2 * NH + 6
N_SMALL = 3 * NH


_INPUTS = [
    "x", "cls_tok", "L0_tok_gamma", "L0_tok_beta", "L0_tok_W", "L0_tok_b", "L0_attn_Wq", "L0_attn_Wk", "L0_attn_Wv",
    "L0_attn_Wgk1", "L0_attn_Wgk2", "L0_attn_bgk2", "L0_attn_gnorm_w", "L0_attn_Wg", "L0_attn_Wo", "L0_ffn_router_w",
    "L0_ffn_w1", "L0_ffn_b1", "L0_ffn_w2", "L0_ffn_b2", "L0_ffn_gamma", "L0_ffn_beta",
]


def kernel(**inputs):
    import concourse.bacc as bacc
    from concourse.bass_utils import run_bass_kernel_spmd

    nc = bacc.Bacc("TRN2", target_bir_lowering=False, num_devices=1)
    arrays, aps = {}, {}
    for name in _INPUTS + ["consts"]:
        arr = const_array() if name == "consts" else np.ascontiguousarray(inputs[name])
        arrays[name + "_in"] = arr
        aps[name] = nc.dram_tensor(name + "_in", arr.shape, DT.from_np(arr.dtype), kind="ExternalInput").ap()
    out = nc.dram_tensor("out", (NTOK, E_DIM), F32, kind="ExternalOutput").ap()
    build(nc, aps, out)
    r = run_bass_kernel_spmd(nc, [arrays], core_ids=[0])
    return r.results[0]["out"].reshape(BATCH, TOK, E_DIM)
```
